# Optimizing a Trainium2 kernel written in Bass

```python
import numpy as np
import jax
import jax.numpy as jnp

def _softmax(x, axis=-1):
    return jax.nn.softmax(x, axis=axis)

def _gelu(x):
    return jax.nn.gelu(x, approximate=True)

def _silu(x):
    return jax.nn.silu(x)

def _sigmoid(x):
    return jax.nn.sigmoid(x)

def _layernorm(x, axis=-1, eps=1e-05):
    m = jnp.mean(x, axis=axis, keepdims=True)
    v = jnp.var(x, axis=axis, keepdims=True)
    return (x - m) / jnp.sqrt(v + eps)

def _scatter_add(tgt, idx, src, axis=0):
    return tgt.at[idx].add(src)

def _segment_sum(src, seg, n):
    return jax.ops.segment_sum(src, seg, n)
kernel_name = 'mk_seq_preln_d2_jaxref_r8_2fbc88'

def setup_inputs(seed: int=0):
    np.random.seed(seed)
    _w = jnp.asarray

    def _L0_attn_setup():
        import jax, jax.numpy as jnp
        import numpy as np
        D_MODEL = 256
        D_INNER = 512
        D_XB = 128
        D_STATE = 64
        HEADDIM = 64
        NHEADS = D_INNER // HEADDIM
        NXB = D_XB // HEADDIM
        D_CONV = 4
        CHUNK = 128
        EPS = 1e-05
        D_FF = 1024
        CONV_DIM = D_XB + D_XB + D_INNER
        D_IN_PROJ = D_INNER + D_XB + D_XB + D_INNER + NHEADS

        def rmsnorm(x, w, eps=EPS):
            return x * jax.lax.rsqrt(jnp.mean(x * x, axis=-1, keepdims=True) + eps) * w

        def causal_depthwise_conv(x, w, b):
            k = w.shape[1]
            xp = jnp.pad(x, ((0, 0), (k - 1, 0), (0, 0)))
            out = jax.lax.conv_general_dilated(xp.transpose(0, 2, 1), w[:, None, :], (1,), 'VALID', feature_group_count=x.shape[-1])
            return out.transpose(0, 2, 1) + b

        def ssd_chunked(xdt, dA, Bm, Cm):
            b, l, h, p = xdt.shape
            n = Bm.shape[-1]
            c, q = (l // CHUNK, CHUNK)
            xdt = xdt.reshape(b, c, q, h, p)
            Bm = Bm.reshape(b, c, q, h, n)
            Cm = Cm.reshape(b, c, q, h, n)
            dA = dA.reshape(b, c, q, h).transpose(0, 3, 1, 2)
            dAc = jnp.cumsum(dA, axis=-1)
            seg = dAc[..., :, None] - dAc[..., None, :]
            mask = jnp.tril(jnp.ones((q, q), bool))
            Lm = jnp.where(mask, jnp.exp(seg), 0.0)
            Y_diag = jnp.einsum('bcqhn,bcshn,bhcqs,bcshp->bcqhp', Cm, Bm, Lm, xdt)
            decay_states = jnp.exp(dAc[..., -1:] - dAc)
            states = jnp.einsum('bcqhn,bhcq,bcqhp->bchpn', Bm, decay_states, xdt)
            chunk_decay = jnp.exp(dAc[..., -1])

            def step(carry, inp):
                s, d = inp
                new = s + d[:, :, None, None] * carry
                return (new, carry)
            init = jnp.zeros((b, h, p, n), xdt.dtype)
            _, prevs = jax.lax.scan(step, init, (states.transpose(1, 0, 2, 3, 4), chunk_decay.transpose(2, 0, 1)))
            Y_off = jnp.einsum('bcqhn,cbhpn,bhcq->bcqhp', Cm, prevs, jnp.exp(dAc))
            return (Y_diag + Y_off).reshape(b, l, h, p)

        def mamba2(x, in_proj_w, conv_w, conv_b, dt_bias, A_log, Dp, norm_w, out_proj_w):
            b, l, _ = x.shape
            zxbcdt = x @ in_proj_w
            z, xb, Bc, Cc, dt = jnp.split(zxbcdt, [D_INNER, D_INNER + D_XB, D_INNER + 2 * D_XB, 2 * D_INNER + 2 * D_XB], axis=-1)
            xBC = jax.nn.silu(causal_depthwise_conv(jnp.concatenate([xb, Bc, Cc], -1), conv_w, conv_b))
            xb, Bc, Cc = jnp.split(xBC, [D_XB, 2 * D_XB], axis=-1)
            dt = jax.nn.softplus(dt + dt_bias)
            A = -jnp.exp(A_log)
            rep = NHEADS // NXB
            x_h = jnp.repeat(xb.reshape(b, l, NXB, HEADDIM), rep, axis=2)
            B_h = jnp.repeat(Bc.reshape(b, l, NXB, D_STATE), rep, axis=2)
            C_h = Cc.reshape(b, l, NHEADS, D_STATE)
            y = ssd_chunked(x_h * dt[..., None], dt * A, B_h, C_h)
            y = y + Dp[None, None, :, None] * x_h
            y = y.reshape(b, l, D_INNER)
            y = rmsnorm(y * jax.nn.silu(z), norm_w)
            return y @ out_proj_w
        key = jax.random.key(seed)
        ks = jax.random.split(key, 8)
        s = 0.02
        return {'hidden_states': jax.random.normal(ks[0], (2, 256, D_MODEL), jnp.float32), 'in_proj_w': jax.random.normal(ks[1], (D_MODEL, D_IN_PROJ), jnp.float32) * s, 'conv_w': jax.random.normal(ks[2], (CONV_DIM, D_CONV), jnp.float32) * 0.1, 'conv_b': jnp.zeros((CONV_DIM,), jnp.float32), 'dt_bias': jnp.log(jnp.expm1(jnp.linspace(0.001, 0.1, NHEADS, dtype=jnp.float32))), 'A_log': jnp.log(jnp.linspace(1.0, 16.0, NHEADS, dtype=jnp.float32)), 'D': jnp.ones((NHEADS,), jnp.float32), 'norm_w': jnp.ones((D_INNER,), jnp.float32), 'out_proj_w': jax.random.normal(ks[3], (D_INNER, D_MODEL), jnp.float32) * s, 'ln1_w': jnp.ones((D_MODEL,), jnp.float32), 'ln2_w': jnp.ones((D_MODEL,), jnp.float32), 'gate_w': jax.random.normal(ks[4], (D_MODEL, D_FF), jnp.float32) * s, 'up_w': jax.random.normal(ks[5], (D_MODEL, D_FF), jnp.float32) * s, 'down_w': jax.random.normal(ks[6], (D_FF, D_MODEL), jnp.float32) * s}
    _L0_attn_in = _L0_attn_setup()

    def _L0_ffn_setup():
        import jax, jax.numpy as jnp
        import numpy as np
        HIDDEN = 256
        INTER = 688
        LUT_SIZE = 16

        def _ghost_linear(x, idx, lut):
            w = lut[idx]
            return jnp.einsum('bsh,oh->bso', x, w)
        key = jax.random.key(seed)
        k_x, k_lut, k_g, k_u, k_d = jax.random.split(key, 5)
        x = jax.random.normal(k_x, (2, 512, HIDDEN), dtype=jnp.float32)
        lut = jax.random.normal(k_lut, (LUT_SIZE,), dtype=jnp.float32) * 0.02
        gate_idx = jax.random.randint(k_g, (INTER, HIDDEN), 0, LUT_SIZE, dtype=jnp.int32)
        up_idx = jax.random.randint(k_u, (INTER, HIDDEN), 0, LUT_SIZE, dtype=jnp.int32)
        down_idx = jax.random.randint(k_d, (HIDDEN, INTER), 0, LUT_SIZE, dtype=jnp.int32)
        return {'x': x, 'lut': lut, 'gate_idx': gate_idx, 'up_idx': up_idx, 'down_idx': down_idx}
    _L0_ffn_in = _L0_ffn_setup()

    def _L1_attn_setup():
        import jax, jax.numpy as jnp
        import numpy as np
        BATCH, SEQ, D_MODEL, N_HEADS, D_HEAD = (2, 256, 256, 16, 128)
        ATTN_SCALE = np.sqrt(D_HEAD).astype(np.float32)
        IGNORE = jnp.float32(-100000.0)
        key = jax.random.key(seed)
        ks = jax.random.split(key, 5)
        init = 1.0 / np.sqrt(D_MODEL)
        return {'x': jax.random.normal(ks[0], (BATCH, SEQ, D_MODEL), jnp.float32), 'W_Q': jax.random.normal(ks[1], (N_HEADS, D_MODEL, D_HEAD), jnp.float32) * init, 'W_K': jax.random.normal(ks[2], (N_HEADS, D_MODEL, D_HEAD), jnp.float32) * init, 'W_V': jax.random.normal(ks[3], (N_HEADS, D_MODEL, D_HEAD), jnp.float32) * init, 'W_O': jax.random.normal(ks[4], (N_HEADS, D_HEAD, D_MODEL), jnp.float32) * init, 'b_Q': jnp.zeros((N_HEADS, D_HEAD), jnp.float32), 'b_K': jnp.zeros((N_HEADS, D_HEAD), jnp.float32), 'b_V': jnp.zeros((N_HEADS, D_HEAD), jnp.float32), 'b_O': jnp.zeros((D_MODEL,), jnp.float32)}
    _L1_attn_in = _L1_attn_setup()

    def _L1_ffn_setup():
        import jax, jax.numpy as jnp
        import numpy as np
        ALPHA = 1.702
        LIMIT = 7.0
        TOP_K = 2
        E, H, I = (8, 256, 256)
        B, S = (2, 256)
        key = jax.random.key(seed)
        ks = jax.random.split(key, 7)
        return {'hidden_states': jax.random.normal(ks[0], (B, S, H), dtype=jnp.float32), 'router_weight': jax.random.normal(ks[1], (E, H), dtype=jnp.float32) * 0.02, 'router_bias': jax.random.normal(ks[2], (E,), dtype=jnp.float32) * 0.02, 'gate_up_proj': jax.random.normal(ks[3], (E, H, 2 * I), dtype=jnp.float32) * 0.02, 'gate_up_proj_bias': jax.random.normal(ks[4], (E, 2 * I), dtype=jnp.float32) * 0.02, 'down_proj': jax.random.normal(ks[5], (E, I, H), dtype=jnp.float32) * 0.02, 'down_proj_bias': jax.random.normal(ks[6], (E, H), dtype=jnp.float32) * 0.02}
    _L1_ffn_in = _L1_ffn_setup()
    _d = {'L0_attn_hidden_states': _L0_attn_in['hidden_states'], 'L0_attn_in_proj_w': _L0_attn_in['in_proj_w'], 'L0_attn_conv_w': _L0_attn_in['conv_w'], 'L0_attn_conv_b': _L0_attn_in['conv_b'], 'L0_attn_dt_bias': _L0_attn_in['dt_bias'], 'L0_attn_A_log': _L0_attn_in['A_log'], 'L0_attn_D': _L0_attn_in['D'], 'L0_attn_norm_w': _L0_attn_in['norm_w'], 'L0_attn_out_proj_w': _L0_attn_in['out_proj_w'], 'L0_attn_ln1_w': _L0_attn_in['ln1_w'], 'L0_attn_ln2_w': _L0_attn_in['ln2_w'], 'L0_attn_gate_w': _L0_attn_in['gate_w'], 'L0_attn_up_w': _L0_attn_in['up_w'], 'L0_attn_down_w': _L0_attn_in['down_w'], 'L0_ffn_lut': _L0_ffn_in['lut'], 'L0_ffn_gate_idx': _L0_ffn_in['gate_idx'], 'L0_ffn_up_idx': _L0_ffn_in['up_idx'], 'L0_ffn_down_idx': _L0_ffn_in['down_idx'], 'L1_attn_W_Q': _L1_attn_in['W_Q'], 'L1_attn_W_K': _L1_attn_in['W_K'], 'L1_attn_W_V': _L1_attn_in['W_V'], 'L1_attn_W_O': _L1_attn_in['W_O'], 'L1_attn_b_Q': _L1_attn_in['b_Q'], 'L1_attn_b_K': _L1_attn_in['b_K'], 'L1_attn_b_V': _L1_attn_in['b_V'], 'L1_attn_b_O': _L1_attn_in['b_O'], 'L1_ffn_router_weight': _L1_ffn_in['router_weight'], 'L1_ffn_router_bias': _L1_ffn_in['router_bias'], 'L1_ffn_gate_up_proj': _L1_ffn_in['gate_up_proj'], 'L1_ffn_gate_up_proj_bias': _L1_ffn_in['gate_up_proj_bias'], 'L1_ffn_down_proj': _L1_ffn_in['down_proj'], 'L1_ffn_down_proj_bias': _L1_ffn_in['down_proj_bias']}
    _x0 = _d['L0_attn_hidden_states']
    _d['L0_attn_hidden_states'] = jax.random.normal(jax.random.fold_in(jax.random.key(seed), 1), (2, 1024, 256), dtype=_x0.dtype)
    del _x0
    return _d

def reference(L0_attn_hidden_states, L0_attn_in_proj_w, L0_attn_conv_w, L0_attn_conv_b, L0_attn_dt_bias, L0_attn_A_log, L0_attn_D, L0_attn_norm_w, L0_attn_out_proj_w, L0_attn_ln1_w, L0_attn_ln2_w, L0_attn_gate_w, L0_attn_up_w, L0_attn_down_w, L0_ffn_lut, L0_ffn_gate_idx, L0_ffn_up_idx, L0_ffn_down_idx, L1_attn_W_Q, L1_attn_W_K, L1_attn_W_V, L1_attn_W_O, L1_attn_b_Q, L1_attn_b_K, L1_attn_b_V, L1_attn_b_O, L1_ffn_router_weight, L1_ffn_router_bias, L1_ffn_gate_up_proj, L1_ffn_gate_up_proj_bias, L1_ffn_down_proj, L1_ffn_down_proj_bias):

    def _L0_attn_ref(hidden_states, in_proj_w, conv_w, conv_b, dt_bias, A_log, D, norm_w, out_proj_w, ln1_w, ln2_w, gate_w, up_w, down_w):
        import jax, jax.numpy as jnp
        import numpy as np
        D_MODEL = 256
        D_INNER = 512
        D_XB = 128
        D_STATE = 64
        HEADDIM = 64
        NHEADS = D_INNER // HEADDIM
        NXB = D_XB // HEADDIM
        D_CONV = 4
        CHUNK = 128
        EPS = 1e-05
        D_FF = 1024
        CONV_DIM = D_XB + D_XB + D_INNER
        D_IN_PROJ = D_INNER + D_XB + D_XB + D_INNER + NHEADS

        def rmsnorm(x, w, eps=EPS):
            return x * jax.lax.rsqrt(jnp.mean(x * x, axis=-1, keepdims=True) + eps) * w

        def causal_depthwise_conv(x, w, b):
            k = w.shape[1]
            xp = jnp.pad(x, ((0, 0), (k - 1, 0), (0, 0)))
            out = jax.lax.conv_general_dilated(xp.transpose(0, 2, 1), w[:, None, :], (1,), 'VALID', feature_group_count=x.shape[-1])
            return out.transpose(0, 2, 1) + b

        def ssd_chunked(xdt, dA, Bm, Cm):
            b, l, h, p = xdt.shape
            n = Bm.shape[-1]
            c, q = (l // CHUNK, CHUNK)
            xdt = xdt.reshape(b, c, q, h, p)
            Bm = Bm.reshape(b, c, q, h, n)
            Cm = Cm.reshape(b, c, q, h, n)
            dA = dA.reshape(b, c, q, h).transpose(0, 3, 1, 2)
            dAc = jnp.cumsum(dA, axis=-1)
            seg = dAc[..., :, None] - dAc[..., None, :]
            mask = jnp.tril(jnp.ones((q, q), bool))
            Lm = jnp.where(mask, jnp.exp(seg), 0.0)
            Y_diag = jnp.einsum('bcqhn,bcshn,bhcqs,bcshp->bcqhp', Cm, Bm, Lm, xdt)
            decay_states = jnp.exp(dAc[..., -1:] - dAc)
            states = jnp.einsum('bcqhn,bhcq,bcqhp->bchpn', Bm, decay_states, xdt)
            chunk_decay = jnp.exp(dAc[..., -1])

            def step(carry, inp):
                s, d = inp
                new = s + d[:, :, None, None] * carry
                return (new, carry)
            init = jnp.zeros((b, h, p, n), xdt.dtype)
            _, prevs = jax.lax.scan(step, init, (states.transpose(1, 0, 2, 3, 4), chunk_decay.transpose(2, 0, 1)))
            Y_off = jnp.einsum('bcqhn,cbhpn,bhcq->bcqhp', Cm, prevs, jnp.exp(dAc))
            return (Y_diag + Y_off).reshape(b, l, h, p)

        def mamba2(x, in_proj_w, conv_w, conv_b, dt_bias, A_log, Dp, norm_w, out_proj_w):
            b, l, _ = x.shape
            zxbcdt = x @ in_proj_w
            z, xb, Bc, Cc, dt = jnp.split(zxbcdt, [D_INNER, D_INNER + D_XB, D_INNER + 2 * D_XB, 2 * D_INNER + 2 * D_XB], axis=-1)
            xBC = jax.nn.silu(causal_depthwise_conv(jnp.concatenate([xb, Bc, Cc], -1), conv_w, conv_b))
            xb, Bc, Cc = jnp.split(xBC, [D_XB, 2 * D_XB], axis=-1)
            dt = jax.nn.softplus(dt + dt_bias)
            A = -jnp.exp(A_log)
            rep = NHEADS // NXB
            x_h = jnp.repeat(xb.reshape(b, l, NXB, HEADDIM), rep, axis=2)
            B_h = jnp.repeat(Bc.reshape(b, l, NXB, D_STATE), rep, axis=2)
            C_h = Cc.reshape(b, l, NHEADS, D_STATE)
            y = ssd_chunked(x_h * dt[..., None], dt * A, B_h, C_h)
            y = y + Dp[None, None, :, None] * x_h
            y = y.reshape(b, l, D_INNER)
            y = rmsnorm(y * jax.nn.silu(z), norm_w)
            return y @ out_proj_w
        residual = hidden_states
        h = rmsnorm(hidden_states, ln1_w)
        h = residual + mamba2(h, in_proj_w, conv_w, conv_b, dt_bias, A_log, D, norm_w, out_proj_w)
        residual = h
        h2 = rmsnorm(h, ln2_w)
        mlp = jax.nn.silu(h2 @ gate_w) * (h2 @ up_w) @ down_w
        return residual + mlp

    def _L0_ffn_ref(x, lut, gate_idx, up_idx, down_idx):
        import jax, jax.numpy as jnp
        import numpy as np
        HIDDEN = 256
        INTER = 688
        LUT_SIZE = 16

        def _ghost_linear(x, idx, lut):
            w = lut[idx]
            return jnp.einsum('bsh,oh->bso', x, w)
        gate = _ghost_linear(x, gate_idx, lut)
        up = _ghost_linear(x, up_idx, lut)
        h = jax.nn.silu(gate) * up
        return _ghost_linear(h, down_idx, lut)

    def _L1_attn_ref(x, W_Q, W_K, W_V, W_O, b_Q, b_K, b_V, b_O):
        import jax, jax.numpy as jnp
        import numpy as np
        BATCH, SEQ, D_MODEL, N_HEADS, D_HEAD = (2, 256, 256, 16, 128)
        ATTN_SCALE = np.sqrt(D_HEAD).astype(np.float32)
        IGNORE = jnp.float32(-100000.0)
        q = jnp.einsum('bpd,hde->bphe', x, W_Q) + b_Q
        k = jnp.einsum('bpd,hde->bphe', x, W_K) + b_K
        v = jnp.einsum('bpd,hde->bphe', x, W_V) + b_V
        scores = jnp.einsum('bqhe,bkhe->bhqk', q, k) / ATTN_SCALE
        S = x.shape[1]
        causal = jnp.tril(jnp.ones((S, S), bool))
        scores = jnp.where(causal, scores, IGNORE)
        attn = jax.nn.softmax(scores, axis=-1)
        z = jnp.einsum('bkhe,bhqk->bqhe', v, attn)
        out = jnp.einsum('bqhe,hed->bqd', z, W_O) + b_O
        return out

    def _L1_ffn_ref(hidden_states, router_weight, router_bias, gate_up_proj, gate_up_proj_bias, down_proj, down_proj_bias):
        import jax, jax.numpy as jnp
        import numpy as np
        ALPHA = 1.702
        LIMIT = 7.0
        TOP_K = 2
        E, H, I = (8, 256, 256)
        B, S = (2, 256)
        bsz, seq_len, hidden = hidden_states.shape
        h = hidden_states.reshape(-1, hidden)
        T = h.shape[0]
        logits = h @ router_weight.T + router_bias
        top_vals, top_idx = jax.lax.top_k(logits, TOP_K)
        top_w = jax.nn.softmax(top_vals, axis=-1)
        scores = jnp.zeros_like(logits).at[jnp.arange(T)[:, None], top_idx].set(top_w)
        gate_up = jnp.einsum('th,ehj->etj', h, gate_up_proj) + gate_up_proj_bias[:, None, :]
        gate = gate_up[..., ::2]
        up = gate_up[..., 1::2]
        gate = jnp.minimum(gate, LIMIT)
        up = jnp.clip(up, -LIMIT, LIMIT)
        glu = gate * jax.nn.sigmoid(gate * ALPHA)
        act = (up + 1.0) * glu
        expert_out = jnp.einsum('eti,eih->eth', act, down_proj) + down_proj_bias[:, None, :]
        out = jnp.einsum('te,eth->th', scores, expert_out)
        return out.reshape(bsz, seq_len, hidden)
    x = L0_attn_hidden_states
    x = x + _L0_attn_ref(_layernorm(x, axis=-1), L0_attn_in_proj_w, L0_attn_conv_w, L0_attn_conv_b, L0_attn_dt_bias, L0_attn_A_log, L0_attn_D, L0_attn_norm_w, L0_attn_out_proj_w, L0_attn_ln1_w, L0_attn_ln2_w, L0_attn_gate_w, L0_attn_up_w, L0_attn_down_w)
    x = x + _L0_ffn_ref(_layernorm(x, axis=-1), L0_ffn_lut, L0_ffn_gate_idx, L0_ffn_up_idx, L0_ffn_down_idx)
    x = x + _L1_attn_ref(_layernorm(x, axis=-1), L1_attn_W_Q, L1_attn_W_K, L1_attn_W_V, L1_attn_W_O, L1_attn_b_Q, L1_attn_b_K, L1_attn_b_V, L1_attn_b_O)
    x = x + _L1_ffn_ref(_layernorm(x, axis=-1), L1_ffn_router_weight, L1_ffn_router_bias, L1_ffn_gate_up_proj, L1_ffn_gate_up_proj_bias, L1_ffn_down_proj, L1_ffn_down_proj_bias)
    return x

_drawn_inputs = setup_inputs


def setup_inputs(seed=0):
    import zlib

    import numpy as np

    out = dict(_drawn_inputs(seed))
    spreads = {'L0_attn_conv_b': (0.0, 0.1),
     'L0_attn_D': (1.0, 0.6),
     'L0_attn_norm_w': (1.0, 0.2),
     'L0_attn_ln1_w': (1.0, 0.2),
     'L0_attn_ln2_w': (1.0, 0.6),
     'L1_attn_b_Q': (0.0, 0.455),
     'L1_attn_b_K': (0.0, 0.8),
     'L1_attn_b_V': (0.0, 0.1),
     'L1_attn_b_O': (0.0, 0.1)}
    factors = {'L0_attn_dt_bias': 8.0,
     'L0_attn_A_log': 8.0,
     'L0_attn_gate_w': 3.03,
     'L0_attn_up_w': 2.99,
     'L0_attn_down_w': 2.994,
     'L0_ffn_lut': 2.754,
     'L1_ffn_router_weight': 3.111,
     'L1_ffn_router_bias': 8.0,
     'L1_ffn_gate_up_proj': 2.95,
     'L1_ffn_gate_up_proj_bias': 8.0,
     'L1_ffn_down_proj': 2.882,
     'L1_ffn_down_proj_bias': 8.0}
    for name, (base, spread) in spreads.items():
        noise = np.random.default_rng([zlib.crc32(name.encode()), seed]).standard_normal(out[name].shape)
        drawn = base * np.exp(spread * noise) if base else spread * noise
        out[name] = jnp.asarray(drawn.astype(out[name].dtype))
    for name, factor in factors.items():
        out[name] = (out[name] * factor).astype(out[name].dtype)
    return out
```

```python
from contextlib import ExitStack

import concourse.bass as bass
from concourse import mybir

F32 = mybir.dt.float32
F32R = mybir.dt.float32r
BF16 = mybir.dt.bfloat16
I32 = mybir.dt.int32
ALU = mybir.AluOpType
ACT = mybir.ActivationFunctionType
AX_X = mybir.AxisListType.X

P = 128
BATCH, SEQ, D = 2, 1024, 256
KD = D // P
TILES = BATCH * SEQ // P
GROUP = 512
TG = GROUP // P
GROUPS = TILES // TG
EPS = 1e-5
INNER, XB, STATE, HEAD, HEADS = 512, 128, 64, 64, 8
REP = HEADS // 2
XBC_BLOCKS = (XB + XB + INNER) // P
Z_BLOCKS = INNER // P
TAPS = 4
CHUNKS = SEQ // P
FF = 1024
LUT_FF, LUT_SIZE = 688, 16
AH, AE = 16, 128
PAIRS = AH // 2
SCORE_SCALE = float(AE) ** -0.5
MASKED = -1.0e30
QT = SEQ // P
EXPERTS, EI = 8, 256
ALPHA, LIMIT = 1.702, 7.0


def chunk_sizes(n):
    return [min(P, n - at) for at in range(0, n, P)]


def three_passes(pe, out, stationary, moving, start, stop):
    (s_hi, s_lo), (m_hi, m_lo) = stationary, moving
    pe.matmul(out, s_hi, m_hi, start=start, stop=False)
    pe.matmul(out, s_hi, m_lo, start=False, stop=False)
    return pe.matmul(out, s_lo, m_hi, start=False, stop=stop)


def pair_at(pair, *where):
    return tuple(t[where] for t in pair)


class Shared:
    pass


def shared_memory(nc, mem):
    s = Shared()
    s.psum = mem.enter_context(nc.psum_tensor("psum", [P, 8, 512], F32))
    s.x = mem.enter_context(nc.sbuf_tensor("x_tok", [P, TILES, D], F32))
    s.act_hi = mem.enter_context(nc.sbuf_tensor("act_hi", [P, KD, TILES * P], F32R))
    s.act_lo = mem.enter_context(nc.sbuf_tensor("act_lo", [P, KD, TILES * P], F32R))
    s.act = (s.act_hi, s.act_lo)
    s.ident = mem.enter_context(nc.sbuf_tensor("ident", [P, P], F32))
    s.upper = mem.enter_context(nc.sbuf_tensor("upper", [P, P], F32))
    s.ones = mem.enter_context(nc.sbuf_tensor("ones", [P, P], F32))
    s.minus_half = mem.enter_context(nc.sbuf_tensor("minus_half", [P, 16], F32))
    s.wait_over = mem.enter_context(nc.semaphore("wait_over"))
    s.consts_ready = mem.enter_context(nc.semaphore("consts_ready"))
    return s


CONSTS = 6


def constants(nc, s):

    def gpsimd(pool):
        pool.memset(s.ident[:, :], 0.0).then_inc(s.consts_ready, 1)
        pool.memset(s.upper[:, :], 1.0).then_inc(s.consts_ready, 1)
        pool.memset(s.ones[:, :], 1.0).then_inc(s.consts_ready, 1)
        pool.memset(s.minus_half[:, :], -0.5).then_inc(s.consts_ready, 1)
        pool.wait_ge(s.consts_ready, 4)
        pool.affine_select(out=s.ident[:, :], in_=s.ident[:, :], compare_op=ALU.not_equal, fill=1.0, base=0,
                           pattern=[[-1, P]], channel_multiplier=1).then_inc(s.consts_ready, 1)
        pool.affine_select(out=s.upper[:, :], in_=s.upper[:, :], compare_op=ALU.is_ge, fill=0.0, base=0,
                           pattern=[[1, P]], channel_multiplier=-1).then_inc(s.consts_ready, 1)

    return gpsimd


def norm_stage(nc, sems, mem, s, name, source, mode, weight=None, keep=None, loaded=None):
    roots = 2 if mode == "layer_rms" else 1

    def sem(what):
        return sems.enter_context(nc.semaphore(f"{name}_{what}"))

    var_ready, root_ready, normed, turned, hi_ready = (
        sem(x) for x in ("var_ready", "root_ready", "normed", "turned", "hi_ready"))
    split_ready = sem("split_ready")
    stats = mem.enter_context(nc.sbuf_tensor(f"{name}_stats", [P, TG, 6], F32))
    moments = mem.enter_context(nc.sbuf_tensor(f"{name}_moments", [P, TG, 2], F32))
    var = mem.enter_context(nc.sbuf_tensor(f"{name}_var", [P, TG], F32))
    root = mem.enter_context(nc.sbuf_tensor(f"{name}_root", [P, TG], F32))
    root2 = mem.enter_context(nc.sbuf_tensor(f"{name}_root2", [P, TG], F32))
    normal = mem.enter_context(nc.sbuf_tensor(f"{name}_normal", [P, TG, D], F32))

    def vector(dve):
        dve.drain()
        if loaded is not None:
            dve.wait_ge(loaded, 16 * GROUPS)
        with dve.Fori(0, GROUPS) as i:
            for t in range(TG):
                dve.bn_stats(stats[:, t, :], source[:, i * TG + t, :])
            dve.drain()
            for t in range(TG):
                dve.bn_aggr(moments[:, t, :], stats[:, t, :])
            dve.drain()
            if mode == "rms":
                dve.tensor_tensor(var[:, :], moments[:, :, 0], moments[:, :, 0], ALU.mult)
                dve.drain()
                dve.tensor_tensor(var[:, :], var[:, :], moments[:, :, 1], ALU.add)
                dve.drain()
                dve.tensor_scalar(var[:, :], var[:, :], EPS, None, ALU.add).then_inc(var_ready, 1)
            else:
                dve.tensor_scalar(var[:, :], moments[:, :, 1], EPS, None, ALU.add).then_inc(var_ready, 1)
            dve.wait_ge(root_ready, roots * i + 1)
            dve.wait_ge(turned, KD * i)
            if mode == "layer_rms":
                dve.tensor_tensor(var[:, :], moments[:, :, 1], root[:, :], ALU.mult)
                dve.drain()
                dve.tensor_tensor(var[:, :], var[:, :], root[:, :], ALU.mult)
                dve.drain()
                dve.tensor_scalar(var[:, :], var[:, :], EPS, None, ALU.add).then_inc(var_ready, 1)
                for t in range(TG):
                    dve.tensor_scalar(keep[:, i * TG + t, :], source[:, i * TG + t, :], moments[:, t, 0:1],
                                      root[:, t:t + 1], ALU.subtract, ALU.mult)
                dve.drain()
                dve.wait_ge(root_ready, 2 * i + 2)
                for t in range(TG):
                    last = dve.tensor_scalar(normal[:, t, :], keep[:, i * TG + t, :], root2[:, t:t + 1], None,
                                             ALU.mult)
            elif mode == "rms":
                for t in range(TG):
                    last = dve.tensor_scalar(normal[:, t, :], source[:, i * TG + t, :], root[:, t:t + 1], None,
                                             ALU.mult)
            else:
                for t in range(TG):
                    last = dve.tensor_scalar(normal[:, t, :], source[:, i * TG + t, :], moments[:, t, 0:1],
                                             root[:, t:t + 1], ALU.subtract, ALU.mult)
            last.then_inc(normed, 1)
            for k in range(KD):
                dve.wait_ge(hi_ready, KD * i + k + 1)
                dve.scalar_tensor_tensor(
                    s.act_lo[:, k, bass.ds(i * GROUP, GROUP)], s.psum[:, k, :], 1.0 if weight is None else weight[:, k:k + 1],
                    s.act_hi[:, k, bass.ds(i * GROUP, GROUP)].bitcast(F32), ALU.mult, ALU.subtract).then_inc(split_ready, 1)

    def gpsimd(pool):
        pool.wait_ge(s.consts_ready, CONSTS)
        with pool.Fori(0, GROUPS) as i:
            pool.wait_ge(var_ready, roots * i + 1)
            pool.tensor_tensor(root[:, :], var[:, :], s.minus_half[:, 0:TG], ALU.pow).then_inc(root_ready, 1)
            if roots == 2:
                pool.wait_ge(var_ready, 2 * i + 2)
                pool.tensor_tensor(root2[:, :], var[:, :], s.minus_half[:, 0:TG], ALU.pow).then_inc(root_ready, 1)

    def tensor(pe):
        pe.wait_ge(s.consts_ready, CONSTS)
        with pe.Fori(0, GROUPS) as i:
            pe.wait_ge(normed, i + 1)
            pe.wait_ge(split_ready, KD * i)
            for k in range(KD):
                for t in range(TG):
                    last = pe.transpose(s.psum[:, k, t * P:(t + 1) * P], normal[:, t, k * P:(k + 1) * P], s.ident[:, :])
                last.then_inc(turned, 1)

    def scalar(act):
        with act.Fori(0, GROUPS) as i:
            for k in range(KD):
                act.wait_ge(turned, KD * i + k + 1)
                act.activation(s.act_hi[:, k, bass.ds(i * GROUP, GROUP)], s.psum[:, k, :], ACT.Copy,
                               scale=1.0 if weight is None else weight[:, k:k + 1]).then_inc(hi_ready, 1)

    return dict(vector=vector, gpsimd=gpsimd, tensor=tensor, scalar=scalar, done=(split_ready, KD * GROUPS))


def gated_stage(nc, sems, mem, s, name, blocks, weights, weights_ready, residual=None, before=None):
    gate_w, up_w, down_w = weights

    def sem(what):
        return sems.enter_context(nc.semaphore(f"{name}_{what}"))

    products, tanh_ready, hidden_done, hi_ready, hidden_split, down_ready, added = (
        sem(x) for x in ("products", "tanh_ready", "hidden_done", "hi_ready", "hidden_split", "down_ready", "added"))
    th = mem.enter_context(nc.sbuf_tensor(f"{name}_th", [P, 2, GROUP], F32))
    silu = mem.enter_context(nc.sbuf_tensor(f"{name}_silu", [P, 2, GROUP], F32))
    hidden = mem.enter_context(nc.sbuf_tensor(f"{name}_hidden", [P, 2, GROUP], F32))
    h_hi = mem.enter_context(nc.sbuf_tensor(f"{name}_h_hi", [P, blocks, GROUP], F32R))
    h_lo = mem.enter_context(nc.sbuf_tensor(f"{name}_h_lo", [P, blocks, GROUP], F32R))
    hid = (h_hi, h_lo)
    total = mem.enter_context(nc.sbuf_tensor(f"{name}_total", [P, 2 * D], F32))
    HALVES = TG // 2

    def tensor(pe):
        for ready, value in weights_ready:
            pe.wait_ge(ready, value)
        if before is not None:
            pe.wait_ge(*before)
        with pe.Fori(0, GROUPS) as i:
            for f in range(blocks):
                pe.wait_ge(hidden_done, blocks * i + f + 1)
                for bank, w in ((2 * (f % 2), gate_w), (2 * (f % 2) + 1, up_w)):
                    for k in range(KD):
                        last = three_passes(pe, s.psum[:, bank, :], pair_at(w, slice(None), k, slice(f * P, (f + 1) * P)),
                                            pair_at(s.act, slice(None), k, bass.ds(i * GROUP, GROUP)),
                                            k == 0, k == KD - 1)
                last.then_inc(products, 1)
            pe.wait_ge(hidden_split, blocks * (i + 1))
            pe.wait_ge(added, HALVES * i)
            for half in range(HALVES):
                for t in (2 * half, 2 * half + 1):
                    for f in range(blocks):
                        last = three_passes(pe, s.psum[:, 4 + half, (t % 2) * D:(t % 2 + 1) * D],
                                            pair_at(hid, slice(None), f, slice(t * P, (t + 1) * P)),
                                            pair_at(down_w, slice(None), f), f == 0, f == blocks - 1)
                last.then_inc(down_ready, 1)

    def scalar(act):
        with act.Fori(0, GROUPS) as i:
            for f in range(blocks + 1):
                if f < blocks:
                    act.wait_ge(products, blocks * i + f + 1)
                    act.activation(th[:, f % 2, :], s.psum[:, 2 * (f % 2), :], ACT.Tanh, scale=0.5).then_inc(tanh_ready, 1)
                if f >= 1:
                    act.wait_ge(hidden_done, 2 + blocks * i + f)
                    if f == 1:
                        act.wait_ge(down_ready, HALVES * i)
                    act.activation(h_hi[:, f - 1, :], hidden[:, (f - 1) % 2, :], ACT.Copy).then_inc(hi_ready, 1)

    def gpsimd(pool):
        with pool.Fori(0, GROUPS) as i:
            for f in range(blocks):
                pool.wait_ge(hi_ready, blocks * i + f + 1)
                pool.tensor_tensor(h_lo[:, f, :], hidden[:, f % 2, :], h_hi[:, f, :].bitcast(F32),
                                   ALU.subtract).then_inc(hidden_split, 1)

    def vector(dve):
        dve.sem_inc(hidden_done, 2)
        with dve.Fori(0, GROUPS) as i:
            for f in range(blocks):
                dve.wait_ge(tanh_ready, blocks * i + f + 1)
                dve.scalar_tensor_tensor(silu[:, f % 2, :], th[:, f % 2, :], 1.0, s.psum[:, 2 * (f % 2), :], ALU.add, ALU.mult)
                dve.drain()
                if f >= 2:
                    dve.wait_ge(hidden_split, blocks * i + f - 1)
                else:
                    dve.wait_ge(hidden_split, blocks * i)
                dve.tensor_tensor(hidden[:, f % 2, :], silu[:, f % 2, :], s.psum[:, 2 * (f % 2) + 1, :],
                                  ALU.mult).then_inc(hidden_done, 1)
            for half in range(HALVES):
                dve.wait_ge(down_ready, HALVES * i + half + 1)
                sums = s.psum[:, 4 + half, :]
                x = s.x[:, bass.ds(i * TG + 2 * half, 2), :].rearrange("p t d -> p (t d)")
                if residual is not None:
                    dve.tensor_tensor(total[:, :], sums,
                                      residual[:, bass.ds(i * TG + 2 * half, 2), :].rearrange("p t d -> p (t d)"), ALU.add)
                    dve.drain()
                    dve.tensor_tensor(x, x, total[:, :], ALU.add).then_inc(added, 1)
                else:
                    dve.tensor_tensor(x, x, sums, ALU.add).then_inc(added, 1)
                dve.drain()

    return dict(vector=vector, gpsimd=gpsimd, tensor=tensor, scalar=scalar, done=(added, HALVES * GROUPS))


def split_weights(nc, sems, name, loaded, jobs):
    scaled = sems.enter_context(nc.semaphore(f"{name}_scaled"))
    hi_ready = sems.enter_context(nc.semaphore(f"{name}_weights_hi"))
    split_ready = sems.enter_context(nc.semaphore(f"{name}_weights_split"))

    def scalar(act):
        n = 0
        act.wait_ge(*loaded)
        for raw, hi, lo, scale in jobs:
            if scale is not None:
                act.activation(raw, raw, ACT.Copy, scale=scale).then_inc(scaled, 1)
                n += 1
                act.wait_ge(scaled, n)
            act.activation(hi, raw, ACT.Copy).then_inc(hi_ready, 1)

    def gpsimd(pool):
        pool.wait_ge(*loaded)
        for n, (raw, hi, lo, scale) in enumerate(jobs):
            pool.wait_ge(hi_ready, n + 1)
            pool.tensor_tensor(lo, raw, hi.bitcast(F32), ALU.subtract).then_inc(split_ready, 1)

    return dict(scalar=scalar, gpsimd=gpsimd, done=(split_ready, len(jobs)))


def table_stage(nc, sems, mem, s, lut, gate_idx, up_idx, down_idx, gate_t, up_t, down_t):

    def sem(what):
        return sems.enter_context(nc.semaphore(f"table_{what}"))

    loaded, steps_ready, bit_ready, leaves_ready, picked, turned, hi_ready, split_ready, zeroed = (
        sem(x) for x in ("table_loaded", "steps_ready", "bit_ready", "leaves_ready", "picked", "turned", "hi_ready",
                         "split_ready", "zeroed"))
    idx_loaded = [sem(f"idx_loaded_{n}") for n in range(2)]
    WIDTH = 3 * D
    PADS = 6
    full, rest = divmod(LUT_FF, P)
    table = mem.enter_context(nc.sbuf_tensor("table", [P, LUT_SIZE], F32))
    steps = mem.enter_context(nc.sbuf_tensor("table_steps", [P, LUT_SIZE // 2], F32))
    idx = mem.enter_context(nc.sbuf_tensor("table_idx", [P, 2, WIDTH], I32))
    bits = mem.enter_context(nc.sbuf_tensor("table_bits", [P, 4, WIDTH], I32))
    leaves = mem.enter_context(nc.sbuf_tensor("table_leaves", [P, LUT_SIZE // 2, WIDTH], F32))
    pieces, halved = [], set()
    for src, out in ((gate_idx, gate_t), (up_idx, up_t)):
        for first, n in ((0, 3), (3, full - 3)):
            loads = [(lambda i, n=n: i.rearrange("p (c d) -> p c d", c=n),
                      src[first * P:(first + n) * P, :].rearrange("(c p) d -> p c d", p=P))]
            turns = [(k, c * P, P, c * D + k * P, P) for k in range(KD) for c in range(n)]
            evac = [(k, P, n * P, pair_at(out, slice(None), k, slice(first * P, (first + n) * P))) for k in range(KD)]
            pieces.append((loads, P, n * D, turns, evac))
    loads = [(lambda i, n=n: i[:, n * D:(n + 1) * D], src[full * P:LUT_FF, :]) for n, src in enumerate((gate_idx, up_idx))]
    turns = [(k, n * P, rest, n * D + k * P, P) for n in range(2) for k in range(KD)]
    evac = [(k, P, (n * P, rest), pair_at(out, slice(None), k, slice(full * P, LUT_FF)))
            for n, out in enumerate((gate_t, up_t)) for k in range(KD)]
    pieces.append((loads, rest, 2 * D, turns, evac))
    for o in range(KD):
        loads = [(lambda i: i, down_idx[o * P:(o + 1) * P, :])]
        turns = [(f // 4, (f % 4) * P, P, f * P, P if f < full else rest) for f in range(full + 1)]
        cols = slice(o * P, (o + 1) * P)
        evac = [(0, P, 4 * P, pair_at(down_t, slice(None), slice(0, 4), cols)),
                (1, P, P, pair_at(down_t, slice(None), 4, cols)),
                (1, rest, (P, P), pair_at(down_t, slice(0, rest), 5, cols))]
        pieces.append((loads, P, LUT_FF, turns, evac))
        halved.add(len(pieces) - 1)
    n_loads = [sum(len(p[0]) for p in pieces[n % 2:n + 1:2]) for n in range(len(pieces))]
    n_evac = [sum(len(p[4]) for p in pieces[:n]) for n in range(len(pieces) + 1)]

    def sync(sp):
        sp.dma_start(table[:, :], lut.partition_broadcast(P)).then_inc(loaded, 16)
        for n, (loads, rows, width, _, _) in enumerate(pieces):
            if n >= 2:
                sp.wait_ge(bit_ready, n - 1)
            for place, src in loads:
                sp.dma_start(place(idx[0:rows, n % 2, 0:width]), src).then_inc(idx_loaded[n % 2], 16)

    def vector(dve):
        dve.wait_ge(loaded, 16)
        dve.tensor_tensor(steps[:, :], table[:, 1::2], table[:, 0::2], ALU.subtract).then_inc(steps_ready, 1)
        for n, (_, rows, width, _, _) in enumerate(pieces):
            dve.wait_ge(idx_loaded[n % 2], 16 * n_loads[n])
            for b in range(4):
                last = dve.tensor_scalar(bits[0:rows, b, 0:width], idx[0:rows, n % 2, 0:width], 1 << b, None,
                                         ALU.bitwise_and)
            last.then_inc(bit_ready, 1)
            dve.drain()
            dve.wait_ge(leaves_ready, n + 1)
            for b, step in ((1, 1), (2, 2), (3, 4)):
                for j in range(0, LUT_SIZE // 2, 2 * step):
                    last = dve.copy_predicated(leaves[0:rows, j, 0:width], bits[0:rows, b, 0:width],
                                               leaves[0:rows, j + step, 0:width])
                dve.drain()
            last.then_inc(picked, 1)
            evacuate(dve, n)

    def evacuate(dve, n):
        dve.wait_ge(hi_ready, n_evac[n + 1])
        for bank, rows, cols, out in pieces[n][4]:
            dve.scalar_tensor_tensor(out[1], turned_at(bank, rows, cols, out[1]), scale(n), out[0].bitcast(F32), ALU.mult,
                                     ALU.subtract).then_inc(split_ready, 1)

    def scale(n):
        return 0.5 if n in halved else 1.0

    def turned_at(bank, rows, cols, like):
        first, n = cols if isinstance(cols, tuple) else (0, cols)
        view = s.psum[0:rows, bank, first:first + n]
        return view.rearrange("p (a b) -> p a b", b=P) if len(like.shape) == 3 else view

    def scalar(act):
        act.wait_ge(steps_ready, 1)
        act.wait_ge(zeroed, PADS)
        for n, (_, rows, width, _, evac) in enumerate(pieces):
            act.wait_ge(bit_ready, n + 1)
            act.wait_ge(turned, n)
            for j in range(LUT_SIZE // 2):
                last = act.activation(leaves[0:rows, j, 0:width], bits[0:rows, 0, 0:width], ACT.Identity,
                                      scale=steps[0:rows, j:j + 1], bias=table[0:rows, 2 * j:2 * j + 1])
            last.then_inc(leaves_ready, 1)
            act.wait_ge(turned, n + 1)
            for bank, r, cols, out in evac:
                act.activation(out[0], turned_at(bank, r, cols, out[0]), ACT.Copy, scale=scale(n)).then_inc(hi_ready, 1)

    def gpsimd(pool):
        for part in (0, 1):
            for pad in (gate_t[part][:, :, LUT_FF:], up_t[part][:, :, LUT_FF:], down_t[part][:, full, :]):
                pool.memset(pad.bitcast(F32), 0.0).then_inc(zeroed, 1)

    def tensor(pe):
        pe.wait_ge(s.consts_ready, CONSTS)
        for n, (_, rows, width, turns, _) in enumerate(pieces):
            pe.wait_ge(picked, n + 1)
            pe.wait_ge(split_ready, n_evac[n])
            for bank, at, size, col, out_rows in turns:
                last = pe.transpose(s.psum[0:out_rows, bank, at:at + size], leaves[0:size, 0, col:col + out_rows],
                                    s.ident[0:size, 0:size])
            last.then_inc(turned, 1)

    return dict(sync=sync, vector=vector, scalar=scalar, gpsimd=gpsimd, tensor=tensor, done=(split_ready, n_evac[-1]),
                zeroed=(zeroed, PADS))


def mamba_stage(nc, sems, mem, s, w, dma, u):

    def sem(what):
        return sems.enter_context(nc.semaphore(f"mamba_{what}"))

    def sb(what, shape, dt=F32):
        return mem.enter_context(nc.sbuf_tensor(f"mamba_{what}", shape, dt))

    names = ("prep dt_product dt_biased dt_exp dt_log dt_log_in dt_done sums_ready sums_copied decay_rate "
             "projected evacuated conv_sum conv_tanh conv_done gate_tanh gate_done "
             "steps rows_ready seg masked row_exp leaves turned b_copied xdt mixed scores_ready c_scaled xdt_decayed "
             "lower_done y_ready state_ready state_done gated gated_hi squares gated_lo out_ready out_var out_root out_done")

    done = {n: sem(n) for n in names.split()}

    conv_in = sb("conv_in", [P, XBC_BLOCKS, GROUP + TAPS - 1])
    conv_sum = sb("conv_sum", [P, 2, GROUP])
    conv_th = sb("conv_th", [P, 2, GROUP])
    xbc = sb("xbc", [P, 2, XBC_BLOCKS, GROUP])
    zs = sb("zs", [P, 2, Z_BLOCKS, GROUP])
    step_dt = sb("step_dt", [P, TILES, HEADS])
    step_da = sb("step_da", [P, TILES, HEADS])
    cum = sb("cum", [P, TILES, HEADS])
    d_head = sb("d_head", [P, Z_BLOCKS, P])
    steps = sb("steps", [P, HEADS, P])
    decay = sb("decay", [P, 2, HEADS, P])
    mixed = sb("mixed", [P, 2, HEADS, P])
    row_exp = sb("row_exp", [P, 2, REP, P])
    b_tok = sb("b_tok", [P, 2, P])
    xdt = sb("xdt", [P, 2, HEADS, HEAD])
    xdt_decayed = sb("xdt_decayed", [P, 2, HEADS, HEAD])
    c_scaled = sb("c_scaled", [P, 2, REP, P])
    state = sb("state", [P, REP, HEAD])
    gated = sb("gated", [P, Z_BLOCKS, P])
    gated_hi = sb("gated_hi", [P, Z_BLOCKS, P], F32R)
    gated_lo = sb("gated_lo", [P, Z_BLOCKS, P], F32R)
    squares = sb("squares", [P, Z_BLOCKS, P])
    out_var = sb("out_var", [P, 1])
    out_root = sb("out_root", [P, 1])

    IP = XBC_BLOCKS + Z_BLOCKS
    GB = SEQ // GROUP
    events = [("project", 0, m) for m in range(IP)]
    for c in range(CHUNKS + 2):
        if c < CHUNKS:
            events.append(("A", c, None))
        if 1 <= c <= CHUNKS:
            events.append(("B", c - 1, None))
        if c >= 2:
            events.append(("C", c - 2, None))
        if c < CHUNKS:
            events.append(("A_end", c, None))
        if c < TG:
            events += [("project", 1, m) for m in range(3 * c, min(3 * c + 3, IP))]
    PER = dict(conv=GB * XBC_BLOCKS, z=GB * Z_BLOCKS, chunk=CHUNKS, ring=GB * IP + CHUNKS)
    order = {}
    for e in events:
        if e[0] == "project":
            order[e] = ("conv", e[1] * XBC_BLOCKS + e[2]) if e[2] < XBC_BLOCKS else ("z", e[1] * Z_BLOCKS + e[2] - XBC_BLOCKS)
    ring = [e for e in events if e[0] in ("project", "C")]
    bank_of = {e: 6 + n % 2 for n, e in enumerate(ring)}
    before = {e: ring[n - 2] if n >= 2 else None for n, e in enumerate(ring)}

    def bank(e):
        return s.psum[:, bank_of[e], :]

    def prep_vector(dve):
        dve.wait_ge(dma["small"][0], dma["small"][1])
        dve.wait_ge(s.consts_ready, CONSTS)
        dve.tensor_scalar(w["conv_w"][:, :, :], w["conv_w"][:, :, :], 0.5, None, ALU.mult)
        dve.tensor_scalar(w["conv_b"][:, :], w["conv_b"][:, :], 0.5, None, ALU.mult)
        for h in range(HEADS):
            g, at = h // REP, (h % 2) * HEAD
            dve.tensor_scalar(d_head[:, h // 2, at:at + HEAD], s.ident[:, g * HEAD:(g + 1) * HEAD], w["D"][:, h:h + 1],
                              None, ALU.mult)
        dve.wait_ge(*dma["w_out"])
        for k in range(Z_BLOCKS):
            last = dve.tensor_scalar(w["out_raw"][:, k, :], w["out_raw"][:, k, :], w["norm_w"][:, k:k + 1], 0.5,
                                     ALU.mult, ALU.mult)
        last.then_inc(done["prep"], 1)
        dve.wait_ge(*dma["in_split"])
        dve.wait_ge(*dma["out_split"])
        dve.wait_ge(done["decay_rate"], 1)
        dve.tensor_scalar(w["A_log"][:, :], w["A_log"][:, :], -1.0, None, ALU.mult)
        dve.wait_ge(done["dt_product"], 1)
        v, e, t, l = dt_v, dt_e, dt_t, dt_l
        product = s.psum[:, 0, 0:TILES * HEADS].rearrange("p (t h) -> p t h", h=HEADS)
        dve.tensor_tensor(v[:, :, :], product, w["dt_bias"][:, :].unsqueeze(1).to_broadcast([P, TILES, HEADS]),
                          ALU.add).then_inc(done["dt_biased"], 1)
        dve.wait_ge(done["dt_exp"], 1)
        dve.drain()
        dve.tensor_scalar(t[:, :, :], e[:, :, :], 1.0, None, ALU.add).then_inc(done["dt_log_in"], 1)
        dve.drain()
        dve.tensor_scalar(step_dt[:, :, :], t[:, :, :], -1.0, None, ALU.add)
        dve.drain()
        dve.tensor_tensor(e[:, :, :], e[:, :, :], step_dt[:, :, :], ALU.subtract)
        dve.reciprocal(step_da[:, :, :], t[:, :, :])
        dve.drain()
        dve.tensor_tensor(e[:, :, :], e[:, :, :], step_da[:, :, :], ALU.mult)
        dve.tensor_scalar(v[:, :, :], v[:, :, :], 0.0, None, ALU.max)
        dve.drain()
        dve.tensor_tensor(v[:, :, :], v[:, :, :], e[:, :, :], ALU.add)
        dve.drain()
        dve.wait_ge(done["dt_log"], 1)
        dve.tensor_tensor(step_dt[:, :, :], v[:, :, :], l[:, :, :], ALU.add)
        dve.drain()
        dve.tensor_tensor(step_da[:, :, :], step_dt[:, :, :], w["A_log"][:, :].unsqueeze(1).to_broadcast([P, TILES, HEADS]),
                          ALU.mult).then_inc(done["dt_done"], 1)
        dve.wait_ge(done["sums_ready"], 1)
        dve.tensor_copy(cum[:, :, :].rearrange("p t h -> p (t h)"), s.psum[:, 1, 0:TILES * HEADS]).then_inc(done["sums_copied"], 1)

    dt_v, dt_e, dt_t, dt_l = (mixed[:, 0, n, :].rearrange("p (t h) -> p t h", h=HEADS) for n in range(4))

    def prep_scalar(act):
        act.wait_ge(dma["small"][0], dma["small"][1])
        act.activation(w["A_log"][:, :], w["A_log"][:, :], ACT.Exp).then_inc(done["decay_rate"], 1)
        act.wait_ge(done["dt_biased"], 1)
        act.activation(dt_e[:, :, :], dt_v[:, :, :], ACT.Abs)
        act.drain()
        act.activation(dt_e[:, :, :], dt_e[:, :, :], ACT.Exp, scale=-1.0).then_inc(done["dt_exp"], 1)
        act.wait_ge(done["dt_log_in"], 1)
        act.activation(dt_l[:, :, :], dt_t[:, :, :], ACT.Ln).then_inc(done["dt_log"], 1)

    def prep_tensor(pe):
        for t in range(TILES):
            for k in range(KD):
                last = three_passes(pe, s.psum[:, 0, t * HEADS:(t + 1) * HEADS],
                                    pair_at(s.act, slice(None), k, slice(t * P, (t + 1) * P)),
                                    pair_at(w["in"], slice(None), k, slice(IP * P, IP * P + HEADS)), k == 0, k == KD - 1)
        last.then_inc(done["dt_product"], 1)
        pe.wait_ge(done["dt_done"], 1)
        pe.matmul(s.psum[:, 1, 0:TILES * HEADS], s.upper[:, :], step_da[:, :, :].rearrange("p t h -> p (t h)"),
                  start=True, stop=True).then_inc(done["sums_ready"], 1)

    def tensor(pe):
        pe.wait_ge(*dma["in_split"])
        pe.wait_ge(*dma["normed"])
        prep_tensor(pe)
        pe.wait_ge(*dma["out_split"])
        pe.wait_ge(done["sums_copied"], 1)
        with pe.Fori(0, BATCH) as b:
            for e in events:
                kind, c, m = e
                n = CHUNKS * b + (c or 0)
                par = (c or 0) // TG % 2
                q = slice((c or 0) % TG * P, (c or 0) % TG * P + P)
                if kind in ("project", "C"):
                    old = before[e]
                    if old is None:
                        pe.wait_ge(done["out_done"], CHUNKS * b)
                        pe.wait_ge(done["gate_done"], PER["z"] * b)
                        pe.wait_ge(done["evacuated"], PER["conv"] * b)
                    elif old[0] == "C":
                        pe.wait_ge(done["out_done"], CHUNKS * b + old[1] + 1)
                    else:
                        what, at = order[old]
                        pe.wait_ge(done["evacuated"] if what == "conv" else done["gate_done"], PER[what] * b + at + 1)
                if kind == "project":
                    for k in range(KD):
                        last = three_passes(pe, bank(e), pair_at(w["in"], slice(None), k, slice(m * P, (m + 1) * P)),
                                            pair_at(s.act, slice(None), k, bass.ds(b * SEQ + c * GROUP, GROUP)),
                                            k == 0, k == KD - 1)
                    last.then_inc(done["projected"], 1)
                elif kind == "A":
                    pe.wait_ge(done["state_done"], n)
                    pe.wait_ge(done["conv_done"], PER["conv"] * b + XBC_BLOCKS * (par + 1))
                    pe.wait_ge(done["xdt"], n)
                    pe.wait_ge(done["b_copied"], n)
                    for k in range(2):
                        last = pe.transpose(s.psum[:, 4, k * P:(k + 1) * P], xbc[:, par, k, q], s.ident[:, :])
                    last.then_inc(done["turned"], 1)
                    pe.wait_ge(done["steps"], n + 1)
                    pe.wait_ge(done["seg"], n)
                    pe.wait_ge(done["row_exp"], n)
                    for k in range(2):
                        last = pe.matmul(s.psum[:, k, :], s.ones[:, :],
                                         steps[:, REP * k:REP * (k + 1), :].rearrange("p h q -> p (h q)"),
                                         start=True, stop=True)
                    last.then_inc(done["rows_ready"], 1)
                    pe.wait_ge(done["mixed"], n)
                    for g in range(2):
                        rows = slice(g * STATE, (g + 1) * STATE)
                        last = pe.matmul(s.psum[:, 2 + g, :].rearrange("p (r q) -> p r q", r=REP), xbc[rows, par, 1, q],
                                         xbc[rows, par, 2:XBC_BLOCKS, q], start=True, stop=True)
                    last.then_inc(done["scores_ready"], 1)
                elif kind == "B":
                    pe.wait_ge(done["mixed"], n + 1)
                    pe.wait_ge(done["c_scaled"], n + 1)
                    pe.wait_ge(done["state_done"], n + 1)
                    pe.wait_ge(done["gated"], n)
                    for m in range(Z_BLOCKS):
                        y = s.psum[:, 5, m * P:(m + 1) * P]
                        pe.matmul(y, d_head[:, m, :], xbc[:, par, 0, q], start=True, stop=False, skip_group_check=True)
                        for j in range(2):
                            h = 2 * m + j
                            g, r = h // REP, h % REP
                            part = s.psum[j * HEAD:(j + 1) * HEAD, 5, m * P:(m + 1) * P]
                            rows = slice(g * STATE, (g + 1) * STATE)
                            if m == 2 and j == 0:
                                pe.wait_ge(done["lower_done"], n + 1)
                            pe.matmul(part, xdt[:, c % 2, h, :], mixed[:, c % 2, h, :], start=False, stop=False,
                                      skip_group_check=True)
                            last = pe.matmul(part, state[rows, r, :], c_scaled[rows, c % 2, r, :], start=False, stop=True,
                                             skip_group_check=True)
                        if m == 1:
                            last.then_inc(done["lower_done"], 1)
                    last.then_inc(done["y_ready"], 1)
                    pe.wait_ge(done["xdt_decayed"], n + 1)
                    if c + 1 < CHUNKS:
                        pe.wait_ge(done["xdt"], n + 2)
                        pe.wait_ge(done["b_copied"], n + 2)
                    for g in range(2):
                        rows = slice(g * STATE, (g + 1) * STATE)
                        last = pe.matmul(s.psum[rows, 4, 256:512], b_tok[:, c % 2, rows],
                                         xdt_decayed[:, c % 2, REP * g:REP * (g + 1), :].rearrange("p h d -> p (h d)"),
                                         start=True, stop=True)
                    last.then_inc(done["state_ready"], 1)
                elif kind == "C":
                    pe.wait_ge(done["gated_lo"], n + 1)
                    for m in range(Z_BLOCKS):
                        three_passes(pe, bank(e)[:, 0:D], pair_at((gated_hi, gated_lo), slice(None), m),
                                     pair_at(w["out"], slice(None), m), m == 0, m == Z_BLOCKS - 1)
                    pe.wait_ge(done["squares"], n + 1)
                    for m in range(Z_BLOCKS):
                        last = pe.matmul(bank(e)[:, D:D + 1], squares[:, m, :], s.ones[:, 0:1], start=m == 0,
                                         stop=m == Z_BLOCKS - 1)
                    last.then_inc(done["out_ready"], 1)

    def scalar(act):
        prep_scalar(act)
        with act.Fori(0, BATCH) as b:
            for e in events:
                kind, c, m = e
                n = CHUNKS * b + (c or 0)
                if kind == "project":
                    what, at = order[e]
                    count = PER[what] * b + at
                    act.wait_ge(done["projected"], (PER["conv"] + PER["z"]) * b + IP * c + m + 1)
                    if what == "conv":
                        act.wait_ge(done["conv_sum"], PER["conv"] * b + max(0, at + 1 - XBC_BLOCKS))
                        act.activation(conv_in[:, m, TAPS - 1:], bank(e), ACT.Copy).then_inc(done["evacuated"], 1)
                        if at % XBC_BLOCKS >= 1:
                            conv_tanh(act, b, at - 1)
                        if at % XBC_BLOCKS == XBC_BLOCKS - 1:
                            conv_tanh(act, b, at)
                    else:
                        act.wait_ge(done["gate_done"], PER["z"] * b + max(0, at - 1))
                        act.activation(gate_th[:, at % 2, :], bank(e), ACT.Tanh, scale=0.5).then_inc(done["gate_tanh"], 1)
                elif kind == "A":
                    act.wait_ge(done["rows_ready"], n + 1)
                    act.wait_ge(done["seg"], n + 1)
                    for g in range(2):
                        rows = slice(g * STATE, (g + 1) * STATE)
                        last = act.activation(row_exp[rows, c % 2, :, :].rearrange("p r q -> p (r q)"), s.psum[rows, g, :],
                                              ACT.Exp)
                    last.then_inc(done["row_exp"], 1)
                    act.wait_ge(done["xdt"], n + 1)
                    act.activation(b_tok[:, c % 2, :], s.psum[:, 4, P:2 * P], ACT.Copy).then_inc(done["b_copied"], 1)
                    act.wait_ge(done["masked"], n + 1)
                    act.activation(decay[:, c % 2, :, :], decay[:, c % 2, :, :], ACT.Exp).then_inc(done["leaves"], 1)
                elif kind == "B":
                    act.wait_ge(done["gated"], n + 1)
                    act.wait_ge(done["out_ready"], n)
                    act.activation(gated_hi[:, :, :], gated[:, :, :], ACT.Copy).then_inc(done["gated_hi"], 1)
                    act.activation(squares[:, :, :], gated[:, :, :], ACT.Square).then_inc(done["squares"], 1)

    gate_th = sb("gate_th", [P, 2, GROUP])

    def conv_tanh(act, b, at):
        act.wait_ge(done["conv_sum"], PER["conv"] * b + at + 1)
        act.wait_ge(done["conv_done"], PER["conv"] * b + max(0, at - 1))
        act.activation(conv_th[:, at % 2, :], conv_sum[:, at % 2, :], ACT.Tanh).then_inc(done["conv_tanh"], 1)

    def vector(dve):
        prep_vector(dve)
        with dve.Fori(0, BATCH) as b:
            dve.memset(state[:, :, :], 0.0).then_inc(done["state_done"], 1)
            dve.memset(conv_in[:, :, 0:TAPS - 1], 0.0)
            dve.drain()
            for e in events:
                kind, c, m = e
                n = CHUNKS * b + (c or 0)
                par = (c or 0) // TG % 2
                q = slice((c or 0) % TG * P, (c or 0) % TG * P + P)
                tile = b * CHUNKS + (c or 0)
                dve.drain()
                if kind == "project":
                    what, at = order[e]
                    if what == "conv":
                        dve.wait_ge(done["evacuated"], PER["conv"] * b + at + 1)
                        acc = conv_sum[:, at % 2, :]
                        dve.tensor_scalar(acc, conv_in[:, m, 0:GROUP], w["conv_w"][:, m, 0:1], w["conv_b"][:, m:m + 1],
                                          ALU.mult, ALU.add)
                        for k in range(1, TAPS):
                            dve.drain()
                            last = dve.scalar_tensor_tensor(acc, conv_in[:, m, k:k + GROUP], w["conv_w"][:, m, k:k + 1], acc,
                                                            ALU.mult, ALU.add)
                        dve.drain()
                        dve.tensor_copy(conv_in[:, m, 0:TAPS - 1], conv_in[:, m, GROUP:GROUP + TAPS - 1]).then_inc(done["conv_sum"], 1)
                        if at % XBC_BLOCKS >= 1:
                            conv_end(dve, b, c, at - 1)
                        if at % XBC_BLOCKS == XBC_BLOCKS - 1:
                            conv_end(dve, b, c, at)
                    else:
                        dve.wait_ge(done["gate_tanh"], PER["z"] * b + at + 1)
                        dve.scalar_tensor_tensor(zs[:, c % 2, m - XBC_BLOCKS, :], gate_th[:, at % 2, :], 1.0, bank(e),
                                                 ALU.add, ALU.mult).then_inc(done["gate_done"], 1)
                elif kind == "A":
                    dve.wait_ge(done["rows_ready"], n + 1)
                    dve.tensor_tensor(decay[:, c % 2, :, :], s.psum[:, 0:2, :].rearrange("p k (r q) -> p (k r) q", r=REP),
                                      cum[:, tile, :].unsqueeze(2).to_broadcast([P, HEADS, P]),
                                      ALU.subtract).then_inc(done["seg"], 1)
                    dve.wait_ge(done["turned"], n + 1)
                    dve.tensor_tensor(xdt[:, c % 2, :, :].rearrange("p (g r) d -> p g r d", g=2),
                                      s.psum[:, 4, 0:P].rearrange("p (g d) -> p g d", g=2).unsqueeze(2).to_broadcast([P, 2, REP, HEAD]),
                                      step_dt[:, tile, :].rearrange("p (g r) -> p g r", g=2).unsqueeze(3).to_broadcast([P, 2, REP, HEAD]),
                                      ALU.mult).then_inc(done["xdt"], 1)
                elif kind == "A_end":
                    dve.wait_ge(done["leaves"], n + 1)
                    dve.wait_ge(done["scores_ready"], n + 1)
                    dve.tensor_tensor(mixed[:, c % 2, :, :], decay[:, c % 2, :, :],
                                      s.psum[:, 2:4, :].rearrange("p k (r q) -> p (k r) q", r=REP), ALU.mult).then_inc(done["mixed"], 1)
                elif kind == "B":
                    dve.wait_ge(done["y_ready"], n + 1)
                    if c < CHUNKS - 1:
                        dve.tensor_tensor(state[:, :, :], state[:, :, :],
                                          row_exp[:, c % 2, :, P - 1:P].to_broadcast([P, REP, HEAD]), ALU.mult)
                        dve.drain()
                        dve.wait_ge(done["state_ready"], n + 1)
                        dve.tensor_tensor(state[:, :, :], state[:, :, :],
                                          s.psum[:, 4, 256:512].rearrange("p (r d) -> p r d", r=REP),
                                          ALU.add).then_inc(done["state_done"], 1)
                    dve.wait_ge(done["gated_lo"], n)
                    dve.wait_ge(done["squares"], n)
                    dve.tensor_tensor(gated[:, :, :], zs[:, par, :, q],
                                      s.psum[:, 5, :].rearrange("p (m q) -> p m q", q=P), ALU.mult).then_inc(done["gated"], 1)
                elif kind == "C":
                    dve.wait_ge(done["out_ready"], n + 1)
                    dve.tensor_scalar(out_var[:, :], bank(e)[:, D:D + 1], 0.25 / INNER, EPS, ALU.mult,
                                      ALU.add).then_inc(done["out_var"], 1)
                    dve.wait_ge(done["out_root"], n + 1)
                    dve.scalar_tensor_tensor(u[:, tile, :], bank(e)[:, 0:D], out_root[:, 0:1], u[:, tile, :], ALU.mult,
                                             ALU.add).then_inc(done["out_done"], 1)

    def conv_end(dve, b, c, at):
        dve.wait_ge(done["conv_tanh"], PER["conv"] * b + at + 1)
        dve.scalar_tensor_tensor(xbc[:, c % 2, at % XBC_BLOCKS, :], conv_th[:, at % 2, :], 1.0, conv_sum[:, at % 2, :],
                                 ALU.add, ALU.mult).then_inc(done["conv_done"], 1)

    def gpsimd(pool):
        pool.wait_ge(done["dt_done"], 1)
        with pool.Fori(0, BATCH) as b:
            for c in range(-1, CHUNKS + 2):
                n = CHUNKS * b + c
                tile = b * CHUNKS + c
                if 0 <= c < CHUNKS:
                    par, q = c // TG, slice(c % TG * P, c % TG * P + P)
                    pool.wait_ge(done["seg"], n + 1)
                    pool.sem_inc(s.wait_over, 1)
                    pool.affine_select(out=decay[:, c % 2, :, :], in_=decay[:, c % 2, :, :], compare_op=ALU.is_ge,
                                       fill=MASKED, base=0, pattern=[[0, HEADS], [1, P]],
                                       channel_multiplier=-1).then_inc(done["masked"], 1)
                    pool.wait_ge(done["row_exp"], n + 1)
                    pool.tensor_tensor(c_scaled[:, c % 2, :, :], xbc[:, par, 2:XBC_BLOCKS, q], row_exp[:, c % 2, :, :],
                                       ALU.mult).then_inc(done["c_scaled"], 1)
                if c + 1 < CHUNKS:
                    pool.wait_ge(done["rows_ready"], n + 1)
                    pool.tensor_tensor(steps[:, :, :], s.upper[:, :].unsqueeze(1).to_broadcast([P, HEADS, P]),
                                       step_da[:, tile + 1, :].unsqueeze(2).to_broadcast([P, HEADS, P]),
                                       ALU.mult).then_inc(done["steps"], 1)
                if 0 <= c < CHUNKS:
                    pool.wait_ge(done["leaves"], n + 1)
                    pool.wait_ge(done["xdt"], n + 1)
                    pool.tensor_tensor(xdt_decayed[:, c % 2, :, :], xdt[:, c % 2, :, :],
                                       decay[:, c % 2, :, P - 1:P].to_broadcast([P, HEADS, HEAD]),
                                       ALU.mult).then_inc(done["xdt_decayed"], 1)
                if 1 <= c <= CHUNKS:
                    pool.wait_ge(done["gated_hi"], n)
                    pool.tensor_tensor(gated_lo[:, :, :], gated[:, :, :], gated_hi[:, :, :].bitcast(F32),
                                       ALU.subtract).then_inc(done["gated_lo"], 1)
                if c >= 2:
                    pool.wait_ge(done["out_var"], n - 1)
                    pool.tensor_tensor(out_root[:, :], out_var[:, :], s.minus_half[:, 0:1], ALU.pow).then_inc(done["out_root"], 1)

    return dict(vector=vector, scalar=scalar, gpsimd=gpsimd, tensor=tensor, done=(done["out_done"], TILES), prep=(done["prep"], 1))


class Counts:

    def __init__(self):
        self.base, self.per, self.i = {}, {}, None

    def at(self, kind, n):
        value = self.base.get(kind, 0) + n
        return value if self.i is None else self.i * self.per.get(kind, 0) + value

    def passed(self, counts, turns=1):
        for kind, n in counts.items():
            self.base[kind] = self.base.get(kind, 0) + n * turns


def attention_stage(nc, sems, mem, s, a, before, normed):

    def sem(what):
        return sems.enter_context(nc.semaphore(f"attn_{what}"))

    def sb(what, shape, dt=F32):
        return mem.enter_context(nc.sbuf_tensor(f"attn_{what}", shape, dt))

    def pair(what, shape):
        return sb(f"{what}_hi", shape, F32R), sb(f"{what}_lo", shape, F32R)

    q, k, v = pair("q", [P, 2, SEQ]), pair("k", [P, 2, SEQ]), pair("v", [P, QT, 2 * AE])
    z, pt = pair("z", [P, 2, SEQ]), pair("pt", [P, 3, GROUP])
    probs = [[sb(f"probs_{h}_{g}", [P, TG, (g + 1) * GROUP]) for g in range(2)] for h in range(2)]
    qkv_raw, wo_raw = sb("qkv_raw", [P, 3, KD, 2, AE]), sb("wo_raw", [P, 2, D])
    qkv, wo = pair("qkv", [P, 3, KD, 2, AE]), pair("wo", [P, 2, D])
    bias = sb("bias", [P, 3, AH])
    b_out = sb("b_out", [P, D])
    ident_b, mask = sb("ident_b", [P, P], BF16), sb("mask", [P, P], BF16)
    neg_max, sums, inverse = (sb(n, [P, 2 * QT]) for n in ("neg_max", "sums", "inverse"))

    small_loaded, qkv_loaded, wo_loaded, masks_ready = (
        sem(n) for n in ("small_loaded", "qkv_loaded", "wo_loaded", "masks_ready"))
    w_hi, w_split = sem("w_hi"), sem("w_split")
    work_ready, work_hi, work_done = sem("work_ready"), sem("work_hi"), sem("work_done")
    scores_ready, max_ready, max_taken, exp_done, inverse_ready, probs_ready = (
        sem(n) for n in ("scores_ready", "max_ready", "max_taken", "exp_done", "inverse_ready", "probs_ready"))
    summed = sem("summed")
    z_hi, z_done = sem("z_hi"), sem("z_done")
    Q, K, V = range(3)
    HALF = SEQ // GROUP
    QKV_LOADS = 3 * KD

    def section(kind):
        events, n = [], dict(work=0, hi=0, tile=0, pt=0, z=0, w=0, qkv=0, wo=0)

        def add(what, counted, **at):
            e = dict(what=what, **at)
            for c in counted:
                e[c] = n[c]
                n[c] += 1
            events.append(e)
            return e

        def project(h):
            return [lambda m=m, half=half: add("project", ("work", "hi"), m=m, h=h, half=half)
                    for m in (Q, K) for half in range(HALF)]

        def values():
            for t in range(QT // 2):
                add("values", ("work", "hi"), t=t)

        def score(h, t, need):
            return add("score", ("tile",), h=h, t=t, need=need)

        if kind == "first":
            n["qkv"] += 1
            for m in (Q, K, V):
                add("split", ("w",), m=m)
            for h in range(2):
                for p in project(h):
                    p()
            need = n["work"]
            values()
            late = None
            for t in range(QT):
                e = score(0, t, need)
                events.append(dict(e, what="exp"))
                if late:
                    events.append(dict(late, what="invert"))
                late = e
            events.append(dict(late, what="invert"))
        else:
            last = kind == "last"
            n["qkv"], n["wo"] = (0 if last else 1), 1
            chunks = [(h, g, j) for h in range(2) for g in range(2) for j in range(TG * (g + 1))]
            half = len(chunks) // 2
            score_at = {0: 0, 2: 1, 3: 2, 5: 3, 6: 4, 8: 5, 9: 6, 11: 7}
            project_at = (3, 5, 8, 10)
            splits = {1: 3} if last else {0: Q, 1: K, 2: V, 3: 3}
            turned, late, need = [], None, 0

            def turn(c):
                h, g, j = chunks[c]
                turned.append(add("turn", ("work", "hi", "pt"), h=h, g=g, j=j))

            turn(0)
            turn(1)
            for c, (h, g, j) in enumerate(chunks):
                if late:
                    events.append(dict(late, what="invert"))
                    late = None
                e = None
                if c % half in score_at and not (last and h == 1):
                    e = score(1 - h, score_at[c % half], need)
                if c in splits:
                    add("split", ("w",), m=splits[c])
                if c + 2 < len(chunks):
                    turn(c + 2)
                events.append(dict(turned[c], what="sum"))
                if j == TG * (g + 1) - 1:
                    add("gather", ("z",), h=h, g=g)
                if e:
                    events.append(dict(e, what="exp"))
                    late = e
                if c % half in project_at and not last:
                    project(h)[project_at.index(c % half)]()
                    if c == half - 1:
                        need = n["work"]
            if late:
                events.append(dict(late, what="invert"))
            if not last:
                values()
            for t in range(QT // 2):
                add("output", ("work",), t=t)
        return events, n

    sections = {kind: section(kind) for kind in ("first", "body", "last")}

    def sections_of(engine, handle):
        counts = Counts()
        for b in range(BATCH):
            for kind in ("first", "body", "last"):
                events, n = sections[kind]
                if kind == "body":
                    with engine.Fori(0, PAIRS - 1) as i:
                        counts.i, counts.per = i, n
                        for e in events:
                            handle(e, counts, b, kind, i)
                    counts.i = None
                    counts.passed(n, PAIRS - 1)
                else:
                    for e in events:
                        handle(e, counts, b, kind, 0 if kind == "first" else PAIRS - 1)
                    counts.passed(n)

    def work_bank(e):
        return 4 + e["work"] % 3

    def first_column(e):
        return max(0, e["j"] - TG * e["g"]) * P

    def score_view(e):
        width = (e["t"] + 1) * P
        slot = 2 * (e["t"] % 2)
        return s.psum[:, slot:slot + 2, :].rearrange("p b c -> p (b c)")[:, 0:width]

    def probs_view(e):
        return probs[e["h"]][e["t"] // TG][:, e["t"] % TG, 0:(e["t"] + 1) * P]

    def stat(tensor, e):
        at = e["h"] * QT + e["t"]
        return tensor[:, at:at + 1]

    def bias_of(e, i, kind):
        if e["what"] == "gather":
            return bias[:, V, bass.ds(i * 2 + e["h"], 1)]
        return bias[:, e["m"], bass.ds(i * 2 + e["h"] + (0 if kind == "first" else 2), 1)]

    def raw_and_split(m):
        if m == 3:
            return wo_raw[:, :, :], wo[0][:, :, :], wo[1][:, :, :]
        return (t[:, m, :, :, :].rearrange("p k h e -> p (k h e)") for t in (qkv_raw, *qkv))

    def destination(e):
        if e["what"] == "project":
            return pair_at((q, k)[e["m"]], slice(None), e["h"], slice(e["half"] * GROUP, (e["half"] + 1) * GROUP))
        if e["what"] == "values":
            return tuple(t[:, 2 * e["t"]:2 * e["t"] + 2, :].rearrange("p t c -> p (t c)") for t in v)
        return pair_at(pt, slice(None), e["pt"] % 3, slice(first_column(e), GROUP))

    def work_view(e):
        return s.psum[:, work_bank(e), (first_column(e) if e["what"] == "turn" else 0):]

    def sync(sp):
        sp.wait_ge(*before)
        with nc.allow_non_contiguous_dma(reason="biases, one element for each partition"):
            for n, name in enumerate("QKV"):
                sp.dma_start(bias[:, n, :], a[f"L1_attn_b_{name}"].rearrange("h e -> e h")).then_inc(small_loaded, 16)
        sp.dma_start(b_out[:, :], a["L1_attn_b_O"].partition_broadcast(P)).then_inc(small_loaded, 16)
        counts = Counts()

        def load_qkv(at):
            sp.wait_ge(w_split, counts.at("w", 0))
            for m, name in enumerate("QKV"):
                for c in range(KD):
                    sp.dma_start(qkv_raw[:, m, c, :, :],
                                 a[f"L1_attn_W_{name}"][bass.ds(at * 2, 2), c * P:(c + 1) * P, :].rearrange("h p e -> p h e")
                                 ).then_inc(qkv_loaded, 16)

        def load_wo(at):
            sp.wait_ge(w_split, counts.at("w", 0))
            sp.dma_start(wo_raw[:, :, :], a["L1_attn_W_O"][bass.ds(at * 2, 2), :, :].rearrange("h e d -> e h d")
                         ).then_inc(wo_loaded, 16)

        for b in range(BATCH):
            load_qkv(0)
            counts.passed(sections["first"][1])
            with sp.Fori(0, PAIRS - 1) as i:
                counts.i, counts.per = i, sections["body"][1]
                load_qkv(i + 1)
                load_wo(i)
            counts.i = None
            counts.passed(sections["body"][1], PAIRS - 1)
            load_wo(PAIRS - 1)
            counts.passed(sections["last"][1])

    def tensor(pe):
        pe.wait_ge(*before)
        pe.wait_ge(*normed)
        pe.wait_ge(masks_ready, 4)
        pe.sem_inc(summed, 2)

        def handle(e, counts, b, kind, i):
            what = e["what"]
            if what in ("project", "values", "turn", "output"):
                pe.wait_ge(work_done, counts.at("work", max(0, e["work"] - 2)))
            if what in ("project", "values"):
                pe.wait_ge(w_split, counts.at("w", (V if what == "values" else e["m"]) + 1))
            if what == "project":
                tokens = slice(b * SEQ + e["half"] * GROUP, b * SEQ + (e["half"] + 1) * GROUP)
                for c in range(KD):
                    last = three_passes(pe, s.psum[:, work_bank(e), :], pair_at(qkv, slice(None), e["m"], c, e["h"]),
                                        pair_at(s.act, slice(None), c, tokens), c == 0, c == KD - 1)
                last.then_inc(work_ready, 1)
            elif what == "values":
                for t in range(2):
                    tokens = slice(b * SEQ + (2 * e["t"] + t) * P, b * SEQ + (2 * e["t"] + t + 1) * P)
                    for c in range(KD):
                        w_hi_lo = tuple(x[:, V, c, :, :].rearrange("p h e -> p (h e)") for x in qkv)
                        last = three_passes(pe, s.psum[:, work_bank(e), t * 2 * AE:(t + 1) * 2 * AE],
                                            pair_at(s.act, slice(None), c, tokens), w_hi_lo, c == 0, c == KD - 1)
                last.then_inc(work_ready, 1)
            elif what == "score":
                pe.wait_ge(work_done, counts.at("work", e["need"]))
                ahead = max(0, e["tile"] - 1) if kind == "first" else e["tile"] - 1
                pe.wait_ge(exp_done, counts.at("tile", ahead))
                t, view = e["t"], score_view(e)
                queries = pair_at(q, slice(None), e["h"], slice(t * P, (t + 1) * P))
                for at in range(0, (t + 1) * P, GROUP):
                    end = min(at + GROUP, (t + 1) * P)
                    (q_hi, q_lo), (k_hi, k_lo) = queries, pair_at(k, slice(None), e["h"], slice(at, end))
                    pe.matmul(view[:, at:end], q_hi, k_hi, start=True, stop=False)
                    if end == (t + 1) * P:
                        pe.matmul(view[:, t * P:], ident_b[:, :], mask[:, :], start=False, stop=False)
                    pe.matmul(view[:, at:end], q_hi, k_lo, start=False, stop=False)
                    last = pe.matmul(view[:, at:end], q_lo, k_hi, start=False, stop=True)
                last.then_inc(scores_ready, 1)
            elif what == "turn":
                tile = TG * (e["g"] + 1)
                ready = counts.at("tile", tile - QT) if e["h"] == 0 else counts.at("tile", tile)
                pe.wait_ge(probs_ready, ready)
                for lq in range(first_column(e) // P, TG):
                    last = pe.transpose(s.psum[:, work_bank(e), lq * P:(lq + 1) * P],
                                        probs[e["h"]][e["g"]][:, lq, e["j"] * P:(e["j"] + 1) * P], s.ident[:, :])
                last.then_inc(work_ready, 1)
            elif what == "sum":
                pe.wait_ge(work_done, counts.at("work", e["work"] + 1))
                j = e["j"]
                if j == 0:
                    pe.wait_ge(z_done, counts.at("z", 2 * e["h"] + e["g"]))
                at = first_column(e)
                v_hi, v_lo = pair_at(v, slice(None), j, slice(e["h"] * AE, (e["h"] + 1) * AE))
                p_hi, p_lo = pair_at(pt, slice(None), e["pt"] % 3)
                pe.matmul(s.psum[:, 7, at:], v_hi, p_hi[:, at:], start=j == 0, stop=False, skip_group_check=True)
                pe.matmul(s.psum[:, 7, at:], v_hi, p_lo[:, at:], start=False, stop=False, skip_group_check=True)
                ends = at + P if j >= TG * e["g"] else at
                if ends > at:
                    last = pe.matmul(s.psum[:, 7, at:ends], v_lo, p_hi[:, at:ends], start=False, stop=True,
                                     skip_group_check=True)
                if ends < GROUP:
                    last = pe.matmul(s.psum[:, 7, ends:], v_lo, p_hi[:, ends:], start=False, stop=False, skip_group_check=True)
                last.then_inc(summed, 1)
            elif what == "output":
                pe.wait_ge(z_done, counts.at("z", 4))
                pe.wait_ge(w_split, counts.at("w", 1 if kind == "last" else 4))
                for t in range(2):
                    tokens = slice((2 * e["t"] + t) * P, (2 * e["t"] + t + 1) * P)
                    for h in range(2):
                        last = three_passes(pe, s.psum[:, work_bank(e), t * D:(t + 1) * D],
                                            pair_at(z, slice(None), h, tokens), pair_at(wo, slice(None), h), h == 0, h == 1)
                last.then_inc(work_ready, 1)

        sections_of(pe, handle)

    def scalar(act):
        act.wait_ge(*before)
        act.wait_ge(small_loaded, 64)

        def handle(e, counts, b, kind, i):
            what = e["what"]
            if what == "split":
                raw, hi, _ = raw_and_split(e["m"])
                if e["m"] == 3:
                    act.wait_ge(wo_loaded, 16 * (counts.at("wo", 1)))
                else:
                    act.wait_ge(qkv_loaded, 16 * QKV_LOADS * (counts.at("qkv", 1)))
                act.wait_ge(work_ready, counts.at("work", 0))
                act.activation(hi, raw, ACT.Copy).then_inc(w_hi, 1)
            elif what in ("project", "values", "turn"):
                act.wait_ge(work_ready, counts.at("work", e["work"] + 1))
                if what == "turn":
                    act.wait_ge(summed, counts.at("pt", e["pt"]))
                if what == "project":
                    act.sem_inc(s.wait_over, 1)
                    act.activation(destination(e)[0], work_view(e), ACT.Identity, bias=bias_of(e, i, kind)).then_inc(work_hi, 1)
                else:
                    act.activation(destination(e)[0], work_view(e), ACT.Copy).then_inc(work_hi, 1)
            elif what == "exp":
                act.wait_ge(max_ready, counts.at("tile", e["tile"] + 1))
                act.activation(probs_view(e), score_view(e), ACT.Exp, bias=stat(neg_max, e), scale=SCORE_SCALE,
                               accum_out=stat(sums, e)).then_inc(exp_done, 1)
            elif what == "gather":
                act.wait_ge(summed, 2 + counts.at("pt", group_end(e)))
                act.sem_inc(s.wait_over, 1)
                act.activation(z[0][:, e["h"], e["g"] * GROUP:(e["g"] + 1) * GROUP], s.psum[:, 7, :], ACT.Identity,
                               bias=bias_of(e, i, kind)).then_inc(z_hi, 1)

        sections_of(act, handle)

    def group_end(e):
        return e["h"] * 3 * TG + (TG if e["g"] == 0 else 3 * TG)

    def vector(dve):
        dve.wait_ge(*before)
        dve.wait_ge(small_loaded, 64)
        dve.drain()
        dve.tensor_tensor(s.x[:, :, :], s.x[:, :, :], b_out[:, :].unsqueeze(1).to_broadcast([P, TILES, D]), ALU.add)
        dve.drain()

        def handle(e, counts, b, kind, i):
            what = e["what"]
            if what in ("project", "values", "turn"):
                dve.wait_ge(work_hi, counts.at("hi", e["hi"] + 1))
                hi, lo = destination(e)
                if what == "project":
                    dve.scalar_tensor_tensor(lo, work_view(e), bias_of(e, i, kind), hi.bitcast(F32), ALU.add,
                                             ALU.subtract).then_inc(work_done, 1)
                else:
                    dve.tensor_tensor(lo, work_view(e), hi.bitcast(F32), ALU.subtract).then_inc(work_done, 1)
            elif what == "score":
                dve.wait_ge(scores_ready, counts.at("tile", e["tile"] + 1))
                dve.tensor_reduce(stat(neg_max, e), score_view(e), AX_X, ALU.max, negate=True)
                dve.drain()
                dve.tensor_scalar(stat(neg_max, e), stat(neg_max, e), SCORE_SCALE, None, ALU.mult).then_inc(max_ready, 1)
            elif what == "invert":
                dve.wait_ge(exp_done, counts.at("tile", e["tile"] + 1))
                dve.reciprocal(stat(inverse, e), stat(sums, e)).then_inc(inverse_ready, 1)
            elif what == "gather":
                dve.wait_ge(z_hi, counts.at("z", e["z"] + 1))
                hi, lo = pair_at(z, slice(None), e["h"], slice(e["g"] * GROUP, (e["g"] + 1) * GROUP))
                dve.scalar_tensor_tensor(lo, s.psum[:, 7, :], bias_of(e, i, kind), hi.bitcast(F32), ALU.add,
                                         ALU.subtract).then_inc(z_done, 1)
            elif what == "output":
                dve.wait_ge(work_ready, counts.at("work", e["work"] + 1))
                x = s.x[:, b * QT + 2 * e["t"]:b * QT + 2 * e["t"] + 2, :].rearrange("p t d -> p (t d)")
                dve.tensor_tensor(x, x, s.psum[:, work_bank(e), :], ALU.add).then_inc(work_done, 1)

        sections_of(dve, handle)

    def gpsimd(pool):
        pool.wait_ge(*before)
        pool.memset(ident_b[:, :], 0.0).then_inc(masks_ready, 1)
        pool.memset(mask[:, :], 0.0).then_inc(masks_ready, 1)
        pool.wait_ge(masks_ready, 2)
        pool.affine_select(out=ident_b[:, :], in_=ident_b[:, :], compare_op=ALU.not_equal, fill=1.0, base=0,
                           pattern=[[-1, P]], channel_multiplier=1).then_inc(masks_ready, 1)
        pool.affine_select(out=mask[:, :], in_=mask[:, :], compare_op=ALU.is_ge, fill=MASKED, base=0,
                           pattern=[[-1, P]], channel_multiplier=1).then_inc(masks_ready, 1)

        def handle(e, counts, b, kind, i):
            if e["what"] == "split":
                raw, hi, lo = raw_and_split(e["m"])
                pool.wait_ge(w_hi, counts.at("w", e["w"] + 1))
                pool.tensor_tensor(lo, raw, hi.bitcast(F32), ALU.subtract).then_inc(w_split, 1)
            elif e["what"] == "invert":
                pool.wait_ge(inverse_ready, counts.at("tile", e["tile"] + 1))
                pool.sem_inc(s.wait_over, 1)
                pool.tensor_scalar(probs_view(e), probs_view(e), stat(inverse, e), 1.0, ALU.mult,
                                   ALU.mult).then_inc(probs_ready, 1)

        sections_of(pool, handle)

    n = sections
    total = BATCH * (n["first"][1]["work"] + (PAIRS - 1) * n["body"][1]["work"] + n["last"][1]["work"])
    return dict(sync=sync, tensor=tensor, scalar=scalar, vector=vector, gpsimd=gpsimd, done=(work_done, total))


def moe_stage(nc, sems, mem, s, a, before, normed):

    def sem(what):
        return sems.enter_context(nc.semaphore(f"moe_{what}"))

    def sb(what, shape, dt=F32):
        return mem.enter_context(nc.sbuf_tensor(f"moe_{what}", shape, dt))

    def pair(what, shape):
        return sb(f"{what}_hi", shape, F32R), sb(f"{what}_lo", shape, F32R)

    BLOCKS = EI // P
    SIDES = 2
    router_raw, router = sb("router_raw", [P, KD, EXPERTS]), pair("router", [P, KD, EXPERTS])
    router_b, down_b = sb("router_b", [P, EXPERTS]), sb("down_b", [EXPERTS, D])
    gu_b, up_b = sb("gu_b", [P, EXPERTS, BLOCKS, SIDES]), sb("up_b", [P, EXPERTS, BLOCKS])
    logits, work, first, second = (sb(n, [P, TILES, EXPERTS]) for n in ("logits", "work", "first", "second"))
    scan = [sb(f"scan_{n}", [P, TILES, EXPERTS]) for n in range(2)]
    best = [sb(f"best_{n}", [P, TILES]) for n in range(2)]
    ratio, share = sb("ratio", [P, TILES]), sb("share", [P, TILES])
    scores = sb("scores", [P, TILES, EXPERTS])
    scores_t = sb("scores_t", [EXPERTS, TILES, P])
    gu_raw, down_raw = sb("gu_raw", [P, 2, KD, SIDES * EI]), sb("down_raw", [P, 2, BLOCKS, D])
    gu, down = pair("gu", [P, 2, KD, SIDES, EI]), pair("down", [P, 2, BLOCKS, D])
    gate, up, th, glu, hidden = (sb(n, [P, 2, GROUP]) for n in ("gate", "up", "th", "glu", "hidden"))
    hid = pair("hid", [P, 2, BLOCKS, GROUP])

    small_loaded, logits_ready, ratio_in, ratio_ready, scores_ready = (
        sem(n) for n in ("small_loaded", "logits_ready", "ratio_in", "ratio_ready", "scores_ready"))
    router_hi, router_split, turned, copied, bias_ready, bias_added = (
        sem(n) for n in ("router_hi", "router_split", "turned", "copied", "bias_ready", "bias_added"))
    raw_loaded = [sem(f"raw_loaded_{n}") for n in range(2)]
    w_scaled, w_hi, w_split = sem("w_scaled"), sem("w_hi"), sem("w_split")
    products, gate_ready, bounded, th_ready, hidden_done, hid_hi, hid_split, down_ready, added = (
        sem(n) for n in ("products", "gate_ready", "bounded", "th_ready", "hidden_done", "hid_hi", "hid_split",
                         "down_ready", "added"))
    PIECES = KD + 1
    UNITS = 2 * GROUPS
    SMALL = 3 + KD + BLOCKS * EXPERTS

    def sync(sp):
        sp.wait_ge(*before)
        with nc.allow_non_contiguous_dma(reason="router weights and biases by partition"):
            for c in range(KD):
                sp.dma_start(router_raw[:, c, :], a["L1_ffn_router_weight"][:, c * P:(c + 1) * P].rearrange("e p -> p e")
                             ).then_inc(small_loaded, 16)
            for e in range(EXPERTS):
                for m in range(BLOCKS):
                    sp.dma_start(gu_b[:, e, m, :],
                                 a["L1_ffn_gate_up_proj_bias"][e, m * P * SIDES:(m + 1) * P * SIDES].rearrange("(p s) -> p s", s=SIDES)
                                 ).then_inc(small_loaded, 16)
        sp.dma_start(router_b[:, :], a["L1_ffn_router_bias"].partition_broadcast(P)).then_inc(small_loaded, 16)
        sp.dma_start(down_b[:, :], a["L1_ffn_down_proj_bias"]).then_inc(small_loaded, 16)

        def load(slot, expert):
            sp.dma_start(gu_raw[:, slot, :, :], a["L1_ffn_gate_up_proj"][bass.ds(expert, 1), :, :].rearrange(
                "e (k p) n -> p (e k) n", p=P)).then_inc(raw_loaded[slot], 16)
            sp.dma_start(down_raw[:, slot, :, :], a["L1_ffn_down_proj"][bass.ds(expert, 1), :, :].rearrange(
                "e (k p) n -> p (e k) n", p=P)).then_inc(raw_loaded[slot], 16)

        load(0, 0)
        load(1, 1)
        with sp.Fori(0, EXPERTS // 2 - 1) as i:
            sp.wait_ge(w_split, PIECES * (2 * i + 1))
            load(0, 2 * i + 2)
            sp.wait_ge(w_split, PIECES * (2 * i + 2))
            load(1, 2 * i + 3)

    def tensor(pe):
        pe.wait_ge(*normed)
        pe.wait_ge(router_split, 1)
        for t in range(TILES):
            for c in range(KD):
                last = three_passes(pe, s.psum[:, 2, t * EXPERTS:(t + 1) * EXPERTS],
                                    pair_at(s.act, slice(None), c, slice(t * P, (t + 1) * P)), pair_at(router, slice(None), c),
                                    c == 0, c == KD - 1)
        last.then_inc(logits_ready, 1)
        pe.wait_ge(scores_ready, 1)
        for t in range(0, TILES, 4):
            if t:
                pe.wait_ge(copied, t // 4)
            for n in range(4):
                last = pe.transpose(s.psum[0:EXPERTS, 3, n * P:(n + 1) * P], scores[:, t + n, :], s.ident[:, :])
            last.then_inc(turned, 1)
        pe.wait_ge(copied, TILES // 4)
        for t in range(0, TILES, 2):
            if t >= 4:
                pe.wait_ge(bias_added, t // 2 - 1)
            for n in range(2):
                last = pe.matmul(s.psum[:, 4 + t // 2 % 2, n * D:(n + 1) * D], scores_t[:, t + n, :], down_b[:, :],
                                 start=True, stop=True)
            last.then_inc(bias_ready, 1)
        pe.wait_ge(bias_added, TILES // 2)
        pe.sem_inc(hidden_done, 2)

        def turn(counts):
            def gate_up(u):
                slot, g = u // GROUPS, u % GROUPS
                if g == 0:
                    pe.wait_ge(w_split, counts.at("w", PIECES * (slot + 1)))
                for m in range(BLOCKS):
                    n = u * BLOCKS + m
                    pe.wait_ge(bounded, counts.at("block", n + 1))
                    for side in range(SIDES):
                        for c in range(KD):
                            last = three_passes(pe, s.psum[:, 2 * (n % 2) + side, :],
                                                pair_at(gu, slice(None), slot, c, side, slice(m * P, (m + 1) * P)),
                                                pair_at(s.act, slice(None), c, slice(g * GROUP, (g + 1) * GROUP)),
                                                c == 0, c == KD - 1)
                    last.then_inc(products, 1)

            gate_up(0)
            for u in range(UNITS):
                if u + 1 < UNITS:
                    gate_up(u + 1)
                pe.wait_ge(hid_split, counts.at("block", BLOCKS * (u + 1)))
                pe.wait_ge(added, counts.at("unit", max(0, u - 1)))
                for t in range(TG):
                    for m in range(BLOCKS):
                        last = three_passes(pe, s.psum[:, 4 + 2 * (u % 2) + t // 2, t % 2 * D:(t % 2 + 1) * D],
                                            pair_at(hid, slice(None), u % 2, m, slice(t * P, (t + 1) * P)),
                                            pair_at(down, slice(None), u // GROUPS, m), m == 0, m == BLOCKS - 1)
                last.then_inc(down_ready, 1)

        turns(pe, turn)

    def turns(engine, turn):
        counts = Counts()
        per = dict(w=2 * PIECES, block=UNITS * BLOCKS, unit=UNITS)
        with engine.Fori(0, EXPERTS // 2) as i:
            counts.i, counts.per = i, per
            turn(counts)

    def scalar(act):
        act.wait_ge(small_loaded, 16 * (KD + 2 + BLOCKS * EXPERTS))
        act.activation(router[0][:, :, :], router_raw[:, :, :], ACT.Copy).then_inc(router_hi, 1)
        act.wait_ge(ratio_in, 1)
        act.activation(ratio[:, :], ratio[:, :], ACT.Exp).then_inc(ratio_ready, 1)
        for t in range(TILES // 4):
            act.wait_ge(turned, t + 1)
            act.activation(scores_t[:, 4 * t:4 * t + 4, :].rearrange("e t q -> e (t q)"), s.psum[0:EXPERTS, 3, :],
                           ACT.Copy).then_inc(copied, 1)

        def split(counts, slot, n, units):
            act.wait_ge(raw_loaded[slot], 32 * (counts.i + 1))
            act.wait_ge(down_ready, counts.at("unit", units))
            for c in range(KD):
                act.activation(gu[0][:, slot, c, :, :], gu_raw[:, slot, c, :].rearrange("p (n s) -> p s n", s=SIDES),
                               ACT.Copy).then_inc(w_hi, 1)
            act.activation(down_raw[:, slot, :, :], down_raw[:, slot, :, :], ACT.Copy, scale=0.5).then_inc(w_scaled, 1)
            act.drain()
            act.activation(down[0][:, slot, :, :], down_raw[:, slot, :, :], ACT.Copy).then_inc(w_hi, 1)

        def turn(counts):
            split(counts, 0, 0, 0)
            for n in range(UNITS * BLOCKS):
                act.wait_ge(gate_ready, counts.at("block", n + 1))
                act.activation(th[:, n % 2, :], gate[:, n % 2, :], ACT.Tanh, scale=ALPHA / 2).then_inc(th_ready, 1)
                if n == 2:
                    split(counts, 1, 1, 0)
                if n >= 1:
                    hi(counts, n - 1)
            hi(counts, UNITS * BLOCKS - 1)

        def hi(counts, n):
            u = n // BLOCKS
            act.wait_ge(hidden_done, counts.at("block", n + 1 + 2))
            act.wait_ge(down_ready, counts.at("unit", max(0, u - 1)))
            act.activation(hid[0][:, u % 2, n % BLOCKS, :], hidden[:, n % 2, :], ACT.Copy).then_inc(hid_hi, 1)

        turns(act, turn)

    def gpsimd(pool):
        pool.wait_ge(router_hi, 1)
        pool.tensor_tensor(router[1][:, :, :], router_raw[:, :, :], router[0][:, :, :].bitcast(F32),
                           ALU.subtract).then_inc(router_split, 1)

        def split(counts, slot):
            for c in range(KD):
                pool.wait_ge(w_hi, counts.at("w", PIECES * slot + c + 1))
                pool.tensor_tensor(gu[1][:, slot, c, :, :], gu_raw[:, slot, c, :].rearrange("p (n s) -> p s n", s=SIDES),
                                   gu[0][:, slot, c, :, :].bitcast(F32), ALU.subtract).then_inc(w_split, 1)
            pool.wait_ge(w_hi, counts.at("w", PIECES * (slot + 1)))
            pool.tensor_tensor(down[1][:, slot, :, :], down_raw[:, slot, :, :], down[0][:, slot, :, :].bitcast(F32),
                               ALU.subtract).then_inc(w_split, 1)

        def turn(counts):
            split(counts, 0)
            for n in range(UNITS * BLOCKS):
                if n == 2:
                    split(counts, 1)
                pool.wait_ge(hid_hi, counts.at("block", n + 1))
                pool.tensor_tensor(hid[1][:, n // BLOCKS % 2, n % BLOCKS, :], hidden[:, n % 2, :],
                                   hid[0][:, n // BLOCKS % 2, n % BLOCKS, :].bitcast(F32), ALU.subtract).then_inc(hid_split, 1)

        turns(pool, turn)

    def first_of(dve, values, top, out):
        dve.tensor_reduce(top[:, :], values[:, :, :], AX_X, ALU.max)
        dve.drain()
        dve.tensor_tensor(scan[0][:, :, :], values[:, :, :], top[:, :].unsqueeze(2).to_broadcast([P, TILES, EXPERTS]),
                          ALU.is_equal)
        dve.drain()
        at, shift = 0, 1
        while shift < EXPERTS:
            old, new = scan[at], scan[1 - at]
            dve.tensor_copy(new[:, :, 0:shift], old[:, :, 0:shift])
            dve.tensor_tensor(new[:, :, shift:], old[:, :, shift:], old[:, :, 0:EXPERTS - shift], ALU.max)
            dve.drain()
            at, shift = 1 - at, 2 * shift
        dve.tensor_copy(out[:, :, 0:1], scan[at][:, :, 0:1])
        dve.tensor_tensor(out[:, :, 1:], scan[at][:, :, 1:], scan[at][:, :, 0:EXPERTS - 1], ALU.subtract)
        dve.drain()

    def vector(dve):
        dve.wait_ge(small_loaded, 16 * (KD + 2 + BLOCKS * EXPERTS))
        dve.tensor_scalar(up_b[:, :, :], gu_b[:, :, :, 1], 1.0, None, ALU.add)
        dve.wait_ge(logits_ready, 1)
        everywhere = [P, TILES, EXPERTS]
        dve.tensor_tensor(logits[:, :, :], s.psum[:, 2, 0:TILES * EXPERTS].rearrange("p (t e) -> p t e", e=EXPERTS),
                          router_b[:, :].unsqueeze(1).to_broadcast(everywhere), ALU.add)
        dve.drain()
        first_of(dve, logits, best[0], first)
        dve.scalar_tensor_tensor(work[:, :, :], first[:, :, :], MASKED, logits[:, :, :], ALU.mult, ALU.add)
        dve.drain()
        first_of(dve, work, best[1], second)
        dve.tensor_tensor(ratio[:, :], best[1][:, :], best[0][:, :], ALU.subtract).then_inc(ratio_in, 1)
        dve.wait_ge(ratio_ready, 1)
        dve.tensor_scalar(share[:, :], ratio[:, :], 1.0, None, ALU.add)
        dve.drain()
        dve.reciprocal(share[:, :], share[:, :])
        dve.drain()
        dve.tensor_tensor(ratio[:, :], ratio[:, :], share[:, :], ALU.mult)
        dve.tensor_tensor(first[:, :, :], first[:, :, :], share[:, :].unsqueeze(2).to_broadcast(everywhere), ALU.mult)
        dve.drain()
        dve.tensor_tensor(second[:, :, :], second[:, :, :], ratio[:, :].unsqueeze(2).to_broadcast(everywhere), ALU.mult)
        dve.drain()
        dve.tensor_tensor(scores[:, :, :], first[:, :, :], second[:, :, :], ALU.add).then_inc(scores_ready, 1)
        for t in range(0, TILES, 2):
            dve.wait_ge(bias_ready, t // 2 + 1)
            x = s.x[:, t:t + 2, :].rearrange("p t d -> p (t d)")
            dve.tensor_tensor(x, x, s.psum[:, 4 + t // 2 % 2, :], ALU.add).then_inc(bias_added, 1)
        dve.sem_inc(bounded, 2)

        def turn(counts):
            def expert(slot):
                return counts.i * 2 + slot

            def bound(n):
                slot, m, bank = n // (BLOCKS * GROUPS), n % BLOCKS, 2 * (n % 2)
                dve.wait_ge(products, counts.at("block", n + 1))
                dve.tensor_scalar(gate[:, n % 2, :], s.psum[:, bank, :],
                                  gu_b[:, bass.ds(expert(slot), 1), m, 0:1].rearrange("p e s -> p (e s)"), LIMIT, ALU.add,
                                  ALU.min).then_inc(gate_ready, 1)
                dve.tensor_scalar(up[:, n % 2, :], s.psum[:, bank + 1, :], up_b[:, bass.ds(expert(slot), 1), m], LIMIT + 1.0,
                                  ALU.add, ALU.min).then_inc(bounded, 1)

            def finish(n):
                dve.wait_ge(th_ready, counts.at("block", n + 1))
                dve.scalar_tensor_tensor(glu[:, n % 2, :], th[:, n % 2, :], 1.0, gate[:, n % 2, :], ALU.add, ALU.mult)
                dve.drain()
                dve.wait_ge(hid_split, counts.at("block", max(0, n - 1)))
                dve.scalar_tensor_tensor(hidden[:, n % 2, :], up[:, n % 2, :], 1.0 - LIMIT, glu[:, n % 2, :], ALU.max,
                                         ALU.mult).then_inc(hidden_done, 1)
                dve.drain()

            def combine(u):
                slot, g = u // GROUPS, u % GROUPS
                dve.wait_ge(down_ready, counts.at("unit", u + 1))
                for t in range(TG):
                    x = s.x[:, g * TG + t, :]
                    last = dve.scalar_tensor_tensor(x, s.psum[:, 4 + 2 * (u % 2) + t // 2, t % 2 * D:(t % 2 + 1) * D],
                                                    scores[:, g * TG + t, bass.ds(expert(slot), 1)], x, ALU.mult, ALU.add)
                last.then_inc(added, 1)

            dve.drain()
            for n in range(UNITS * BLOCKS):
                bound(n)
                if n >= 1:
                    finish(n - 1)
                if n % BLOCKS == BLOCKS - 1 and n >= 2 * BLOCKS:
                    combine(n // BLOCKS - 2)
            finish(UNITS * BLOCKS - 1)
            combine(UNITS - 2)
            combine(UNITS - 1)

        turns(dve, turn)

    return dict(sync=sync, tensor=tensor, scalar=scalar, vector=vector, gpsimd=gpsimd,
                done=(added, UNITS * EXPERTS // 2))


def program(nc, a, out):
    with ExitStack() as sems, ExitStack() as base:
        s = shared_memory(nc, base)

        def sem(name):
            return sems.enter_context(nc.semaphore(name))

        x_loaded, small_loaded, in_loaded, w_out_loaded, ff_loaded, stored, out_scaled, out_split = (
            sem(n) for n in ("x_loaded", "small_loaded", "in_loaded", "w_out_loaded", "ff_loaded", "stored", "out_scaled",
                             "out_split"))
        x_dram = a["L0_attn_hidden_states"].rearrange("b (t p) d -> p (b t) d", p=P)
        out_dram = out.rearrange("b (t p) d -> p (b t) d", p=P)
        init_constants = constants(nc, s)

        with ExitStack() as layer0:
            u = layer0.enter_context(nc.sbuf_tensor("u_tok", [P, TILES, D], F32))
            with ExitStack() as mem:
                def sb(name, shape, dt=F32):
                    return mem.enter_context(nc.sbuf_tensor(name, shape, dt))

                cols = (XBC_BLOCKS + Z_BLOCKS) * P + HEADS
                w = dict(
                    conv_w=sb("conv_w", [P, XBC_BLOCKS, TAPS]), conv_b=sb("conv_b", [P, XBC_BLOCKS]),
                    D=sb("w_d", [P, HEADS]), norm_w=sb("norm_w", [P, Z_BLOCKS]), A_log=sb("a_log", [P, HEADS]),
                    dt_bias=sb("dt_bias", [P, HEADS]), ln1=sb("ln1", [P, KD]))
                w["in"] = (sb("in_hi", [P, KD, cols], F32R), sb("in_lo", [P, KD, cols], F32R))
                w["out"] = (sb("out_hi", [P, Z_BLOCKS, D], F32R), sb("out_lo", [P, Z_BLOCKS, D], F32R))
                with ExitStack() as early:
                    in_raw = early.enter_context(nc.sbuf_tensor("in_raw", [P, KD, cols], F32))
                    w["out_raw"] = early.enter_context(nc.sbuf_tensor("out_raw", [P, Z_BLOCKS, D], F32))
                    norm_mamba = norm_stage(nc, sems, early, s, "norm_mamba", s.x, "layer_rms", weight=w["ln1"], keep=u,
                                            loaded=x_loaded)
                conv_w, conv_b = a["L0_attn_conv_w"], a["L0_attn_conv_b"]
                small = [(w["conv_w"][:, 0:2, :], conv_w[0:2 * P, :].rearrange("(m p) k -> p m k", p=P)),
                         (w["conv_b"][:, 0:2], conv_b[0:2 * P].rearrange("(m p) -> p m", p=P))]
                for g in range(2):
                    rows = slice(g * STATE, (g + 1) * STATE)
                    at = 2 * P + g * REP * STATE
                    small += [(w["conv_w"][rows, 2:, :],
                               conv_w[at:at + REP * STATE, :].rearrange("(m p) k -> p m k", p=STATE)),
                              (w["conv_b"][rows, 2:], conv_b[at:at + REP * STATE].rearrange("(m p) -> p m", p=STATE))]
                small += [(w["D"][:, :], a["L0_attn_D"].partition_broadcast(P)),
                          (w["A_log"][:, :], a["L0_attn_A_log"].partition_broadcast(P)),
                          (w["dt_bias"][:, :], a["L0_attn_dt_bias"].partition_broadcast(P)),
                          (w["norm_w"][:, :], a["L0_attn_norm_w"].rearrange("(m p) -> p m", p=P)),
                          (w["ln1"][:, :], a["L0_attn_ln1_w"].rearrange("(m p) -> p m", p=P))]

                def in_job(to, at, n):
                    return [(in_raw[:, k, at:at + n], w["in"][0][:, k, to:to + n], w["in"][1][:, k, to:to + n], None)
                            for k in range(KD)]

                jobs = in_job(0, INNER, 2 * XB)
                for g in range(2):
                    for k in range(KD):
                        at = INNER + 2 * XB + g * REP * STATE
                        raw = in_raw[:, k, at:at + REP * STATE].rearrange("p (m n) -> p m n", n=STATE)
                        hi, lo = (part[:, k, 2 * XB:2 * XB + INNER].rearrange("p (m g n) -> p m g n", g=2, n=STATE)[:, :, g, :]
                                  for part in w["in"])
                        jobs.append((raw, hi, lo, None))
                jobs += in_job(2 * XB + INNER, 0, INNER) + in_job(2 * XB + 2 * INNER, 2 * XB + 2 * INNER, HEADS)
                in_split = split_weights(nc, sems, "in", (in_loaded, 16), jobs)
                mamba = mamba_stage(nc, sems, mem, s, w,
                                    dict(small=(small_loaded, 16 * len(small)), w_out=(w_out_loaded, 16),
                                         in_split=in_split["done"], normed=norm_mamba["done"], out_split=(out_split, 1)), u)

            blocks = len(chunk_sizes(LUT_FF))
            gate_t, up_t, down_t = (
                tuple(layer0.enter_context(nc.sbuf_tensor(f"{name}_{part}", shape, F32R)) for part in ("hi", "lo"))
                for name, shape in (("gate_t", [P, KD, blocks * P]), ("up_t", [P, KD, blocks * P]),
                                    ("down_t", [P, blocks, D])))
            with ExitStack() as mem:
                table = table_stage(nc, sems, mem, s, a["L0_ffn_lut"], a["L0_ffn_gate_idx"], a["L0_ffn_up_idx"],
                                    a["L0_ffn_down_idx"], gate_t, up_t, down_t)

            with ExitStack() as mem:
                def sb(name, shape, dt=F32):
                    return mem.enter_context(nc.sbuf_tensor(name, shape, dt))

                ln2 = sb("ln2", [P, KD])
                gate, up = ((sb(f"{n}_hi", [P, KD, FF], F32R), sb(f"{n}_lo", [P, KD, FF], F32R)) for n in ("gate", "up"))
                down = (sb("down_hi", [P, FF // P, D], F32R), sb("down_lo", [P, FF // P, D], F32R))
                with ExitStack() as early:
                    raws = [early.enter_context(nc.sbuf_tensor(f"{n}_raw", shape, F32)) for n, shape in (
                        ("gate", [P, KD, FF]), ("up", [P, KD, FF]), ("down", [P, FF // P, D]))]
                    norm_mlp = norm_stage(nc, sems, early, s, "norm_mlp", u, "rms", weight=ln2)
                mlp_split = split_weights(nc, sems, "mlp", (ff_loaded, 64), [
                    (raw[:, :, :], pair[0][:, :, :], pair[1][:, :, :], scale)
                    for raw, pair, scale in zip(raws, (gate, up, down), (None, None, 0.5))])
                mlp = gated_stage(nc, sems, mem, s, "mlp", FF // P, (gate, up, down), [mlp_split["done"], norm_mlp["done"]],
                                  residual=u)

            with ExitStack() as mem:
                norm_ffn = norm_stage(nc, sems, mem, s, "norm_ffn", s.x, "layer")
                ffn = gated_stage(nc, sems, mem, s, "ffn", blocks, (gate_t, up_t, down_t),
                                  [table["done"], table["zeroed"], norm_ffn["done"]])

        with ExitStack() as mem:
            norm_attention = norm_stage(nc, sems, mem, s, "norm_attn", s.x, "layer")
        with ExitStack() as mem:
            attention = attention_stage(nc, sems, mem, s, a, ffn["done"], norm_attention["done"])

        with ExitStack() as mem:
            norm_moe = norm_stage(nc, sems, mem, s, "norm_moe", s.x, "layer")
            moe = moe_stage(nc, sems, mem, s, a, attention["done"], norm_moe["done"])

        block = base.enter_context(nc.Block())

        @block.sync
        def _(sp):
            for g in range(GROUPS):
                sp.dma_start(s.x[:, g * TG:(g + 1) * TG, :], x_dram[:, g * TG:(g + 1) * TG, :]).then_inc(x_loaded, 16)
            with nc.allow_non_contiguous_dma(reason="small vectors, one element for each partition"):
                for dst, src in small:
                    sp.dma_start(dst, src).then_inc(small_loaded, 16)
            sp.dma_start(in_raw[:, :, :], a["L0_attn_in_proj_w"].rearrange("(k p) n -> p k n", p=P)).then_inc(in_loaded, 16)
            sp.dma_start(w["out_raw"][:, :, :],
                         a["L0_attn_out_proj_w"].rearrange("(k p) n -> p k n", p=P)).then_inc(w_out_loaded, 16)
            sp.wait_ge(*mamba["done"])
            table["sync"](sp)
            sp.wait_ge(*table["done"])
            with nc.allow_non_contiguous_dma(reason="one element for each partition"):
                sp.dma_start(ln2[:, :], a["L0_attn_ln2_w"].rearrange("(m p) -> p m", p=P)).then_inc(ff_loaded, 16)
            for n, raw in zip(("gate", "up", "down"), raws):
                sp.dma_start(raw[:, :, :], a[f"L0_attn_{n}_w"].rearrange("(k p) n -> p k n", p=P)).then_inc(ff_loaded, 16)
            attention["sync"](sp)
            moe["sync"](sp)
            sp.wait_ge(*moe["done"])
            sp.dma_start(out_dram, s.x[:, :, :]).then_inc(stored, 16)
            sp.wait_ge(stored, 16)

        @block.vector
        def _(dve):
            norm_mamba["vector"](dve)
            mamba["vector"](dve)
            table["vector"](dve)
            dve.wait_ge(ff_loaded, 64)
            norm_mlp["vector"](dve)
            mlp["vector"](dve)
            norm_ffn["vector"](dve)
            ffn["vector"](dve)
            norm_attention["vector"](dve)
            attention["vector"](dve)
            norm_moe["vector"](dve)
            moe["vector"](dve)

        @block.scalar
        def _(act):
            in_split["scalar"](act)
            norm_mamba["scalar"](act)
            act.wait_ge(*mamba["prep"])
            act.activation(w["out"][0][:, :, :], w["out_raw"][:, :, :], ACT.Copy).then_inc(out_scaled, 1)
            mamba["scalar"](act)
            act.wait_ge(*mamba["done"])
            table["scalar"](act)
            mlp_split["scalar"](act)
            norm_mlp["scalar"](act)
            mlp["scalar"](act)
            norm_ffn["scalar"](act)
            ffn["scalar"](act)
            norm_attention["scalar"](act)
            attention["scalar"](act)
            norm_moe["scalar"](act)
            moe["scalar"](act)

        @block.gpsimd
        def _(pool):
            init_constants(pool)
            in_split["gpsimd"](pool)
            norm_mamba["gpsimd"](pool)
            pool.wait_ge(out_scaled, 1)
            pool.tensor_tensor(w["out"][1][:, :, :], w["out_raw"][:, :, :], w["out"][0][:, :, :].bitcast(F32),
                               ALU.subtract).then_inc(out_split, 1)
            mamba["gpsimd"](pool)
            pool.wait_ge(*mamba["done"])
            table["gpsimd"](pool)
            mlp_split["gpsimd"](pool)
            norm_mlp["gpsimd"](pool)
            mlp["gpsimd"](pool)
            norm_ffn["gpsimd"](pool)
            ffn["gpsimd"](pool)
            norm_attention["gpsimd"](pool)
            attention["gpsimd"](pool)
            norm_moe["gpsimd"](pool)
            moe["gpsimd"](pool)

        @block.tensor
        def _(pe):
            norm_mamba["tensor"](pe)
            mamba["tensor"](pe)
            table["tensor"](pe)
            norm_mlp["tensor"](pe)
            mlp["tensor"](pe)
            norm_ffn["tensor"](pe)
            ffn["tensor"](pe)
            norm_attention["tensor"](pe)
            attention["tensor"](pe)
            norm_moe["tensor"](pe)
            moe["tensor"](pe)


_INS = [
    "L0_attn_hidden_states", "L0_attn_in_proj_w", "L0_attn_conv_w", "L0_attn_conv_b", "L0_attn_dt_bias",
    "L0_attn_A_log", "L0_attn_D", "L0_attn_norm_w", "L0_attn_out_proj_w", "L0_attn_ln1_w", "L0_attn_ln2_w",
    "L0_attn_gate_w", "L0_attn_up_w", "L0_attn_down_w", "L0_ffn_lut", "L0_ffn_gate_idx", "L0_ffn_up_idx",
    "L0_ffn_down_idx", "L1_attn_W_Q", "L1_attn_W_K", "L1_attn_W_V", "L1_attn_W_O", "L1_attn_b_Q", "L1_attn_b_K",
    "L1_attn_b_V", "L1_attn_b_O", "L1_ffn_router_weight", "L1_ffn_router_bias", "L1_ffn_gate_up_proj",
    "L1_ffn_gate_up_proj_bias", "L1_ffn_down_proj", "L1_ffn_down_proj_bias",
]


def kernel(**inputs):
    import numpy as _np
    import concourse.bacc as _bacc
    from concourse.bass_utils import run_bass_kernel_spmd as _run

    nc = _bacc.Bacc("TRN2", target_bir_lowering=False, num_devices=1)
    arrays, args = {}, {}
    for name in _INS:
        array = _np.ascontiguousarray(inputs[name])
        arrays[f"in_{name}_dram"] = array
        args[name] = nc.dram_tensor(f"in_{name}_dram", array.shape, mybir.dt.from_np(array.dtype), kind="ExternalInput").ap()
    out = nc.dram_tensor("out_0_dram", (BATCH, SEQ, D), F32, kind="ExternalOutput").ap()
    program(nc, args, out)
    r = _run(nc, [arrays], core_ids=[0])
    return r.results[0]["out_0_dram"]
```

```python
from contextlib import ExitStack

import concourse.bass as bass
from concourse import mybir

F32 = mybir.dt.float32
F32R = mybir.dt.float32r
BF16 = mybir.dt.bfloat16
I32 = mybir.dt.int32
ALU = mybir.AluOpType
ACT = mybir.ActivationFunctionType
AX_X = mybir.AxisListType.X

P = 128
BATCH, SEQ, D = 2, 1024, 256
KD = D // P
TILES = BATCH * SEQ // P
GROUP = 512
TG = GROUP // P
GROUPS = TILES // TG
EPS = 1e-5
INNER, XB, STATE, HEAD, HEADS = 512, 128, 64, 64, 8
REP = HEADS // 2
XBC_BLOCKS = (XB + XB + INNER) // P
Z_BLOCKS = INNER // P
TAPS = 4
CHUNKS = SEQ // P
FF = 1024
LUT_FF, LUT_SIZE = 688, 16
TABLE_MEMORY = 26 * 3 * D + LUT_SIZE * 3 // 2
MLP_WEIGHTS = 2 * (2 * KD * FF + FF // P * D)
AH, AE = 16, 128
PAIRS = AH // 2
SCORE_SCALE = float(AE) ** -0.5
MASKED = -1.0e30
QT = SEQ // P
EXPERTS, EI = 8, 256
ALPHA, LIMIT = 1.702, 7.0


def chunk_sizes(n):
    return [min(P, n - at) for at in range(0, n, P)]


def three_passes(pe, out, stationary, moving, start, stop):
    (s_hi, s_lo), (m_hi, m_lo) = stationary, moving
    pe.matmul(out, s_hi, m_hi, start=start, stop=False)
    pe.matmul(out, s_hi, m_lo, start=False, stop=False)
    return pe.matmul(out, s_lo, m_hi, start=False, stop=stop)


def pair_at(pair, *where):
    return tuple(t[where] for t in pair)


class Shared:
    pass


def shared_memory(nc, mem):
    s = Shared()
    s.psum = mem.enter_context(nc.psum_tensor("psum", [P, 8, 512], F32))
    s.x = mem.enter_context(nc.sbuf_tensor("x_tok", [P, TILES, D], F32))
    s.act_hi = mem.enter_context(nc.sbuf_tensor("act_hi", [P, KD, TILES * P], F32R))
    s.act_lo = mem.enter_context(nc.sbuf_tensor("act_lo", [P, KD, TILES * P], F32R))
    s.act = (s.act_hi, s.act_lo)
    s.ident = mem.enter_context(nc.sbuf_tensor("ident", [P, P], F32))
    s.upper = mem.enter_context(nc.sbuf_tensor("upper", [P, P], F32))
    s.ones = mem.enter_context(nc.sbuf_tensor("ones", [P, P], F32))
    s.minus_half = mem.enter_context(nc.sbuf_tensor("minus_half", [P, 16], F32))
    s.wait_over = mem.enter_context(nc.semaphore("wait_over"))
    s.consts_ready = mem.enter_context(nc.semaphore("consts_ready"))
    return s


CONSTS = 6


def constants(nc, s):

    def gpsimd(pool):
        pool.memset(s.ident[:, :], 0.0).then_inc(s.consts_ready, 1)
        pool.memset(s.upper[:, :], 1.0).then_inc(s.consts_ready, 1)
        pool.memset(s.ones[:, :], 1.0).then_inc(s.consts_ready, 1)
        pool.memset(s.minus_half[:, :], -0.5).then_inc(s.consts_ready, 1)
        pool.wait_ge(s.consts_ready, 4)
        pool.affine_select(out=s.ident[:, :], in_=s.ident[:, :], compare_op=ALU.not_equal, fill=1.0, base=0,
                           pattern=[[-1, P]], channel_multiplier=1).then_inc(s.consts_ready, 1)
        pool.affine_select(out=s.upper[:, :], in_=s.upper[:, :], compare_op=ALU.is_ge, fill=0.0, base=0,
                           pattern=[[1, P]], channel_multiplier=-1).then_inc(s.consts_ready, 1)

    return gpsimd


def norm_stage(nc, sems, mem, s, name, source, mode, weight=None, keep=None, bank=0):
    roots = 2 if mode == "layer_rms" else 1

    def sem(what):
        return sems.enter_context(nc.semaphore(f"{name}_{what}"))

    var_ready, root_ready, normed, turned, hi_ready, split_ready = (
        sem(x) for x in ("var_ready", "root_ready", "normed", "turned", "hi_ready", "split_ready"))
    stats = mem.enter_context(nc.sbuf_tensor(f"{name}_stats", [P, TG, 6], F32))
    moments = mem.enter_context(nc.sbuf_tensor(f"{name}_moments", [P, TG, 2], F32))
    var = mem.enter_context(nc.sbuf_tensor(f"{name}_var", [P, TG], F32))
    root = mem.enter_context(nc.sbuf_tensor(f"{name}_root", [P, TG], F32))
    root2 = mem.enter_context(nc.sbuf_tensor(f"{name}_root2", [P, TG], F32))
    normal = mem.enter_context(nc.sbuf_tensor(f"{name}_normal", [P, TG, D], F32))

    def tile(i, t):
        return (i % GROUPS if isinstance(i, int) else i) * TG + t

    def tokens(i):
        return bass.ds((i % GROUPS if isinstance(i, int) else i) * GROUP, GROUP)

    def stats_step(dve, i):
        dve.drain()
        for t in range(TG):
            dve.bn_stats(stats[:, t, :], source[:, tile(i, t), :])
        dve.drain()
        for t in range(TG):
            dve.bn_aggr(moments[:, t, :], stats[:, t, :])
        dve.drain()
        if mode == "rms":
            dve.tensor_tensor(var[:, :], moments[:, :, 0], moments[:, :, 0], ALU.mult)
            dve.drain()
            dve.tensor_tensor(var[:, :], var[:, :], moments[:, :, 1], ALU.add)
            dve.drain()
            dve.tensor_scalar(var[:, :], var[:, :], EPS, None, ALU.add).then_inc(var_ready, 1)
        else:
            dve.tensor_scalar(var[:, :], moments[:, :, 1], EPS, None, ALU.add).then_inc(var_ready, 1)

    def roots_step(pool, i):
        pool.wait_ge(var_ready, roots * i + 1)
        pool.tensor_tensor(root[:, :], var[:, :], s.minus_half[:, 0:TG], ALU.pow).then_inc(root_ready, 1)
        if roots == 2:
            pool.wait_ge(var_ready, 2 * i + 2)
            pool.tensor_tensor(root2[:, :], var[:, :], s.minus_half[:, 0:TG], ALU.pow).then_inc(root_ready, 1)

    def apply_step(dve, i):
        dve.wait_ge(root_ready, roots * i + 1)
        dve.wait_ge(turned, KD * i)
        if mode == "layer_rms":
            dve.tensor_tensor(var[:, :], moments[:, :, 1], root[:, :], ALU.mult)
            dve.drain()
            dve.tensor_tensor(var[:, :], var[:, :], root[:, :], ALU.mult)
            dve.drain()
            dve.tensor_scalar(var[:, :], var[:, :], EPS, None, ALU.add).then_inc(var_ready, 1)
            for t in range(TG):
                dve.tensor_scalar(keep[:, i * TG + t, :], source[:, tile(i, t), :], moments[:, t, 0:1],
                                  root[:, t:t + 1], ALU.subtract, ALU.mult)
            dve.drain()
            dve.wait_ge(root_ready, 2 * i + 2)
            for t in range(TG):
                last = dve.tensor_scalar(normal[:, t, :], keep[:, i * TG + t, :], root2[:, t:t + 1], None,
                                         ALU.mult)
        elif mode == "rms":
            for t in range(TG):
                last = dve.tensor_scalar(normal[:, t, :], source[:, tile(i, t), :], root[:, t:t + 1], None,
                                         ALU.mult)
        else:
            for t in range(TG):
                last = dve.tensor_scalar(normal[:, t, :], source[:, tile(i, t), :], moments[:, t, 0:1],
                                         root[:, t:t + 1], ALU.subtract, ALU.mult)
        last.then_inc(normed, 1)

    def turn_step(pe, i):
        pe.wait_ge(normed, i + 1)
        pe.wait_ge(split_ready, KD * i)
        for k in range(KD):
            for t in range(TG):
                last = pe.transpose(s.psum[:, bank + k, t * P:(t + 1) * P], normal[:, t, k * P:(k + 1) * P], s.ident[:, :])
            last.then_inc(turned, 1)

    def high_step(act, i):
        for k in range(KD):
            act.wait_ge(turned, KD * i + k + 1)
            act.activation(s.act_hi[:, k, tokens(i)], s.psum[:, bank + k, :], ACT.Copy,
                           scale=1.0 if weight is None else weight[:, k:k + 1]).then_inc(hi_ready, 1)

    def low_step(dve, i):
        for k in range(KD):
            dve.wait_ge(hi_ready, KD * i + k + 1)
            dve.scalar_tensor_tensor(
                s.act_lo[:, k, tokens(i)], s.psum[:, bank + k, :], 1.0 if weight is None else weight[:, k:k + 1],
                s.act_hi[:, k, tokens(i)].bitcast(F32), ALU.mult, ALU.subtract).then_inc(split_ready, 1)

    def ready(i):
        return split_ready, KD * (i + 1)

    return dict(stats=stats_step, roots=roots_step, apply=apply_step, turn=turn_step, high=high_step, low=low_step,
                ready=ready)


def norm_groups(norm, groups):

    def vector(dve):
        for i in groups:
            norm["stats"](dve, i)
            norm["apply"](dve, i)
            norm["low"](dve, i)

    def gpsimd(pool):
        for i in groups:
            norm["roots"](pool, i)

    def tensor(pe):
        for i in groups:
            norm["turn"](pe, i)

    def scalar(act):
        for i in groups:
            norm["high"](act, i)

    return dict(vector=vector, gpsimd=gpsimd, tensor=tensor, scalar=scalar)


def gated_stage(nc, sems, mem, s, name, blocks, weights, weights_ready, norm, residual=None):
    gate_w, up_w, down_w = weights

    def sem(what):
        return sems.enter_context(nc.semaphore(f"{name}_{what}"))

    products, tanh_ready, hidden_done, hi_ready, hidden_split, down_ready, added = (
        sem(x) for x in ("products", "tanh_ready", "hidden_done", "hi_ready", "hidden_split", "down_ready", "added"))
    th = mem.enter_context(nc.sbuf_tensor(f"{name}_th", [P, 2, GROUP], F32))
    silu = mem.enter_context(nc.sbuf_tensor(f"{name}_silu", [P, 2, GROUP], F32))
    hidden = mem.enter_context(nc.sbuf_tensor(f"{name}_hidden", [P, 2, GROUP], F32))
    h_hi = mem.enter_context(nc.sbuf_tensor(f"{name}_h_hi", [P, blocks, GROUP], F32R))
    h_lo = mem.enter_context(nc.sbuf_tensor(f"{name}_h_lo", [P, blocks, GROUP], F32R))
    hid = (h_hi, h_lo)
    total = mem.enter_context(nc.sbuf_tensor(f"{name}_total", [P, 2 * D], F32))
    HALVES = TG // 2

    def groups(engine, group):
        with engine.Fori(0, GROUPS - 1) as i:
            group(i, norm)
        group(GROUPS - 1, None)

    def tensor(pe):
        for ready, value in weights_ready:
            pe.wait_ge(ready, value)
        norm["turn"](pe, 0)

        def group(i, norm_next):
            pe.wait_ge(*norm["ready"](i))
            for f in range(blocks):
                pe.wait_ge(hidden_done, blocks * i + f + 1)
                for bank, w in ((2 * (f % 2), gate_w), (2 * (f % 2) + 1, up_w)):
                    for k in range(KD):
                        last = three_passes(pe, s.psum[:, bank, :], pair_at(w, slice(None), k, slice(f * P, (f + 1) * P)),
                                            pair_at(s.act, slice(None), k, bass.ds(i * GROUP, GROUP)),
                                            k == 0, k == KD - 1)
                last.then_inc(products, 1)
            if norm_next:
                norm_next["turn"](pe, i + 1)
            pe.wait_ge(hidden_split, blocks * (i + 1))
            pe.wait_ge(added, HALVES * i)
            for half in range(HALVES):
                for t in (2 * half, 2 * half + 1):
                    for f in range(blocks):
                        last = three_passes(pe, s.psum[:, 4 + half, (t % 2) * D:(t % 2 + 1) * D],
                                            pair_at(hid, slice(None), f, slice(t * P, (t + 1) * P)),
                                            pair_at(down_w, slice(None), f), f == 0, f == blocks - 1)
                last.then_inc(down_ready, 1)

        groups(pe, group)

    def scalar(act):
        norm["high"](act, 0)

        def group(i, norm_next):
            for f in range(blocks + 1):
                if f < blocks:
                    act.wait_ge(products, blocks * i + f + 1)
                    act.activation(th[:, f % 2, :], s.psum[:, 2 * (f % 2), :], ACT.Tanh, scale=0.5).then_inc(tanh_ready, 1)
                if f >= 1:
                    act.wait_ge(hidden_done, 2 + blocks * i + f)
                    if f == 1:
                        act.wait_ge(down_ready, HALVES * i)
                    act.activation(h_hi[:, f - 1, :], hidden[:, (f - 1) % 2, :], ACT.Copy).then_inc(hi_ready, 1)
            if norm_next:
                norm_next["high"](act, i + 1)

        groups(act, group)

    def gpsimd(pool):
        norm["roots"](pool, 0)

        def group(i, norm_next):
            for f in range(blocks):
                if norm_next and f == 1:
                    norm_next["roots"](pool, i + 1)
                pool.wait_ge(hi_ready, blocks * i + f + 1)
                pool.tensor_tensor(h_lo[:, f, :], hidden[:, f % 2, :], h_hi[:, f, :].bitcast(F32),
                                   ALU.subtract).then_inc(hidden_split, 1)

        groups(pool, group)

    def vector(dve):
        dve.sem_inc(hidden_done, 2)
        for step in ("stats", "apply", "low"):
            norm[step](dve, 0)

        def group(i, norm_next):
            for f in range(blocks):
                dve.wait_ge(tanh_ready, blocks * i + f + 1)
                dve.scalar_tensor_tensor(silu[:, f % 2, :], th[:, f % 2, :], 1.0, s.psum[:, 2 * (f % 2), :], ALU.add, ALU.mult)
                dve.drain()
                if f >= 2:
                    dve.wait_ge(hidden_split, blocks * i + f - 1)
                else:
                    dve.wait_ge(hidden_split, blocks * i)
                dve.tensor_tensor(hidden[:, f % 2, :], silu[:, f % 2, :], s.psum[:, 2 * (f % 2) + 1, :],
                                  ALU.mult).then_inc(hidden_done, 1)
                if norm_next and f == 0:
                    norm_next["stats"](dve, i + 1)
                if norm_next and f == 2:
                    norm_next["apply"](dve, i + 1)
            if norm_next:
                norm_next["low"](dve, i + 1)
            for half in range(HALVES):
                dve.wait_ge(down_ready, HALVES * i + half + 1)
                sums = s.psum[:, 4 + half, :]
                x = s.x[:, bass.ds(i * TG + 2 * half, 2), :].rearrange("p t d -> p (t d)")
                if residual is not None:
                    dve.tensor_tensor(total[:, :], sums,
                                      residual[:, bass.ds(i * TG + 2 * half, 2), :].rearrange("p t d -> p (t d)"), ALU.add)
                    dve.drain()
                    dve.tensor_tensor(x, x, total[:, :], ALU.add).then_inc(added, 1)
                else:
                    dve.tensor_tensor(x, x, sums, ALU.add).then_inc(added, 1)
                dve.drain()

        groups(dve, group)

    return dict(vector=vector, gpsimd=gpsimd, tensor=tensor, scalar=scalar, done=(added, HALVES * GROUPS))


def split_weights(nc, sems, name, loaded, jobs):
    scaled = sems.enter_context(nc.semaphore(f"{name}_scaled"))
    hi_ready = sems.enter_context(nc.semaphore(f"{name}_weights_hi"))
    split_ready = sems.enter_context(nc.semaphore(f"{name}_weights_split"))

    def scalar(act):
        n = 0
        act.wait_ge(*loaded)
        for raw, hi, lo, scale in jobs:
            if scale is not None:
                act.activation(raw, raw, ACT.Copy, scale=scale).then_inc(scaled, 1)
                n += 1
                act.wait_ge(scaled, n)
            act.activation(hi, raw, ACT.Copy).then_inc(hi_ready, 1)

    def gpsimd(pool):
        pool.wait_ge(*loaded)
        for n, (raw, hi, lo, scale) in enumerate(jobs):
            pool.wait_ge(hi_ready, n + 1)
            pool.tensor_tensor(lo, raw, hi.bitcast(F32), ALU.subtract).then_inc(split_ready, 1)

    return dict(scalar=scalar, gpsimd=gpsimd, done=(split_ready, len(jobs)))


def table_stage(nc, sems, mem, s, lut, gate_idx, up_idx, down_idx, gate_t, up_t, down_t):

    def sem(what):
        return sems.enter_context(nc.semaphore(f"table_{what}"))

    loaded, steps_ready, bit_ready, leaves_ready, picked, turned, hi_ready, split_ready, zeroed = (
        sem(x) for x in ("table_loaded", "steps_ready", "bit_ready", "leaves_ready", "picked", "turned", "hi_ready",
                         "split_ready", "zeroed"))
    idx_loaded = [sem(f"idx_loaded_{n}") for n in range(2)]
    WIDTH = 3 * D
    PADS = 6
    full, rest = divmod(LUT_FF, P)
    table = mem.enter_context(nc.sbuf_tensor("table", [P, LUT_SIZE], F32))
    steps = mem.enter_context(nc.sbuf_tensor("table_steps", [P, LUT_SIZE // 2], F32))
    idx = mem.enter_context(nc.sbuf_tensor("table_idx", [P, 2, WIDTH], I32))
    bits = mem.enter_context(nc.sbuf_tensor("table_bits", [P, 2, 4, WIDTH], I32))
    leaves = mem.enter_context(nc.sbuf_tensor("table_leaves", [P, 2, LUT_SIZE // 2, WIDTH], F32))
    pieces, halved = [], set()
    for src, out in ((gate_idx, gate_t), (up_idx, up_t)):
        for first, n in ((0, 3), (3, full - 3)):
            loads = [(lambda i, n=n: i.rearrange("p (c d) -> p c d", c=n),
                      src[first * P:(first + n) * P, :].rearrange("(c p) d -> p c d", p=P))]
            turns = [(k, c * P, P, c * D + k * P, P) for k in range(KD) for c in range(n)]
            evac = [(k, P, n * P, pair_at(out, slice(None), k, slice(first * P, (first + n) * P))) for k in range(KD)]
            pieces.append((loads, P, n * D, turns, evac))
    loads = [(lambda i, n=n: i[:, n * D:(n + 1) * D], src[full * P:LUT_FF, :]) for n, src in enumerate((gate_idx, up_idx))]
    turns = [(k, n * P, rest, n * D + k * P, P) for n in range(2) for k in range(KD)]
    evac = [(k, P, (n * P, rest), pair_at(out, slice(None), k, slice(full * P, LUT_FF)))
            for n, out in enumerate((gate_t, up_t)) for k in range(KD)]
    pieces.append((loads, rest, 2 * D, turns, evac))
    for o in range(KD):
        loads = [(lambda i: i, down_idx[o * P:(o + 1) * P, :])]
        turns = [(f // 4, (f % 4) * P, P, f * P, P if f < full else rest) for f in range(full + 1)]
        cols = slice(o * P, (o + 1) * P)
        evac = [(0, P, 4 * P, pair_at(down_t, slice(None), slice(0, 4), cols)),
                (1, P, P, pair_at(down_t, slice(None), 4, cols)),
                (1, rest, (P, P), pair_at(down_t, slice(0, rest), 5, cols))]
        pieces.append((loads, P, LUT_FF, turns, evac))
        halved.add(len(pieces) - 1)
    n_loads = [sum(len(p[0]) for p in pieces[n % 2:n + 1:2]) for n in range(len(pieces))]
    n_evac = [sum(len(p[4]) for p in pieces[:n]) for n in range(len(pieces) + 1)]

    def sync(sp):
        sp.dma_start(table[:, :], lut.partition_broadcast(P)).then_inc(loaded, 16)
        for n, (loads, rows, width, _, _) in enumerate(pieces):
            if n >= 2:
                sp.wait_ge(bit_ready, n - 1)
            for place, src in loads:
                sp.dma_start(place(idx[0:rows, n % 2, 0:width]), src).then_inc(idx_loaded[n % 2], 16)

    def vector(dve):
        dve.wait_ge(loaded, 16)
        dve.tensor_tensor(steps[:, :], table[:, 1::2], table[:, 0::2], ALU.subtract).then_inc(steps_ready, 1)
        take_bits(dve, 0)
        for n in range(len(pieces)):
            if n + 1 < len(pieces):
                take_bits(dve, n + 1)
            pick(dve, n)
            if n >= 1:
                evacuate(dve, n - 1)
        evacuate(dve, len(pieces) - 1)

    def take_bits(dve, n):
        _, rows, width, _, _ = pieces[n]
        dve.wait_ge(idx_loaded[n % 2], 16 * n_loads[n])
        if n >= 2:
            dve.wait_ge(leaves_ready, n - 1)
        for b in range(4):
            last = dve.tensor_scalar(bits[0:rows, n % 2, b, 0:width], idx[0:rows, n % 2, 0:width], 1 << b, None,
                                     ALU.bitwise_and)
        last.then_inc(bit_ready, 1)

    def pick(dve, n):
        _, rows, width, _, _ = pieces[n]
        dve.drain()
        dve.wait_ge(leaves_ready, n + 1)
        for b, step in ((1, 1), (2, 2), (3, 4)):
            for j in range(0, LUT_SIZE // 2, 2 * step):
                last = dve.copy_predicated(leaves[0:rows, n % 2, j, 0:width], bits[0:rows, n % 2, b, 0:width],
                                           leaves[0:rows, n % 2, j + step, 0:width])
            dve.drain()
        last.then_inc(picked, 1)

    def evacuate(dve, n):
        dve.wait_ge(hi_ready, n_evac[n + 1])
        for bank, rows, cols, out in pieces[n][4]:
            dve.scalar_tensor_tensor(out[1], turned_at(n, bank, rows, cols, out[1]), scale(n), out[0].bitcast(F32), ALU.mult,
                                     ALU.subtract).then_inc(split_ready, 1)

    def scale(n):
        return 0.5 if n in halved else 1.0

    def turned_at(n, bank, rows, cols, like):
        first, size = cols if isinstance(cols, tuple) else (0, cols)
        view = s.psum[0:rows, 2 * (n % 2) + bank, first:first + size]
        return view.rearrange("p (a b) -> p a b", b=P) if len(like.shape) == 3 else view

    def scalar(act):
        act.wait_ge(steps_ready, 1)
        act.wait_ge(zeroed, PADS)
        grow(act, 0)
        for n in range(len(pieces)):
            if n + 1 < len(pieces):
                grow(act, n + 1)
            act.wait_ge(turned, n + 1)
            for bank, r, cols, out in pieces[n][4]:
                act.activation(out[0], turned_at(n, bank, r, cols, out[0]), ACT.Copy, scale=scale(n)).then_inc(hi_ready, 1)

    def grow(act, n):
        _, rows, width, _, _ = pieces[n]
        act.wait_ge(bit_ready, n + 1)
        if n >= 2:
            act.wait_ge(turned, n - 1)
        for j in range(LUT_SIZE // 2):
            last = act.activation(leaves[0:rows, n % 2, j, 0:width], bits[0:rows, n % 2, 0, 0:width], ACT.Identity,
                                  scale=steps[0:rows, j:j + 1], bias=table[0:rows, 2 * j:2 * j + 1])
        last.then_inc(leaves_ready, 1)

    def gpsimd(pool):
        for part in (0, 1):
            for pad in (gate_t[part][:, :, LUT_FF:], up_t[part][:, :, LUT_FF:], down_t[part][:, full, :]):
                pool.memset(pad.bitcast(F32), 0.0).then_inc(zeroed, 1)

    def tensor(pe):
        pe.wait_ge(s.consts_ready, CONSTS)
        for n, (_, rows, width, turns, _) in enumerate(pieces):
            pe.wait_ge(picked, n + 1)
            if n >= 2:
                pe.wait_ge(split_ready, n_evac[n - 1])
            for bank, at, size, col, out_rows in turns:
                last = pe.transpose(s.psum[0:out_rows, 2 * (n % 2) + bank, at:at + size], leaves[0:size, n % 2, 0, col:col + out_rows],
                                    s.ident[0:size, 0:size])
            last.then_inc(turned, 1)

    return dict(sync=sync, vector=vector, scalar=scalar, gpsimd=gpsimd, tensor=tensor, done=(split_ready, n_evac[-1]),
                zeroed=(zeroed, PADS))


def mamba_stage(nc, sems, mem, s, w, dma, u):

    def sem(what):
        return sems.enter_context(nc.semaphore(f"mamba_{what}"))

    def sb(what, shape, dt=F32):
        return mem.enter_context(nc.sbuf_tensor(f"mamba_{what}", shape, dt))

    names = ("prep dt_product dt_biased dt_exp dt_log dt_log_in dt_done sums_ready sums_copied decay_rate "
             "projected evacuated conv_sum conv_tanh conv_done gate_tanh gate_done "
             "steps rows_ready masks masked row_exp leaves turned b_copied xdt mixed scores_ready c_scaled xdt_decayed "
             "lower_done y_ready state_ready state_done gated gated_hi squares gated_lo out_ready out_var out_root out_done")

    done = {n: sem(n) for n in names.split()}

    conv_in = sb("conv_in", [P, XBC_BLOCKS, GROUP + TAPS - 1])
    conv_sum = sb("conv_sum", [P, 2, GROUP])
    conv_th = sb("conv_th", [P, 2, GROUP])
    xbc = sb("xbc", [P, 2, XBC_BLOCKS, GROUP])
    zs = sb("zs", [P, 2, Z_BLOCKS, GROUP])
    step_dt = sb("step_dt", [P, TILES, HEADS])
    step_da = sb("step_da", [P, TILES, HEADS])
    minus_cum = sb("minus_cum", [P, TILES, HEADS])
    d_head = sb("d_head", [P, Z_BLOCKS, P])
    steps = sb("steps", [P, HEADS, P])
    decay = sb("decay", [P, 2, HEADS, P])
    mixed = sb("mixed", [P, 2, HEADS, P])
    row_exp = sb("row_exp", [P, 2, REP, P])
    b_tok = sb("b_tok", [P, 2, P])
    xdt = sb("xdt", [P, 2, HEADS, HEAD])
    xdt_decayed = sb("xdt_decayed", [P, HEADS, HEAD])
    ident_b, mask = sb("ident_b", [P, P], BF16), sb("mask", [P, P], BF16)
    c_scaled = sb("c_scaled", [P, 2, REP, P])
    state = sb("state", [P, REP, HEAD])
    gated = sb("gated", [P, Z_BLOCKS, P])
    gated_hi = sb("gated_hi", [P, Z_BLOCKS, P], F32R)
    gated_lo = sb("gated_lo", [P, Z_BLOCKS, P], F32R)
    squares = sb("squares", [P, Z_BLOCKS, P])
    out_var = sb("out_var", [P, 1])
    out_root = sb("out_root", [P, 1])

    IP = XBC_BLOCKS + Z_BLOCKS
    GB = SEQ // GROUP
    SPREAD = ((2, 2), (2, 2), (0, 2, 2), (0, 2, 2))

    def sequence_steps(last):
        steps = []
        for c in range(CHUNKS + 2):
            group = c // TG + 1
            blocks = []
            if group <= (1 if last else GB):
                first = sum(len(x) for x in SPREAD[:c % TG])
                blocks = [(place, ("project", group, first + n)) for n, place in enumerate(SPREAD[c % TG])]
            parts = [[("A", c, None)] if c < CHUNKS else [],
                     ([("B", c - 1, None)] if 1 <= c <= CHUNKS else []) + ([("C", c - 2, None)] if c >= 2 else []),
                     ([("A_end", c, None)] if c < CHUNKS else []) + ([("C_end", c - 2, None)] if c >= 2 else [])]
            for place, part in enumerate(parts):
                steps += part + [e for at, e in blocks if at == place]
        return steps

    first_steps = [("project", 0, m) for m in range(IP)]
    PER = dict(conv=GB * XBC_BLOCKS, z=GB * Z_BLOCKS, chunk=CHUNKS)

    def place_of(e):
        return ("conv", e[1] * XBC_BLOCKS + e[2]) if e[2] < XBC_BLOCKS else ("z", e[1] * Z_BLOCKS + e[2] - XBC_BLOCKS)

    def with_banks(events):
        ring = [e for e in events if e[0] in ("project", "C")]
        assert len(ring) % 2 == 0
        at = {e: n for n, e in enumerate(ring)}
        users = [("C", e[1], None) if e[0] == "C_end" else e for e in events]
        return [(e, s.psum[:, 6 + at[user] % 2, :], ring[at[user] - 2] if at[user] >= 2 else None) if user in at
                else (e, None, None) for e, user in zip(events, users)]

    def sequences(engine, step, start=None):
        for e in with_banks(first_steps):
            step(0, *e)
        with engine.Fori(0, BATCH - 1) as b:
            if start:
                start(b)
            for e in with_banks(sequence_steps(False)):
                step(b, *e)
        if start:
            start(BATCH - 1)
        for e in with_banks(sequence_steps(True)):
            step(BATCH - 1, *e)

    def prep_vector(dve):
        dve.wait_ge(dma["small"][0], dma["small"][1])
        dve.wait_ge(s.consts_ready, CONSTS)
        dve.tensor_scalar(w["conv_w"][:, :, :], w["conv_w"][:, :, :], 0.5, None, ALU.mult)
        dve.tensor_scalar(w["conv_b"][:, :], w["conv_b"][:, :], 0.5, None, ALU.mult)
        for h in range(HEADS):
            g, at = h // REP, (h % 2) * HEAD
            dve.tensor_scalar(d_head[:, h // 2, at:at + HEAD], s.ident[:, g * HEAD:(g + 1) * HEAD], w["D"][:, h:h + 1],
                              None, ALU.mult)
        dve.wait_ge(*dma["w_out"])
        for k in range(Z_BLOCKS):
            last = dve.tensor_scalar(w["out_raw"][:, k, :], w["out_raw"][:, k, :], w["norm_w"][:, k:k + 1], 0.5,
                                     ALU.mult, ALU.mult)
        last.then_inc(done["prep"], 1)
        dve.wait_ge(*dma["in_split"])
        dve.wait_ge(*dma["out_split"])
        dve.wait_ge(done["decay_rate"], 1)
        dve.tensor_scalar(w["A_log"][:, :], w["A_log"][:, :], -1.0, None, ALU.mult)
        dve.wait_ge(done["dt_product"], 1)
        v, e, t, l = dt_v, dt_e, dt_t, dt_l
        product = s.psum[:, 0, 0:TILES * HEADS].rearrange("p (t h) -> p t h", h=HEADS)
        dve.tensor_tensor(v[:, :, :], product, w["dt_bias"][:, :].unsqueeze(1).to_broadcast([P, TILES, HEADS]),
                          ALU.add).then_inc(done["dt_biased"], 1)
        dve.wait_ge(done["dt_exp"], 1)
        dve.drain()
        dve.tensor_scalar(t[:, :, :], e[:, :, :], 1.0, None, ALU.add).then_inc(done["dt_log_in"], 1)
        dve.drain()
        dve.tensor_scalar(step_dt[:, :, :], t[:, :, :], -1.0, None, ALU.add)
        dve.drain()
        dve.tensor_tensor(e[:, :, :], e[:, :, :], step_dt[:, :, :], ALU.subtract)
        dve.reciprocal(step_da[:, :, :], t[:, :, :])
        dve.drain()
        dve.tensor_tensor(e[:, :, :], e[:, :, :], step_da[:, :, :], ALU.mult)
        dve.tensor_scalar(v[:, :, :], v[:, :, :], 0.0, None, ALU.max)
        dve.drain()
        dve.tensor_tensor(v[:, :, :], v[:, :, :], e[:, :, :], ALU.add)
        dve.drain()
        dve.wait_ge(done["dt_log"], 1)
        dve.tensor_tensor(step_dt[:, :, :], v[:, :, :], l[:, :, :], ALU.add)
        dve.drain()
        dve.tensor_tensor(step_da[:, :, :], step_dt[:, :, :], w["A_log"][:, :].unsqueeze(1).to_broadcast([P, TILES, HEADS]),
                          ALU.mult).then_inc(done["dt_done"], 1)
        dve.wait_ge(done["sums_ready"], 1)
        dve.tensor_scalar(minus_cum[:, :, :].rearrange("p t h -> p (t h)"), s.psum[:, 1, 0:TILES * HEADS], -1.0, None,
                          ALU.mult).then_inc(done["sums_copied"], 1)

    dt_v, dt_e, dt_t, dt_l = (mixed[:, 0, n, :].rearrange("p (t h) -> p t h", h=HEADS) for n in range(4))

    def prep_scalar(act):
        act.wait_ge(dma["small"][0], dma["small"][1])
        act.activation(w["A_log"][:, :], w["A_log"][:, :], ACT.Exp).then_inc(done["decay_rate"], 1)
        act.wait_ge(done["dt_biased"], 1)
        act.activation(dt_e[:, :, :], dt_v[:, :, :], ACT.Abs)
        act.drain()
        act.activation(dt_e[:, :, :], dt_e[:, :, :], ACT.Exp, scale=-1.0).then_inc(done["dt_exp"], 1)
        act.wait_ge(done["dt_log_in"], 1)
        act.activation(dt_l[:, :, :], dt_t[:, :, :], ACT.Ln).then_inc(done["dt_log"], 1)

    def prep_tensor(pe):
        for t in range(TILES):
            for k in range(KD):
                last = three_passes(pe, s.psum[:, 0, t * HEADS:(t + 1) * HEADS],
                                    pair_at(s.act, slice(None), k, slice(t * P, (t + 1) * P)),
                                    pair_at(w["in"], slice(None), k, slice(IP * P, IP * P + HEADS)), k == 0, k == KD - 1)
        last.then_inc(done["dt_product"], 1)
        pe.wait_ge(done["dt_done"], 1)
        pe.matmul(s.psum[:, 1, 0:TILES * HEADS], s.upper[:, :], step_da[:, :, :].rearrange("p t h -> p (t h)"),
                  start=True, stop=True).then_inc(done["sums_ready"], 1)

    def tensor(pe):
        pe.wait_ge(*dma["in_split"])
        pe.wait_ge(*dma["normed"])
        prep_tensor(pe)
        pe.wait_ge(*dma["out_split"])
        pe.wait_ge(done["sums_copied"], 1)
        pe.wait_ge(done["masks"], 4)

        def step(b, e, bank, old):
                kind, c, m = e
                n = CHUNKS * b + (c or 0)
                par = (c or 0) // TG % 2
                q = slice((c or 0) % TG * P, (c or 0) % TG * P + P)
                if kind in ("project", "C"):
                    if old is None and c != 0:
                        pe.wait_ge(done["out_done"], CHUNKS * b)
                        pe.wait_ge(done["gate_done"], PER["z"] * b + Z_BLOCKS)
                    elif old is None:
                        pass
                    elif old[0] == "C":
                        pe.wait_ge(done["out_done"], CHUNKS * b + old[1] + 1)
                    else:
                        what, at = place_of(old)
                        pe.wait_ge(done["evacuated"] if what == "conv" else done["gate_done"], PER[what] * b + at + 1)
                if kind == "project":
                    for k in range(KD):
                        last = three_passes(pe, bank, pair_at(w["in"], slice(None), k, slice(m * P, (m + 1) * P)),
                                            pair_at(s.act, slice(None), k, bass.ds(b * SEQ + c * GROUP, GROUP)),
                                            k == 0, k == KD - 1)
                    last.then_inc(done["projected"], 1)
                elif kind == "A":
                    pe.wait_ge(done["state_done"], n)
                    pe.wait_ge(done["conv_done"], PER["conv"] * b + XBC_BLOCKS * (par + 1))
                    pe.wait_ge(done["xdt"], n)
                    pe.wait_ge(done["b_copied"], n)
                    for k in range(2):
                        last = pe.transpose(s.psum[:, 4, k * P:(k + 1) * P], xbc[:, par, k, q], s.ident[:, :])
                    last.then_inc(done["turned"], 1)
                    pe.wait_ge(done["steps"], n + 1)
                    pe.wait_ge(done["leaves"], n)
                    for k in range(2):
                        last = pe.matmul(s.psum[:, k, :], s.ones[:, :],
                                         steps[:, REP * k:REP * (k + 1), :].rearrange("p h q -> p (h q)"),
                                         start=True, stop=True)
                    last.then_inc(done["rows_ready"], 1)
                    pe.wait_ge(done["mixed"], n)
                    for g in range(2):
                        rows = slice(g * STATE, (g + 1) * STATE)
                        last = pe.matmul(s.psum[:, 2 + g, :].rearrange("p (r q) -> p r q", r=REP), xbc[rows, par, 1, q],
                                         xbc[rows, par, 2:XBC_BLOCKS, q], start=True, stop=True)
                    last.then_inc(done["scores_ready"], 1)
                    pe.wait_ge(done["row_exp"], n + 1)
                    for k in range(2):
                        last = pe.matmul(s.psum[:, k, :].rearrange("p (r q) -> p r q", r=REP), ident_b[:, :],
                                         mask[:, :].unsqueeze(1).to_broadcast([P, REP, P]), start=False, stop=True,
                                         skip_group_check=True)
                    last.then_inc(done["masked"], 1)
                elif kind == "B":
                    pe.wait_ge(done["mixed"], n + 1)
                    pe.wait_ge(done["c_scaled"], n + 1)
                    pe.wait_ge(done["state_done"], n + 1)
                    pe.wait_ge(done["gated"], n)
                    for m in range(Z_BLOCKS):
                        y = s.psum[:, 5, m * P:(m + 1) * P]
                        pe.matmul(y, d_head[:, m, :], xbc[:, par, 0, q], start=True, stop=False, skip_group_check=True)
                        for j in range(2):
                            h = 2 * m + j
                            g, r = h // REP, h % REP
                            part = s.psum[j * HEAD:(j + 1) * HEAD, 5, m * P:(m + 1) * P]
                            rows = slice(g * STATE, (g + 1) * STATE)
                            if m == 2 and j == 0:
                                pe.wait_ge(done["lower_done"], n + 1)
                            pe.matmul(part, xdt[:, c % 2, h, :], mixed[:, c % 2, h, :], start=False, stop=False,
                                      skip_group_check=True)
                            last = pe.matmul(part, state[rows, r, :], c_scaled[rows, c % 2, r, :], start=False, stop=True,
                                             skip_group_check=True)
                        if m == 1:
                            last.then_inc(done["lower_done"], 1)
                    last.then_inc(done["y_ready"], 1)
                    pe.wait_ge(done["xdt_decayed"], n + 1)
                    if c + 1 < CHUNKS:
                        pe.wait_ge(done["xdt"], n + 2)
                        pe.wait_ge(done["b_copied"], n + 2)
                    for g in range(2):
                        rows = slice(g * STATE, (g + 1) * STATE)
                        last = pe.matmul(s.psum[rows, 4, 256:512], b_tok[:, c % 2, rows],
                                         xdt_decayed[:, REP * g:REP * (g + 1), :].rearrange("p h d -> p (h d)"),
                                         start=True, stop=True)
                    last.then_inc(done["state_ready"], 1)
                elif kind == "C":
                    pe.wait_ge(done["gated_lo"], n + 1)
                    for m in range(Z_BLOCKS):
                        three_passes(pe, bank[:, 0:D], pair_at((gated_hi, gated_lo), slice(None), m),
                                     pair_at(w["out"], slice(None), m), m == 0, m == Z_BLOCKS - 1)
                    pe.wait_ge(done["squares"], n + 1)
                    for m in range(Z_BLOCKS):
                        last = pe.matmul(bank[:, D:D + 1], squares[:, m, :], s.ones[:, 0:1], start=m == 0,
                                         stop=m == Z_BLOCKS - 1)
                    last.then_inc(done["out_ready"], 1)

        sequences(pe, step)

    def scalar(act):
        prep_scalar(act)

        def step(b, e, bank, old):
                kind, c, m = e
                n = CHUNKS * b + (c or 0)
                tile = b * CHUNKS + (c or 0)
                if kind == "project":
                    what, at = place_of(e)
                    count = PER[what] * b + at
                    act.wait_ge(done["projected"], (PER["conv"] + PER["z"]) * b + IP * c + m + 1)
                    if what == "conv":
                        act.wait_ge(done["conv_sum"], PER["conv"] * b + max(0, at + 1 - XBC_BLOCKS))
                        act.activation(conv_in[:, m, TAPS - 1:], bank, ACT.Copy).then_inc(done["evacuated"], 1)
                        if at % XBC_BLOCKS >= 1:
                            conv_tanh(act, b, at - 1)
                        if at % XBC_BLOCKS == XBC_BLOCKS - 1:
                            conv_tanh(act, b, at)
                    else:
                        act.wait_ge(done["gate_done"], PER["z"] * b + max(0, at - 1))
                        act.activation(gate_th[:, at % 2, :], bank, ACT.Tanh, scale=0.5).then_inc(done["gate_tanh"], 1)
                elif kind == "A":
                    act.wait_ge(done["rows_ready"], n + 1)
                    for g in range(2):
                        rows = slice(g * STATE, (g + 1) * STATE)
                        last = act.activation(row_exp[rows, c % 2, :, :].rearrange("p r q -> p (r q)"), s.psum[rows, g, :],
                                              ACT.Exp)
                    last.then_inc(done["row_exp"], 1)
                    act.wait_ge(done["masked"], n + 1)
                    for h in range(HEADS):
                        last = act.activation(decay[:, c % 2, h, :], s.psum[:, h // REP, h % REP * P:(h % REP + 1) * P],
                                              ACT.Exp, bias=minus_cum[:, tile, h:h + 1])
                    last.then_inc(done["leaves"], 1)
                    act.wait_ge(done["xdt"], n + 1)
                    act.activation(b_tok[:, c % 2, :], s.psum[:, 4, P:2 * P], ACT.Copy).then_inc(done["b_copied"], 1)
                elif kind == "B":
                    act.wait_ge(done["gated"], n + 1)
                    act.wait_ge(done["out_ready"], n)
                    act.activation(gated_hi[:, :, :], gated[:, :, :], ACT.Copy).then_inc(done["gated_hi"], 1)
                    act.activation(squares[:, :, :], gated[:, :, :], ACT.Square).then_inc(done["squares"], 1)

        sequences(act, step)

    gate_th = sb("gate_th", [P, 2, GROUP])

    def conv_tanh(act, b, at):
        act.wait_ge(done["conv_sum"], PER["conv"] * b + at + 1)
        act.wait_ge(done["conv_done"], PER["conv"] * b + max(0, at - 1))
        act.activation(conv_th[:, at % 2, :], conv_sum[:, at % 2, :], ACT.Tanh).then_inc(done["conv_tanh"], 1)

    def vector(dve):
        prep_vector(dve)
        dve.memset(conv_in[:, :, 0:TAPS - 1], 0.0)
        dve.drain()

        def start(b):
            dve.memset(state[:, :, :], 0.0).then_inc(done["state_done"], 1)

        def step(b, e, bank, old):
                kind, c, m = e
                n = CHUNKS * b + (c or 0)
                par = (c or 0) // TG % 2
                q = slice((c or 0) % TG * P, (c or 0) % TG * P + P)
                tile = b * CHUNKS + (c or 0)
                dve.drain()
                if kind == "project":
                    what, at = place_of(e)
                    if what == "conv":
                        dve.wait_ge(done["evacuated"], PER["conv"] * b + at + 1)
                        acc = conv_sum[:, at % 2, :]
                        dve.tensor_scalar(acc, conv_in[:, m, 0:GROUP], w["conv_w"][:, m, 0:1], w["conv_b"][:, m:m + 1],
                                          ALU.mult, ALU.add)
                        for k in range(1, TAPS):
                            dve.drain()
                            last = dve.scalar_tensor_tensor(acc, conv_in[:, m, k:k + GROUP], w["conv_w"][:, m, k:k + 1], acc,
                                                            ALU.mult, ALU.add)
                        dve.drain()
                        if c % GB == GB - 1:
                            dve.memset(conv_in[:, m, 0:TAPS - 1], 0.0).then_inc(done["conv_sum"], 1)
                        else:
                            dve.tensor_copy(conv_in[:, m, 0:TAPS - 1],
                                            conv_in[:, m, GROUP:GROUP + TAPS - 1]).then_inc(done["conv_sum"], 1)
                        if at % XBC_BLOCKS >= 1:
                            conv_end(dve, b, c, at - 1)
                        if at % XBC_BLOCKS == XBC_BLOCKS - 1:
                            conv_end(dve, b, c, at)
                    else:
                        dve.wait_ge(done["gate_tanh"], PER["z"] * b + at + 1)
                        dve.scalar_tensor_tensor(zs[:, c % 2, m - XBC_BLOCKS, :], gate_th[:, at % 2, :], 1.0, bank,
                                                 ALU.add, ALU.mult).then_inc(done["gate_done"], 1)
                elif kind == "A":
                    dve.wait_ge(done["turned"], n + 1)
                    dve.tensor_tensor(xdt[:, c % 2, :, :].rearrange("p (g r) d -> p g r d", g=2),
                                      s.psum[:, 4, 0:P].rearrange("p (g d) -> p g d", g=2).unsqueeze(2).to_broadcast([P, 2, REP, HEAD]),
                                      step_dt[:, tile, :].rearrange("p (g r) -> p g r", g=2).unsqueeze(3).to_broadcast([P, 2, REP, HEAD]),
                                      ALU.mult).then_inc(done["xdt"], 1)
                elif kind == "A_end":
                    dve.wait_ge(done["leaves"], n + 1)
                    dve.wait_ge(done["scores_ready"], n + 1)
                    dve.tensor_tensor(mixed[:, c % 2, :, :], decay[:, c % 2, :, :],
                                      s.psum[:, 2:4, :].rearrange("p k (r q) -> p (k r) q", r=REP), ALU.mult).then_inc(done["mixed"], 1)
                elif kind == "B":
                    dve.wait_ge(done["y_ready"], n + 1)
                    if c < CHUNKS - 1:
                        dve.tensor_tensor(state[:, :, :], state[:, :, :],
                                          row_exp[:, c % 2, :, P - 1:P].to_broadcast([P, REP, HEAD]), ALU.mult)
                        dve.drain()
                        dve.wait_ge(done["state_ready"], n + 1)
                        dve.tensor_tensor(state[:, :, :], state[:, :, :],
                                          s.psum[:, 4, 256:512].rearrange("p (r d) -> p r d", r=REP),
                                          ALU.add).then_inc(done["state_done"], 1)
                    dve.wait_ge(done["gated_lo"], n)
                    dve.wait_ge(done["squares"], n)
                    dve.tensor_tensor(gated[:, :, :], zs[:, par, :, q],
                                      s.psum[:, 5, :].rearrange("p (m q) -> p m q", q=P), ALU.mult).then_inc(done["gated"], 1)
                elif kind == "C":
                    dve.wait_ge(done["out_ready"], n + 1)
                    dve.tensor_scalar(out_var[:, :], bank[:, D:D + 1], 0.25 / INNER, EPS, ALU.mult,
                                      ALU.add).then_inc(done["out_var"], 1)
                elif kind == "C_end":
                    dve.wait_ge(done["out_root"], n + 1)
                    dve.scalar_tensor_tensor(u[:, tile, :], bank[:, 0:D], out_root[:, 0:1], u[:, tile, :], ALU.mult,
                                             ALU.add).then_inc(done["out_done"], 1)

        sequences(dve, step, start)

    def conv_end(dve, b, c, at):
        if c >= 1:
            dve.wait_ge(done["y_ready"], CHUNKS * b + (c - 1) * TG)
        dve.wait_ge(done["conv_tanh"], PER["conv"] * b + at + 1)
        dve.scalar_tensor_tensor(xbc[:, c % 2, at % XBC_BLOCKS, :], conv_th[:, at % 2, :], 1.0, conv_sum[:, at % 2, :],
                                 ALU.add, ALU.mult).then_inc(done["conv_done"], 1)

    def gpsimd(pool):
        pool.memset(ident_b[:, :], 0.0).then_inc(done["masks"], 1)
        pool.memset(mask[:, :], 0.0).then_inc(done["masks"], 1)
        pool.wait_ge(done["masks"], 2)
        pool.affine_select(out=ident_b[:, :], in_=ident_b[:, :], compare_op=ALU.not_equal, fill=1.0, base=0,
                           pattern=[[-1, P]], channel_multiplier=1).then_inc(done["masks"], 1)
        pool.affine_select(out=mask[:, :], in_=mask[:, :], compare_op=ALU.is_ge, fill=MASKED, base=0,
                           pattern=[[1, P]], channel_multiplier=-1).then_inc(done["masks"], 1)
        pool.wait_ge(done["dt_done"], 1)
        with pool.Fori(0, BATCH) as b:
            for c in range(-1, CHUNKS + 2):
                n = CHUNKS * b + c
                tile = b * CHUNKS + c
                if 0 <= c < CHUNKS:
                    par, q = c // TG, slice(c % TG * P, c % TG * P + P)
                    pool.wait_ge(done["row_exp"], n + 1)
                    pool.tensor_tensor(c_scaled[:, c % 2, :, :], xbc[:, par, 2:XBC_BLOCKS, q], row_exp[:, c % 2, :, :],
                                       ALU.mult).then_inc(done["c_scaled"], 1)
                if c + 1 < CHUNKS:
                    pool.wait_ge(done["rows_ready"], n + 1)
                    pool.tensor_tensor(steps[:, :, :], s.upper[:, :].unsqueeze(1).to_broadcast([P, HEADS, P]),
                                       step_da[:, tile + 1, :].unsqueeze(2).to_broadcast([P, HEADS, P]),
                                       ALU.mult).then_inc(done["steps"], 1)
                if 0 <= c < CHUNKS:
                    pool.wait_ge(done["leaves"], n + 1)
                    pool.wait_ge(done["state_ready"], n)
                    pool.wait_ge(done["xdt"], n + 1)
                    pool.tensor_tensor(xdt_decayed[:, :, :], xdt[:, c % 2, :, :],
                                       decay[:, c % 2, :, P - 1:P].to_broadcast([P, HEADS, HEAD]),
                                       ALU.mult).then_inc(done["xdt_decayed"], 1)
                if c >= 2:
                    pool.wait_ge(done["out_var"], n - 1)
                    pool.tensor_tensor(out_root[:, :], out_var[:, :], s.minus_half[:, 0:1], ALU.pow).then_inc(done["out_root"], 1)
                if 1 <= c <= CHUNKS:
                    pool.wait_ge(done["gated_hi"], n)
                    pool.tensor_tensor(gated_lo[:, :, :], gated[:, :, :], gated_hi[:, :, :].bitcast(F32),
                                       ALU.subtract).then_inc(done["gated_lo"], 1)

    return dict(vector=vector, scalar=scalar, gpsimd=gpsimd, tensor=tensor, done=(done["out_done"], TILES), prep=(done["prep"], 1))


class Counts:

    def __init__(self):
        self.base, self.per, self.i = {}, {}, None

    def at(self, kind, n):
        value = self.base.get(kind, 0) + n
        return value if self.i is None else self.i * self.per.get(kind, 0) + value

    def passed(self, counts, turns=1):
        for kind, n in counts.items():
            self.base[kind] = self.base.get(kind, 0) + n * turns


def attention_stage(nc, sems, mem, s, a, before, norm):

    def sem(what):
        return sems.enter_context(nc.semaphore(f"attn_{what}"))

    def sb(what, shape, dt=F32):
        return mem.enter_context(nc.sbuf_tensor(f"attn_{what}", shape, dt))

    def pair(what, shape):
        return sb(f"{what}_hi", shape, F32R), sb(f"{what}_lo", shape, F32R)

    q, k, v = pair("q", [P, 2, SEQ]), pair("k", [P, 2, SEQ]), pair("v", [P, QT, 2 * AE])
    z, pt = pair("z", [P, 2, SEQ]), pair("pt", [P, 3, GROUP])
    probs = [[sb(f"probs_{h}_{g}", [P, TG, (g + 1) * GROUP]) for g in range(2)] for h in range(2)]
    qkv_raw, wo_raw = sb("qkv_raw", [P, 3, KD, 2, AE]), sb("wo_raw", [P, 2, D])
    qkv, wo = pair("qkv", [P, 3, KD, 2, AE]), pair("wo", [P, 2, D])
    bias = sb("bias", [P, 3, AH])
    b_out = sb("b_out", [P, D])
    ident_b, mask = sb("ident_b", [P, P], BF16), sb("mask", [P, P], BF16)
    neg_max, sums, inverse = (sb(n, [P, 2 * QT]) for n in ("neg_max", "sums", "inverse"))

    small_loaded, qkv_loaded, wo_loaded, masks_ready = (
        sem(n) for n in ("small_loaded", "qkv_loaded", "wo_loaded", "masks_ready"))
    w_hi, w_split = sem("w_hi"), sem("w_split")
    work_ready, work_hi, work_done = sem("work_ready"), sem("work_hi"), sem("work_done")
    scores_ready, max_ready, max_taken, exp_done, inverse_ready, probs_ready = (
        sem(n) for n in ("scores_ready", "max_ready", "max_taken", "exp_done", "inverse_ready", "probs_ready"))
    summed = sem("summed")
    z_hi, z_done = sem("z_hi"), sem("z_done")
    Q, K, V = range(3)
    HALF = SEQ // GROUP
    QKV_LOADS = 3 * KD

    def section(kind):
        events, n = [], dict(work=0, hi=0, tile=0, pt=0, z=0, w=0, qkv=0, wo=0)

        def add(what, counted, **at):
            e = dict(what=what, **at)
            for c in counted:
                e[c] = n[c]
                n[c] += 1
            events.append(e)
            return e

        def project(h):
            return [lambda m=m, half=half: add("project", ("work", "hi"), m=m, h=h, half=half)
                    for m in (Q, K) for half in range(HALF)]

        def values():
            for t in range(QT // 2):
                add("values", ("work", "hi"), t=t)

        def score(h, t, need):
            return add("score", ("tile",), h=h, t=t, need=need)

        if kind == "first":
            n["qkv"] += 1
            for m in (Q, K, V):
                add("split", ("w",), m=m)
            for h in range(2):
                for p in project(h):
                    p()
            need = n["work"]
            values()
            late = None
            for t in range(QT):
                e = score(0, t, need)
                events.append(dict(e, what="exp"))
                if late:
                    events.append(dict(late, what="invert"))
                late = e
            events.append(dict(late, what="invert"))
        else:
            last = kind == "last"
            n["qkv"], n["wo"] = (0 if last else 1), 1
            chunks = [(h, g, j) for h in range(2) for g in range(2) for j in range(TG * (g + 1))]
            half = len(chunks) // 2
            score_at = {0: 0, 2: 1, 3: 2, 5: 3, 6: 4, 8: 5, 9: 6, 11: 7}
            project_at = (3, 5, 8, 10)
            norm_at = {0: ("stats", 0), 2: ("apply", 0), 4: ("turn", 0), 6: ("stats", 1), 8: ("apply", 1), 10: ("turn", 1)}
            splits = {1: 3} if last else {0: Q, 1: K, 2: V, 3: 3}
            turned, late, need = [], None, 0

            def turn(c):
                h, g, j = chunks[c]
                turned.append(add("turn", ("work", "hi", "pt"), h=h, g=g, j=j))

            turn(0)
            turn(1)
            for c, (h, g, j) in enumerate(chunks):
                if late:
                    events.append(dict(late, what="invert"))
                    late = None
                e = None
                if c % half in score_at and not (last and h == 1):
                    e = score(1 - h, score_at[c % half], need)
                if c in splits:
                    add("split", ("w",), m=splits[c])
                if c + 2 < len(chunks):
                    turn(c + 2)
                if last and c - half in norm_at:
                    step, group = norm_at[c - half]
                    events.append(dict(what="norm", step=step, group=group))
                events.append(dict(turned[c], what="sum"))
                if j == TG * (g + 1) - 1:
                    add("gather", ("z",), h=h, g=g)
                if e:
                    events.append(dict(e, what="exp"))
                    late = e
                if c % half in project_at and not last:
                    project(h)[project_at.index(c % half)]()
                    if c == half - 1:
                        need = n["work"]
            if late:
                events.append(dict(late, what="invert"))
            if not last:
                values()
            for t in range(QT // 2):
                add("output", ("work",), t=t)
        return events, n

    sections = {kind: section(kind) for kind in ("first", "body", "last")}

    def sections_of(engine, handle):
        counts = Counts()
        for b in range(BATCH):
            for kind in ("first", "body", "last"):
                events, n = sections[kind]
                if kind == "body":
                    with engine.Fori(0, PAIRS - 1) as i:
                        counts.i, counts.per = i, n
                        for e in events:
                            handle(e, counts, b, kind, i)
                    counts.i = None
                    counts.passed(n, PAIRS - 1)
                else:
                    for e in events:
                        handle(e, counts, b, kind, 0 if kind == "first" else PAIRS - 1)
                    counts.passed(n)

    def norm_group(e, b):
        return HALF * (b + 1) + e["group"]

    def work_bank(e):
        return 4 + e["work"] % 3

    def first_column(e):
        return max(0, e["j"] - TG * e["g"]) * P

    def score_view(e):
        width = (e["t"] + 1) * P
        slot = 2 * (e["t"] % 2)
        return s.psum[:, slot:slot + 2, :].rearrange("p b c -> p (b c)")[:, 0:width]

    def probs_view(e):
        return probs[e["h"]][e["t"] // TG][:, e["t"] % TG, 0:(e["t"] + 1) * P]

    def stat(tensor, e):
        at = e["h"] * QT + e["t"]
        return tensor[:, at:at + 1]

    def bias_of(e, i, kind):
        if e["what"] == "gather":
            return bias[:, V, bass.ds(i * 2 + e["h"], 1)]
        return bias[:, e["m"], bass.ds(i * 2 + e["h"] + (0 if kind == "first" else 2), 1)]

    def raw_and_split(m):
        if m == 3:
            return wo_raw[:, :, :], wo[0][:, :, :], wo[1][:, :, :]
        return (t[:, m, :, :, :].rearrange("p k h e -> p (k h e)") for t in (qkv_raw, *qkv))

    def destination(e):
        if e["what"] == "project":
            return pair_at((q, k)[e["m"]], slice(None), e["h"], slice(e["half"] * GROUP, (e["half"] + 1) * GROUP))
        if e["what"] == "values":
            return tuple(t[:, 2 * e["t"]:2 * e["t"] + 2, :].rearrange("p t c -> p (t c)") for t in v)
        return pair_at(pt, slice(None), e["pt"] % 3, slice(first_column(e), GROUP))

    def work_view(e):
        return s.psum[:, work_bank(e), (first_column(e) if e["what"] == "turn" else 0):]

    def sync(sp):
        sp.wait_ge(*before)
        with nc.allow_non_contiguous_dma(reason="biases, one element for each partition"):
            for n, name in enumerate("QKV"):
                sp.dma_start(bias[:, n, :], a[f"L1_attn_b_{name}"].rearrange("h e -> e h")).then_inc(small_loaded, 16)
        sp.dma_start(b_out[:, :], a["L1_attn_b_O"].partition_broadcast(P)).then_inc(small_loaded, 16)
        counts = Counts()

        def load_qkv(at):
            sp.wait_ge(w_split, counts.at("w", 0))
            for m, name in enumerate("QKV"):
                for c in range(KD):
                    sp.dma_start(qkv_raw[:, m, c, :, :],
                                 a[f"L1_attn_W_{name}"][bass.ds(at * 2, 2), c * P:(c + 1) * P, :].rearrange("h p e -> p h e")
                                 ).then_inc(qkv_loaded, 16)

        def load_wo(at):
            sp.wait_ge(w_split, counts.at("w", 0))
            sp.dma_start(wo_raw[:, :, :], a["L1_attn_W_O"][bass.ds(at * 2, 2), :, :].rearrange("h e d -> e h d")
                         ).then_inc(wo_loaded, 16)

        for b in range(BATCH):
            load_qkv(0)
            counts.passed(sections["first"][1])
            with sp.Fori(0, PAIRS - 1) as i:
                counts.i, counts.per = i, sections["body"][1]
                load_qkv(i + 1)
                load_wo(i)
            counts.i = None
            counts.passed(sections["body"][1], PAIRS - 1)
            load_wo(PAIRS - 1)
            counts.passed(sections["last"][1])

    def tensor(pe):
        pe.wait_ge(*before)
        pe.wait_ge(masks_ready, 4)
        pe.sem_inc(summed, 2)

        def handle(e, counts, b, kind, i):
            what = e["what"]
            if what == "norm" and e["step"] == "turn":
                pe.wait_ge(exp_done, counts.at("tile", QT))
                norm["turn"](pe, norm_group(e, b))
            if what in ("project", "values"):
                pe.wait_ge(*norm["ready"](HALF * b + HALF - 1))
            if what in ("project", "values", "turn", "output"):
                pe.wait_ge(work_done, counts.at("work", max(0, e["work"] - 2)))
            if what in ("project", "values"):
                pe.wait_ge(w_split, counts.at("w", (V if what == "values" else e["m"]) + 1))
            if what == "project":
                tokens = slice(b * SEQ + e["half"] * GROUP, b * SEQ + (e["half"] + 1) * GROUP)
                for c in range(KD):
                    last = three_passes(pe, s.psum[:, work_bank(e), :], pair_at(qkv, slice(None), e["m"], c, e["h"]),
                                        pair_at(s.act, slice(None), c, tokens), c == 0, c == KD - 1)
                last.then_inc(work_ready, 1)
            elif what == "values":
                for t in range(2):
                    tokens = slice(b * SEQ + (2 * e["t"] + t) * P, b * SEQ + (2 * e["t"] + t + 1) * P)
                    for c in range(KD):
                        w_hi_lo = tuple(x[:, V, c, :, :].rearrange("p h e -> p (h e)") for x in qkv)
                        last = three_passes(pe, s.psum[:, work_bank(e), t * 2 * AE:(t + 1) * 2 * AE],
                                            pair_at(s.act, slice(None), c, tokens), w_hi_lo, c == 0, c == KD - 1)
                last.then_inc(work_ready, 1)
            elif what == "score":
                pe.wait_ge(work_done, counts.at("work", e["need"]))
                ahead = max(0, e["tile"] - 1) if kind == "first" else e["tile"] - 1
                pe.wait_ge(exp_done, counts.at("tile", ahead))
                t, view = e["t"], score_view(e)
                queries = pair_at(q, slice(None), e["h"], slice(t * P, (t + 1) * P))
                for at in range(0, (t + 1) * P, GROUP):
                    end = min(at + GROUP, (t + 1) * P)
                    (q_hi, q_lo), (k_hi, k_lo) = queries, pair_at(k, slice(None), e["h"], slice(at, end))
                    pe.matmul(view[:, at:end], q_hi, k_hi, start=True, stop=False)
                    if end == (t + 1) * P:
                        pe.matmul(view[:, t * P:], ident_b[:, :], mask[:, :], start=False, stop=False)
                    pe.matmul(view[:, at:end], q_hi, k_lo, start=False, stop=False)
                    last = pe.matmul(view[:, at:end], q_lo, k_hi, start=False, stop=True)
                last.then_inc(scores_ready, 1)
            elif what == "turn":
                tile = TG * (e["g"] + 1)
                ready = counts.at("tile", tile - QT) if e["h"] == 0 else counts.at("tile", tile)
                pe.wait_ge(probs_ready, ready)
                for lq in range(first_column(e) // P, TG):
                    last = pe.transpose(s.psum[:, work_bank(e), lq * P:(lq + 1) * P],
                                        probs[e["h"]][e["g"]][:, lq, e["j"] * P:(e["j"] + 1) * P], s.ident[:, :])
                last.then_inc(work_ready, 1)
            elif what == "sum":
                pe.wait_ge(work_done, counts.at("work", e["work"] + 1))
                j = e["j"]
                if j == 0:
                    pe.wait_ge(z_done, counts.at("z", 2 * e["h"] + e["g"]))
                at = first_column(e)
                v_hi, v_lo = pair_at(v, slice(None), j, slice(e["h"] * AE, (e["h"] + 1) * AE))
                p_hi, p_lo = pair_at(pt, slice(None), e["pt"] % 3)
                pe.matmul(s.psum[:, 7, at:], v_hi, p_hi[:, at:], start=j == 0, stop=False, skip_group_check=True)
                pe.matmul(s.psum[:, 7, at:], v_hi, p_lo[:, at:], start=False, stop=False, skip_group_check=True)
                ends = at + P if j >= TG * e["g"] else at
                if ends > at:
                    last = pe.matmul(s.psum[:, 7, at:ends], v_lo, p_hi[:, at:ends], start=False, stop=True,
                                     skip_group_check=True)
                if ends < GROUP:
                    last = pe.matmul(s.psum[:, 7, ends:], v_lo, p_hi[:, ends:], start=False, stop=False, skip_group_check=True)
                last.then_inc(summed, 1)
            elif what == "output":
                pe.wait_ge(z_done, counts.at("z", 4))
                pe.wait_ge(w_split, counts.at("w", 1 if kind == "last" else 4))
                for t in range(2):
                    tokens = slice((2 * e["t"] + t) * P, (2 * e["t"] + t + 1) * P)
                    for h in range(2):
                        last = three_passes(pe, s.psum[:, work_bank(e), t * D:(t + 1) * D],
                                            pair_at(z, slice(None), h, tokens), pair_at(wo, slice(None), h), h == 0, h == 1)
                last.then_inc(work_ready, 1)

        sections_of(pe, handle)

    def scalar(act):
        act.wait_ge(*before)
        act.wait_ge(small_loaded, 64)

        def handle(e, counts, b, kind, i):
            what = e["what"]
            if what == "split":
                raw, hi, _ = raw_and_split(e["m"])
                if e["m"] == 3:
                    act.wait_ge(wo_loaded, 16 * (counts.at("wo", 1)))
                else:
                    act.wait_ge(qkv_loaded, 16 * QKV_LOADS * (counts.at("qkv", 1)))
                act.wait_ge(work_ready, counts.at("work", 0))
                act.activation(hi, raw, ACT.Copy).then_inc(w_hi, 1)
            elif what in ("project", "values", "turn"):
                act.wait_ge(work_ready, counts.at("work", e["work"] + 1))
                if what == "turn":
                    act.wait_ge(summed, counts.at("pt", e["pt"]))
                if what == "project":
                    act.sem_inc(s.wait_over, 1)
                    act.activation(destination(e)[0], work_view(e), ACT.Identity, bias=bias_of(e, i, kind)).then_inc(work_hi, 1)
                else:
                    act.activation(destination(e)[0], work_view(e), ACT.Copy).then_inc(work_hi, 1)
            elif what == "norm" and e["step"] == "turn":
                norm["high"](act, norm_group(e, b))
            elif what == "exp":
                act.wait_ge(max_ready, counts.at("tile", e["tile"] + 1))
                act.activation(probs_view(e), score_view(e), ACT.Exp, bias=stat(neg_max, e), scale=SCORE_SCALE,
                               accum_out=stat(sums, e)).then_inc(exp_done, 1)
            elif what == "gather":
                act.wait_ge(summed, 2 + counts.at("pt", group_end(e)))
                act.sem_inc(s.wait_over, 1)
                act.activation(z[0][:, e["h"], e["g"] * GROUP:(e["g"] + 1) * GROUP], s.psum[:, 7, :], ACT.Identity,
                               bias=bias_of(e, i, kind)).then_inc(z_hi, 1)

        sections_of(act, handle)

    def group_end(e):
        return e["h"] * 3 * TG + (TG if e["g"] == 0 else 3 * TG)

    def vector(dve):
        dve.wait_ge(*before)
        dve.wait_ge(small_loaded, 64)

        def add_bias(b):
            dve.drain()
            x = s.x[:, b * QT:(b + 1) * QT, :]
            dve.tensor_tensor(x, x, b_out[:, :].unsqueeze(1).to_broadcast([P, QT, D]), ALU.add)
            dve.drain()

        add_bias(0)

        def handle(e, counts, b, kind, i):
            what = e["what"]
            if what in ("project", "values", "turn"):
                dve.wait_ge(work_hi, counts.at("hi", e["hi"] + 1))
                hi, lo = destination(e)
                if what == "project":
                    dve.scalar_tensor_tensor(lo, work_view(e), bias_of(e, i, kind), hi.bitcast(F32), ALU.add,
                                             ALU.subtract).then_inc(work_done, 1)
                else:
                    dve.tensor_tensor(lo, work_view(e), hi.bitcast(F32), ALU.subtract).then_inc(work_done, 1)
            elif what == "score":
                dve.wait_ge(scores_ready, counts.at("tile", e["tile"] + 1))
                dve.tensor_reduce(stat(neg_max, e), score_view(e), AX_X, ALU.max, negate=True)
                dve.drain()
                dve.tensor_scalar(stat(neg_max, e), stat(neg_max, e), SCORE_SCALE, None, ALU.mult).then_inc(max_ready, 1)
            elif what == "invert":
                dve.wait_ge(exp_done, counts.at("tile", e["tile"] + 1))
                dve.reciprocal(stat(inverse, e), stat(sums, e)).then_inc(inverse_ready, 1)
            elif what == "gather":
                dve.wait_ge(z_hi, counts.at("z", e["z"] + 1))
                hi, lo = pair_at(z, slice(None), e["h"], slice(e["g"] * GROUP, (e["g"] + 1) * GROUP))
                dve.scalar_tensor_tensor(lo, s.psum[:, 7, :], bias_of(e, i, kind), hi.bitcast(F32), ALU.add,
                                         ALU.subtract).then_inc(z_done, 1)
            elif what == "output":
                dve.wait_ge(work_ready, counts.at("work", e["work"] + 1))
                x = s.x[:, b * QT + 2 * e["t"]:b * QT + 2 * e["t"] + 2, :].rearrange("p t d -> p (t d)")
                dve.tensor_tensor(x, x, s.psum[:, work_bank(e), :], ALU.add).then_inc(work_done, 1)
            elif what == "norm":
                group = norm_group(e, b)
                norm[{"stats": "stats", "apply": "apply", "turn": "low"}[e["step"]]](dve, group)
                if group == GROUPS - 1 and e["step"] == "apply":
                    add_bias(1)

        sections_of(dve, handle)

    def gpsimd(pool):
        pool.wait_ge(*before)
        pool.memset(ident_b[:, :], 0.0).then_inc(masks_ready, 1)
        pool.memset(mask[:, :], 0.0).then_inc(masks_ready, 1)
        pool.wait_ge(masks_ready, 2)
        pool.affine_select(out=ident_b[:, :], in_=ident_b[:, :], compare_op=ALU.not_equal, fill=1.0, base=0,
                           pattern=[[-1, P]], channel_multiplier=1).then_inc(masks_ready, 1)
        pool.affine_select(out=mask[:, :], in_=mask[:, :], compare_op=ALU.is_ge, fill=MASKED, base=0,
                           pattern=[[-1, P]], channel_multiplier=1).then_inc(masks_ready, 1)

        def handle(e, counts, b, kind, i):
            if e["what"] == "split":
                raw, hi, lo = raw_and_split(e["m"])
                pool.wait_ge(w_hi, counts.at("w", e["w"] + 1))
                pool.tensor_tensor(lo, raw, hi.bitcast(F32), ALU.subtract).then_inc(w_split, 1)
            elif e["what"] == "norm" and e["step"] == "stats":
                norm["roots"](pool, norm_group(e, b))
            elif e["what"] == "invert":
                pool.wait_ge(inverse_ready, counts.at("tile", e["tile"] + 1))
                pool.sem_inc(s.wait_over, 1)
                pool.tensor_scalar(probs_view(e), probs_view(e), stat(inverse, e), 1.0, ALU.mult,
                                   ALU.mult).then_inc(probs_ready, 1)

        sections_of(pool, handle)

    n = sections
    total = BATCH * (n["first"][1]["work"] + (PAIRS - 1) * n["body"][1]["work"] + n["last"][1]["work"])
    return dict(sync=sync, tensor=tensor, scalar=scalar, vector=vector, gpsimd=gpsimd, done=(work_done, total))


def moe_stage(nc, sems, mem, s, a, before, normed):

    def sem(what):
        return sems.enter_context(nc.semaphore(f"moe_{what}"))

    def sb(what, shape, dt=F32):
        return mem.enter_context(nc.sbuf_tensor(f"moe_{what}", shape, dt))

    def pair(what, shape):
        return sb(f"{what}_hi", shape, F32R), sb(f"{what}_lo", shape, F32R)

    BLOCKS = EI // P
    SIDES = 2
    router_raw, router = sb("router_raw", [P, KD, EXPERTS]), pair("router", [P, KD, EXPERTS])
    router_b, down_b = sb("router_b", [P, EXPERTS]), sb("down_b", [EXPERTS, D])
    gu_b, up_b = sb("gu_b", [P, EXPERTS, BLOCKS, SIDES]), sb("up_b", [P, EXPERTS, BLOCKS])
    logits, work, first, second = (sb(n, [P, TILES, EXPERTS]) for n in ("logits", "work", "first", "second"))
    scan = [sb(f"scan_{n}", [P, TILES, EXPERTS]) for n in range(2)]
    best = [sb(f"best_{n}", [P, TILES]) for n in range(2)]
    ratio, share = sb("ratio", [P, TILES]), sb("share", [P, TILES])
    scores = sb("scores", [P, TILES, EXPERTS])
    scores_t = sb("scores_t", [EXPERTS, TILES, P])
    gu_raw, down_raw = sb("gu_raw", [P, 2, KD, SIDES * EI]), sb("down_raw", [P, 2, BLOCKS, D])
    gu, down = pair("gu", [P, 2, KD, SIDES, EI]), pair("down", [P, 2, BLOCKS, D])
    gate, up, th, glu, hidden = (sb(n, [P, 2, GROUP]) for n in ("gate", "up", "th", "glu", "hidden"))
    hid = pair("hid", [P, 2, BLOCKS, GROUP])

    small_loaded, logits_ready, ratio_in, ratio_ready, scores_ready = (
        sem(n) for n in ("small_loaded", "logits_ready", "ratio_in", "ratio_ready", "scores_ready"))
    router_hi, router_split, turned, copied, bias_ready, bias_added = (
        sem(n) for n in ("router_hi", "router_split", "turned", "copied", "bias_ready", "bias_added"))
    raw_loaded = [sem(f"raw_loaded_{n}") for n in range(2)]
    w_scaled, w_hi, w_split = sem("w_scaled"), sem("w_hi"), sem("w_split")
    products, gate_ready, bounded, th_ready, hidden_done, hid_hi, hid_split, down_ready, added = (
        sem(n) for n in ("products", "gate_ready", "bounded", "th_ready", "hidden_done", "hid_hi", "hid_split",
                         "down_ready", "added"))
    PIECES = KD + 1
    UNITS = 2 * GROUPS

    def sync(sp):
        sp.wait_ge(*before)
        with nc.allow_non_contiguous_dma(reason="router weights and biases by partition"):
            for c in range(KD):
                sp.dma_start(router_raw[:, c, :], a["L1_ffn_router_weight"][:, c * P:(c + 1) * P].rearrange("e p -> p e")
                             ).then_inc(small_loaded, 16)
            for e in range(EXPERTS):
                for m in range(BLOCKS):
                    sp.dma_start(gu_b[:, e, m, :],
                                 a["L1_ffn_gate_up_proj_bias"][e, m * P * SIDES:(m + 1) * P * SIDES].rearrange("(p s) -> p s", s=SIDES)
                                 ).then_inc(small_loaded, 16)
        sp.dma_start(router_b[:, :], a["L1_ffn_router_bias"].partition_broadcast(P)).then_inc(small_loaded, 16)
        sp.dma_start(down_b[:, :], a["L1_ffn_down_proj_bias"]).then_inc(small_loaded, 16)

        def load(slot, expert):
            sp.dma_start(gu_raw[:, slot, :, :], a["L1_ffn_gate_up_proj"][bass.ds(expert, 1), :, :].rearrange(
                "e (k p) n -> p (e k) n", p=P)).then_inc(raw_loaded[slot], 16)
            sp.dma_start(down_raw[:, slot, :, :], a["L1_ffn_down_proj"][bass.ds(expert, 1), :, :].rearrange(
                "e (k p) n -> p (e k) n", p=P)).then_inc(raw_loaded[slot], 16)

        load(0, 0)
        load(1, 1)
        with sp.Fori(0, EXPERTS // 2 - 1) as i:
            sp.wait_ge(w_split, PIECES * (2 * i + 1))
            load(0, 2 * i + 2)
            sp.wait_ge(w_split, PIECES * (2 * i + 2))
            load(1, 2 * i + 3)

    def tensor(pe):
        pe.wait_ge(*normed)
        pe.wait_ge(router_split, 1)
        for t in range(TILES):
            for c in range(KD):
                last = three_passes(pe, s.psum[:, 2, t * EXPERTS:(t + 1) * EXPERTS],
                                    pair_at(s.act, slice(None), c, slice(t * P, (t + 1) * P)), pair_at(router, slice(None), c),
                                    c == 0, c == KD - 1)
        last.then_inc(logits_ready, 1)
        pe.wait_ge(scores_ready, 1)
        for t in range(0, TILES, 4):
            if t:
                pe.wait_ge(copied, t // 4)
            for n in range(4):
                last = pe.transpose(s.psum[0:EXPERTS, 3, n * P:(n + 1) * P], scores[:, t + n, :], s.ident[:, :])
            last.then_inc(turned, 1)
        pe.wait_ge(copied, TILES // 4)
        for t in range(0, TILES, 2):
            if t >= 4:
                pe.wait_ge(bias_added, t // 2 - 1)
            for n in range(2):
                last = pe.matmul(s.psum[:, 4 + t // 2 % 2, n * D:(n + 1) * D], scores_t[:, t + n, :], down_b[:, :],
                                 start=True, stop=True)
            last.then_inc(bias_ready, 1)
        pe.wait_ge(bias_added, TILES // 2)
        pe.sem_inc(hidden_done, 2)

        def turn(counts, last):
            def gate_up(u):
                slot, g = u // GROUPS, u % GROUPS
                if g == 0:
                    pe.wait_ge(w_split, counts.at("w", PIECES * (slot + 1)))
                for m in range(BLOCKS):
                    n = u * BLOCKS + m
                    pe.wait_ge(bounded, counts.at("block", n + 1))
                    for side in range(SIDES):
                        for c in range(KD):
                            last = three_passes(pe, s.psum[:, 2 * (n % 2) + side, :],
                                                pair_at(gu, slice(None), slot, c, side, slice(m * P, (m + 1) * P)),
                                                pair_at(s.act, slice(None), c, slice(g * GROUP, (g + 1) * GROUP)),
                                                c == 0, c == KD - 1)
                    last.then_inc(products, 1)

            gate_up(0)
            for u in range(UNITS):
                if u + 1 < UNITS:
                    gate_up(u + 1)
                pe.wait_ge(hid_split, counts.at("block", BLOCKS * (u + 1)))
                pe.wait_ge(added, counts.at("unit", max(0, u - 1)))
                for t in range(TG):
                    for m in range(BLOCKS):
                        last = three_passes(pe, s.psum[:, 4 + 2 * (u % 2) + t // 2, t % 2 * D:(t % 2 + 1) * D],
                                            pair_at(hid, slice(None), u % 2, m, slice(t * P, (t + 1) * P)),
                                            pair_at(down, slice(None), u // GROUPS, m), m == 0, m == BLOCKS - 1)
                last.then_inc(down_ready, 1)

        turns(pe, turn)

    split_at = {1: (1, 0), 2: (1, 1), 3: (1, 2), 12: (0, 0), 13: (0, 1), 14: (0, 2)}

    def due(n, last):
        slot, piece = split_at.get(n, (None, None))
        return None if slot is None or last and slot == 0 else (slot, piece)

    def turns(engine, turn):
        counts = Counts()
        per = dict(loads=32, w=2 * PIECES, block=UNITS * BLOCKS, unit=UNITS)
        with engine.Fori(0, EXPERTS // 2 - 1) as i:
            counts.i, counts.per = i, per
            turn(counts, False)
        counts.i = None
        counts.passed(per, EXPERTS // 2 - 1)
        turn(counts, True)

    def scalar(act):
        act.wait_ge(small_loaded, 16 * (KD + 2 + BLOCKS * EXPERTS))
        act.activation(router[0][:, :, :], router_raw[:, :, :], ACT.Copy).then_inc(router_hi, 1)
        act.wait_ge(ratio_in, 1)
        act.activation(ratio[:, :], ratio[:, :], ACT.Exp).then_inc(ratio_ready, 1)
        for t in range(TILES // 4):
            act.wait_ge(turned, t + 1)
            act.activation(scores_t[:, 4 * t:4 * t + 4, :].rearrange("e t q -> e (t q)"), s.psum[0:EXPERTS, 3, :],
                           ACT.Copy).then_inc(copied, 1)

        def split(slot, piece):
            if piece < KD:
                act.activation(gu[0][:, slot, piece, :, :], gu_raw[:, slot, piece, :].rearrange("p (n s) -> p s n", s=SIDES),
                               ACT.Copy).then_inc(w_hi, 1)
            else:
                act.activation(down_raw[:, slot, :, :], down_raw[:, slot, :, :], ACT.Copy, scale=0.5)
                act.drain()
                act.activation(down[0][:, slot, :, :], down_raw[:, slot, :, :], ACT.Copy).then_inc(w_hi, 1)

        act.wait_ge(raw_loaded[0], 32)
        for piece in range(PIECES):
            split(0, piece)

        def turn(counts, last):
            for n in range(UNITS * BLOCKS):
                act.wait_ge(gate_ready, counts.at("block", n + 1))
                act.activation(th[:, n % 2, :], gate[:, n % 2, :], ACT.Tanh, scale=ALPHA / 2).then_inc(th_ready, 1)
                hi(counts, n)
                if due(n, last):
                    slot, piece = due(n, last)
                    act.wait_ge(raw_loaded[slot], counts.at("loads", 32 * (2 - slot)))
                    act.wait_ge(down_ready, counts.at("unit", 0 if slot else GROUPS))
                    split(slot, piece)

        def hi(counts, n):
            u = n // BLOCKS
            act.wait_ge(hidden_done, counts.at("block", n + 1 + 2))
            act.wait_ge(down_ready, counts.at("unit", max(0, u - 1)))
            act.activation(hid[0][:, u % 2, n % BLOCKS, :], hidden[:, n % 2, :], ACT.Copy).then_inc(hid_hi, 1)

        turns(act, turn)

    def gpsimd(pool):
        pool.wait_ge(router_hi, 1)
        pool.tensor_tensor(router[1][:, :, :], router_raw[:, :, :], router[0][:, :, :].bitcast(F32),
                           ALU.subtract).then_inc(router_split, 1)

        def split(slot, piece):
            if piece < KD:
                pool.tensor_tensor(gu[1][:, slot, piece, :, :],
                                   gu_raw[:, slot, piece, :].rearrange("p (n s) -> p s n", s=SIDES),
                                   gu[0][:, slot, piece, :, :].bitcast(F32), ALU.subtract).then_inc(w_split, 1)
            else:
                pool.tensor_tensor(down[1][:, slot, :, :], down_raw[:, slot, :, :], down[0][:, slot, :, :].bitcast(F32),
                                   ALU.subtract).then_inc(w_split, 1)

        for piece in range(PIECES):
            pool.wait_ge(w_hi, piece + 1)
            split(0, piece)

        def turn(counts, last):
            for n in range(UNITS * BLOCKS):
                pool.wait_ge(hid_hi, counts.at("block", n + 1))
                pool.tensor_tensor(hid[1][:, n // BLOCKS % 2, n % BLOCKS, :], hidden[:, n % 2, :],
                                   hid[0][:, n // BLOCKS % 2, n % BLOCKS, :].bitcast(F32), ALU.subtract).then_inc(hid_split, 1)
                if due(n, last):
                    slot, piece = due(n, last)
                    pool.wait_ge(w_hi, counts.at("w", PIECES * (2 - slot) + piece + 1))
                    split(slot, piece)

        turns(pool, turn)

    def first_of(dve, values, top, out):
        dve.tensor_reduce(top[:, :], values[:, :, :], AX_X, ALU.max)
        dve.drain()
        dve.tensor_tensor(scan[0][:, :, :], values[:, :, :], top[:, :].unsqueeze(2).to_broadcast([P, TILES, EXPERTS]),
                          ALU.is_equal)
        dve.drain()
        at, shift = 0, 1
        while shift < EXPERTS:
            old, new = scan[at], scan[1 - at]
            dve.tensor_copy(new[:, :, 0:shift], old[:, :, 0:shift])
            dve.tensor_tensor(new[:, :, shift:], old[:, :, shift:], old[:, :, 0:EXPERTS - shift], ALU.max)
            dve.drain()
            at, shift = 1 - at, 2 * shift
        dve.tensor_copy(out[:, :, 0:1], scan[at][:, :, 0:1])
        dve.tensor_tensor(out[:, :, 1:], scan[at][:, :, 1:], scan[at][:, :, 0:EXPERTS - 1], ALU.subtract)
        dve.drain()

    def vector(dve):
        dve.wait_ge(small_loaded, 16 * (KD + 2 + BLOCKS * EXPERTS))
        dve.tensor_scalar(up_b[:, :, :], gu_b[:, :, :, 1], 1.0, None, ALU.add)
        dve.wait_ge(logits_ready, 1)
        everywhere = [P, TILES, EXPERTS]
        dve.tensor_tensor(logits[:, :, :], s.psum[:, 2, 0:TILES * EXPERTS].rearrange("p (t e) -> p t e", e=EXPERTS),
                          router_b[:, :].unsqueeze(1).to_broadcast(everywhere), ALU.add)
        dve.drain()
        first_of(dve, logits, best[0], first)
        dve.scalar_tensor_tensor(work[:, :, :], first[:, :, :], MASKED, logits[:, :, :], ALU.mult, ALU.add)
        dve.drain()
        first_of(dve, work, best[1], second)
        dve.tensor_tensor(ratio[:, :], best[1][:, :], best[0][:, :], ALU.subtract).then_inc(ratio_in, 1)
        dve.wait_ge(ratio_ready, 1)
        dve.tensor_scalar(share[:, :], ratio[:, :], 1.0, None, ALU.add)
        dve.drain()
        dve.reciprocal(share[:, :], share[:, :])
        dve.drain()
        dve.tensor_tensor(ratio[:, :], ratio[:, :], share[:, :], ALU.mult)
        dve.tensor_tensor(first[:, :, :], first[:, :, :], share[:, :].unsqueeze(2).to_broadcast(everywhere), ALU.mult)
        dve.drain()
        dve.tensor_tensor(second[:, :, :], second[:, :, :], ratio[:, :].unsqueeze(2).to_broadcast(everywhere), ALU.mult)
        dve.drain()
        dve.tensor_tensor(scores[:, :, :], first[:, :, :], second[:, :, :], ALU.add).then_inc(scores_ready, 1)
        for t in range(0, TILES, 2):
            dve.wait_ge(bias_ready, t // 2 + 1)
            x = s.x[:, t:t + 2, :].rearrange("p t d -> p (t d)")
            dve.tensor_tensor(x, x, s.psum[:, 4 + t // 2 % 2, :], ALU.add).then_inc(bias_added, 1)
        dve.sem_inc(bounded, 2)

        def turn(counts, last):
            def expert(slot):
                return EXPERTS - 2 + slot if last else counts.i * 2 + slot

            def bound(n):
                slot, m, bank = n // (BLOCKS * GROUPS), n % BLOCKS, 2 * (n % 2)
                dve.wait_ge(products, counts.at("block", n + 1))
                dve.tensor_scalar(gate[:, n % 2, :], s.psum[:, bank, :],
                                  gu_b[:, bass.ds(expert(slot), 1), m, 0:1].rearrange("p e s -> p (e s)"), LIMIT, ALU.add,
                                  ALU.min).then_inc(gate_ready, 1)
                dve.tensor_scalar(up[:, n % 2, :], s.psum[:, bank + 1, :], up_b[:, bass.ds(expert(slot), 1), m], LIMIT + 1.0,
                                  ALU.add, ALU.min).then_inc(bounded, 1)

            def finish(n):
                dve.wait_ge(th_ready, counts.at("block", n + 1))
                dve.scalar_tensor_tensor(glu[:, n % 2, :], th[:, n % 2, :], 1.0, gate[:, n % 2, :], ALU.add, ALU.mult)
                dve.drain()
                dve.wait_ge(hid_split, counts.at("block", max(0, n - 1)))
                dve.scalar_tensor_tensor(hidden[:, n % 2, :], up[:, n % 2, :], 1.0 - LIMIT, glu[:, n % 2, :], ALU.max,
                                         ALU.mult).then_inc(hidden_done, 1)
                dve.drain()

            def combine(u):
                slot, g = u // GROUPS, u % GROUPS
                dve.wait_ge(down_ready, counts.at("unit", u + 1))
                for t in range(TG):
                    x = s.x[:, g * TG + t, :]
                    last = dve.scalar_tensor_tensor(x, s.psum[:, 4 + 2 * (u % 2) + t // 2, t % 2 * D:(t % 2 + 1) * D],
                                                    scores[:, g * TG + t, bass.ds(expert(slot), 1)], x, ALU.mult, ALU.add)
                last.then_inc(added, 1)

            dve.drain()
            for n in range(UNITS * BLOCKS):
                bound(n)
                finish(n)
                if n % BLOCKS == BLOCKS - 1 and n >= 2 * BLOCKS:
                    combine(n // BLOCKS - 2)
            combine(UNITS - 2)
            combine(UNITS - 1)

        turns(dve, turn)

    return dict(sync=sync, tensor=tensor, scalar=scalar, vector=vector, gpsimd=gpsimd,
                done=(added, UNITS * EXPERTS // 2))


def program(nc, a, out):
    with ExitStack() as sems, ExitStack() as base:
        s = shared_memory(nc, base)

        def sem(name):
            return sems.enter_context(nc.semaphore(name))

        x_loaded, small_loaded, in_loaded, w_out_loaded, ff_loaded, stored, out_scaled, out_split = (
            sem(n) for n in ("x_loaded", "small_loaded", "in_loaded", "w_out_loaded", "ff_loaded", "stored", "out_scaled",
                             "out_split"))
        x_dram = a["L0_attn_hidden_states"].rearrange("b (t p) d -> p (b t) d", p=P)
        out_dram = out.rearrange("b (t p) d -> p (b t) d", p=P)
        init_constants = constants(nc, s)

        with ExitStack() as layer0:
            u = layer0.enter_context(nc.sbuf_tensor("u_tok", [P, TILES, D], F32))
            with ExitStack() as mem:
                def sb(name, shape, dt=F32):
                    return mem.enter_context(nc.sbuf_tensor(name, shape, dt))

                cols = (XBC_BLOCKS + Z_BLOCKS) * P + HEADS
                w = dict(
                    conv_w=sb("conv_w", [P, XBC_BLOCKS, TAPS]), conv_b=sb("conv_b", [P, XBC_BLOCKS]),
                    D=sb("w_d", [P, HEADS]), norm_w=sb("norm_w", [P, Z_BLOCKS]), A_log=sb("a_log", [P, HEADS]),
                    dt_bias=sb("dt_bias", [P, HEADS]), ln1=sb("ln1", [P, KD]))
                w["in"] = (sb("in_hi", [P, KD, cols], F32R), sb("in_lo", [P, KD, cols], F32R))
                w["out"] = (sb("out_hi", [P, Z_BLOCKS, D], F32R), sb("out_lo", [P, Z_BLOCKS, D], F32R))
                with ExitStack() as early:
                    in_raw = early.enter_context(nc.sbuf_tensor("in_raw", [P, KD, cols], F32))
                    w["out_raw"] = early.enter_context(nc.sbuf_tensor("out_raw", [P, Z_BLOCKS, D], F32))
                    norm_mamba = norm_stage(nc, sems, early, s, "norm_mamba", s.x, "layer_rms", weight=w["ln1"], keep=u)
                conv_w, conv_b = a["L0_attn_conv_w"], a["L0_attn_conv_b"]
                small = [(w["conv_w"][:, 0:2, :], conv_w[0:2 * P, :].rearrange("(m p) k -> p m k", p=P)),
                         (w["conv_b"][:, 0:2], conv_b[0:2 * P].rearrange("(m p) -> p m", p=P))]
                for g in range(2):
                    rows = slice(g * STATE, (g + 1) * STATE)
                    at = 2 * P + g * REP * STATE
                    small += [(w["conv_w"][rows, 2:, :],
                               conv_w[at:at + REP * STATE, :].rearrange("(m p) k -> p m k", p=STATE)),
                              (w["conv_b"][rows, 2:], conv_b[at:at + REP * STATE].rearrange("(m p) -> p m", p=STATE))]
                small += [(w["D"][:, :], a["L0_attn_D"].partition_broadcast(P)),
                          (w["A_log"][:, :], a["L0_attn_A_log"].partition_broadcast(P)),
                          (w["dt_bias"][:, :], a["L0_attn_dt_bias"].partition_broadcast(P)),
                          (w["norm_w"][:, :], a["L0_attn_norm_w"].rearrange("(m p) -> p m", p=P)),
                          (w["ln1"][:, :], a["L0_attn_ln1_w"].rearrange("(m p) -> p m", p=P))]

                def in_job(to, at, n):
                    return [(in_raw[:, k, at:at + n], w["in"][0][:, k, to:to + n], w["in"][1][:, k, to:to + n], None)
                            for k in range(KD)]

                jobs = in_job(0, INNER, 2 * XB)
                for g in range(2):
                    for k in range(KD):
                        at = INNER + 2 * XB + g * REP * STATE
                        raw = in_raw[:, k, at:at + REP * STATE].rearrange("p (m n) -> p m n", n=STATE)
                        hi, lo = (part[:, k, 2 * XB:2 * XB + INNER].rearrange("p (m g n) -> p m g n", g=2, n=STATE)[:, :, g, :]
                                  for part in w["in"])
                        jobs.append((raw, hi, lo, None))
                jobs += in_job(2 * XB + INNER, 0, INNER) + in_job(2 * XB + 2 * INNER, 2 * XB + 2 * INNER, HEADS)
                in_split = split_weights(nc, sems, "in", (in_loaded, 16), jobs)
                mamba = mamba_stage(nc, sems, mem, s, w,
                                    dict(small=(small_loaded, 16 * len(small)), w_out=(w_out_loaded, 16),
                                         in_split=in_split["done"], normed=norm_mamba["ready"](GROUPS - 1), out_split=(out_split, 1)), u)

            blocks = len(chunk_sizes(LUT_FF))
            ln2 = layer0.enter_context(nc.sbuf_tensor("ln2", [P, KD], F32))
            gate_t, up_t, down_t = (
                tuple(layer0.enter_context(nc.sbuf_tensor(f"{name}_{part}", shape, F32R)) for part in ("hi", "lo"))
                for name, shape in (("gate_t", [P, KD, blocks * P]), ("up_t", [P, KD, blocks * P]),
                                    ("down_t", [P, blocks, D])))
            with ExitStack() as mem:
                table = table_stage(nc, sems, mem, s, a["L0_ffn_lut"], a["L0_ffn_gate_idx"], a["L0_ffn_up_idx"],
                                    a["L0_ffn_down_idx"], gate_t, up_t, down_t)

            with ExitStack() as mem:
                def sb(name, shape, dt=F32):
                    return mem.enter_context(nc.sbuf_tensor(name, shape, dt))

                gate, up = ((sb(f"{n}_hi", [P, KD, FF], F32R), sb(f"{n}_lo", [P, KD, FF], F32R)) for n in ("gate", "up"))
                down = (sb("down_hi", [P, FF // P, D], F32R), sb("down_lo", [P, FF // P, D], F32R))
                norm_mlp = norm_stage(nc, sems, mem, s, "norm_mlp", u, "rms", weight=ln2, bank=6)
                with ExitStack() as early:
                    early.enter_context(nc.sbuf_tensor("above_table", [P, TABLE_MEMORY - MLP_WEIGHTS - TG * D], F32))
                    raws = [early.enter_context(nc.sbuf_tensor(f"{n}_raw", shape, F32)) for n, shape in (
                        ("gate", [P, KD, FF]), ("up", [P, KD, FF]), ("down", [P, FF // P, D]))]
                mlp_split = split_weights(nc, sems, "mlp", (ff_loaded, 64), [
                    (raw[:, :, :], pair[0][:, :, :], pair[1][:, :, :], scale)
                    for raw, pair, scale in zip(raws, (gate, up, down), (None, None, 0.5))])
                mlp = gated_stage(nc, sems, mem, s, "mlp", FF // P, (gate, up, down), [mlp_split["done"]], norm_mlp, residual=u)

            with ExitStack() as mem:
                norm_ffn = norm_stage(nc, sems, mem, s, "norm_ffn", s.x, "layer", bank=6)
                ffn = gated_stage(nc, sems, mem, s, "ffn", blocks, (gate_t, up_t, down_t),
                                  [table["done"], table["zeroed"]], norm_ffn)

        with ExitStack() as layer1:
            norm1 = norm_stage(nc, sems, layer1, s, "norm1", s.x, "layer")
            HALF = GROUPS // BATCH
            with ExitStack() as mem:
                attention = attention_stage(nc, sems, mem, s, a, ffn["done"], norm1)

            with ExitStack() as mem:
                moe = moe_stage(nc, sems, mem, s, a, attention["done"], norm1["ready"](2 * GROUPS - 1))

        block = base.enter_context(nc.Block())

        @block.sync
        def _(sp):
            for g in range(GROUPS):
                sp.dma_start(s.x[:, g * TG:(g + 1) * TG, :], x_dram[:, g * TG:(g + 1) * TG, :]).then_inc(x_loaded, 16)
            with nc.allow_non_contiguous_dma(reason="small vectors, one element for each partition"):
                for dst, src in small:
                    sp.dma_start(dst, src).then_inc(small_loaded, 16)
            sp.dma_start(in_raw[:, :, :], a["L0_attn_in_proj_w"].rearrange("(k p) n -> p k n", p=P)).then_inc(in_loaded, 16)
            sp.dma_start(w["out_raw"][:, :, :],
                         a["L0_attn_out_proj_w"].rearrange("(k p) n -> p k n", p=P)).then_inc(w_out_loaded, 16)
            sp.wait_ge(*mamba["done"])
            table["sync"](sp)
            with nc.allow_non_contiguous_dma(reason="one element for each partition"):
                sp.dma_start(ln2[:, :], a["L0_attn_ln2_w"].rearrange("(m p) -> p m", p=P)).then_inc(ff_loaded, 16)
            for n, raw in zip(("gate", "up", "down"), raws):
                sp.dma_start(raw[:, :, :], a[f"L0_attn_{n}_w"].rearrange("(k p) n -> p k n", p=P)).then_inc(ff_loaded, 16)
            attention["sync"](sp)
            moe["sync"](sp)
            sp.wait_ge(*moe["done"])
            sp.dma_start(out_dram, s.x[:, :, :]).then_inc(stored, 16)
            sp.wait_ge(stored, 16)

        @block.vector
        def _(dve):
            dve.wait_ge(x_loaded, 16 * GROUPS)
            norm_groups(norm_mamba, range(GROUPS))["vector"](dve)
            mamba["vector"](dve)
            table["vector"](dve)
            dve.wait_ge(ff_loaded, 64)
            mlp["vector"](dve)
            ffn["vector"](dve)
            norm_groups(norm1, range(HALF))["vector"](dve)
            attention["vector"](dve)
            norm_groups(norm1, range(GROUPS + HALF, 2 * GROUPS))["vector"](dve)
            moe["vector"](dve)

        @block.scalar
        def _(act):
            in_split["scalar"](act)
            norm_groups(norm_mamba, range(GROUPS))["scalar"](act)
            act.wait_ge(*mamba["prep"])
            act.activation(w["out"][0][:, :, :], w["out_raw"][:, :, :], ACT.Copy).then_inc(out_scaled, 1)
            mamba["scalar"](act)
            act.wait_ge(*mamba["done"])
            table["scalar"](act)
            act.wait_ge(*table["done"])
            mlp_split["scalar"](act)
            mlp["scalar"](act)
            ffn["scalar"](act)
            norm_groups(norm1, range(HALF))["scalar"](act)
            attention["scalar"](act)
            norm_groups(norm1, range(GROUPS + HALF, 2 * GROUPS))["scalar"](act)
            moe["scalar"](act)

        @block.gpsimd
        def _(pool):
            init_constants(pool)
            pool.wait_ge(s.consts_ready, CONSTS)
            in_split["gpsimd"](pool)
            norm_groups(norm_mamba, range(GROUPS))["gpsimd"](pool)
            pool.wait_ge(out_scaled, 1)
            pool.tensor_tensor(w["out"][1][:, :, :], w["out_raw"][:, :, :], w["out"][0][:, :, :].bitcast(F32),
                               ALU.subtract).then_inc(out_split, 1)
            mamba["gpsimd"](pool)
            pool.wait_ge(*mamba["done"])
            table["gpsimd"](pool)
            mlp_split["gpsimd"](pool)
            mlp["gpsimd"](pool)
            ffn["gpsimd"](pool)
            norm_groups(norm1, range(HALF))["gpsimd"](pool)
            attention["gpsimd"](pool)
            norm_groups(norm1, range(GROUPS + HALF, 2 * GROUPS))["gpsimd"](pool)
            moe["gpsimd"](pool)

        @block.tensor
        def _(pe):
            pe.wait_ge(s.consts_ready, CONSTS)
            norm_groups(norm_mamba, range(GROUPS))["tensor"](pe)
            mamba["tensor"](pe)
            table["tensor"](pe)
            mlp["tensor"](pe)
            ffn["tensor"](pe)
            norm_groups(norm1, range(HALF))["tensor"](pe)
            attention["tensor"](pe)
            norm_groups(norm1, range(GROUPS + HALF, 2 * GROUPS))["tensor"](pe)
            moe["tensor"](pe)


_INS = [
    "L0_attn_hidden_states", "L0_attn_in_proj_w", "L0_attn_conv_w", "L0_attn_conv_b", "L0_attn_dt_bias",
    "L0_attn_A_log", "L0_attn_D", "L0_attn_norm_w", "L0_attn_out_proj_w", "L0_attn_ln1_w", "L0_attn_ln2_w",
    "L0_attn_gate_w", "L0_attn_up_w", "L0_attn_down_w", "L0_ffn_lut", "L0_ffn_gate_idx", "L0_ffn_up_idx",
    "L0_ffn_down_idx", "L1_attn_W_Q", "L1_attn_W_K", "L1_attn_W_V", "L1_attn_W_O", "L1_attn_b_Q", "L1_attn_b_K",
    "L1_attn_b_V", "L1_attn_b_O", "L1_ffn_router_weight", "L1_ffn_router_bias", "L1_ffn_gate_up_proj",
    "L1_ffn_gate_up_proj_bias", "L1_ffn_down_proj", "L1_ffn_down_proj_bias",
]


def kernel(**inputs):
    import numpy as _np
    import concourse.bacc as _bacc
    from concourse.bass_utils import run_bass_kernel_spmd as _run

    nc = _bacc.Bacc("TRN2", target_bir_lowering=False, num_devices=1)
    arrays, args = {}, {}
    for name in _INS:
        array = _np.ascontiguousarray(inputs[name])
        arrays[f"in_{name}_dram"] = array
        args[name] = nc.dram_tensor(f"in_{name}_dram", array.shape, mybir.dt.from_np(array.dtype), kind="ExternalInput").ap()
    out = nc.dram_tensor("out_0_dram", (BATCH, SEQ, D), F32, kind="ExternalOutput").ap()
    program(nc, args, out)
    r = _run(nc, [arrays], core_ids=[0])
    return r.results[0]["out_0_dram"]
```
